# Optimizing a Trainium2 kernel written in Bass

```python
import numpy as np
import jax
import jax.numpy as jnp

def _softmax(x, axis=-1):
    return jax.nn.softmax(x, axis=axis)

def _gelu(x):
    return jax.nn.gelu(x, approximate=True)

def _silu(x):
    return jax.nn.silu(x)

def _sigmoid(x):
    return jax.nn.sigmoid(x)

def _layernorm(x, axis=-1, eps=1e-05):
    m = jnp.mean(x, axis=axis, keepdims=True)
    v = jnp.var(x, axis=axis, keepdims=True)
    return (x - m) / jnp.sqrt(v + eps)

def _scatter_add(tgt, idx, src, axis=0):
    return tgt.at[idx].add(src)

def _segment_sum(src, seg, n):
    return jax.ops.segment_sum(src, seg, n)
kernel_name = 'mk_xattn_ffn_d2_seqx_r8_9e25c6'

def setup_inputs(seed: int=0):
    np.random.seed(seed)
    _w = jnp.asarray

    def _rec_inputs():
        import jax
        import jax.numpy as jnp
        _rk = jax.random.key(seed)
        x = -0.0003929 + 0.9999 * jax.random.normal(jax.random.fold_in(_rk, 1), (4, 256, 128), jnp.float32)
        _lenS = 256 - jax.random.randint(jax.random.fold_in(_rk, 7), (4,), 0, max(1, 256 // 4) + 1, jnp.int32)
        _lenS2 = 256 - jax.random.randint(jax.random.fold_in(_rk, 8), (4,), 0, max(1, 256 // 4) + 1, jnp.int32)
        _ctx_768P = jax.random.normal(jax.random.fold_in(_rk, 11), (4, 16, 96), jnp.float32)
        _ctx_768c = jax.random.dirichlet(jax.random.fold_in(_rk, 511), 0.3 * jnp.ones((16,), jnp.float32), (4, 256))
        _ctx_768t = jnp.einsum('bsk,bkd->bsd', _ctx_768c, _ctx_768P)
        _ctx_768t = _ctx_768t * jax.lax.rsqrt(jnp.mean(jnp.square(_ctx_768t)) + 1e-12) * 0.953939
        ctx_768 = -7.36909e-05 + 0.999899 * (_ctx_768t + 0.3 * jax.random.normal(jax.random.fold_in(_rk, 611), (4, 256, 96), jnp.float32))
        return (x, ctx_768)
    x, ctx_768 = _rec_inputs()

    def _L0_xattn_setup():
        import jax, jax.numpy as jnp
        import numpy as np
        IMG_DIM, TXT_DIM, HID = (128, 96, 128)
        B, LQ, LK = (8, 256, 256)
        key = jax.random.key(seed)
        ks = jax.random.split(key, 8)
        s_img = 1.0 / np.sqrt(IMG_DIM)
        s_txt = 1.0 / np.sqrt(TXT_DIM)
        return {'image_features': jax.random.normal(ks[0], (B, LQ, IMG_DIM), jnp.float32), 'text_features': jax.random.normal(ks[1], (B, LK, TXT_DIM), jnp.float32), 'Wq': jax.random.uniform(ks[2], (IMG_DIM, HID), jnp.float32, -s_img, s_img), 'bq': jax.random.uniform(ks[3], (HID,), jnp.float32, -s_img, s_img), 'Wk': jax.random.uniform(ks[4], (TXT_DIM, HID), jnp.float32, -s_txt, s_txt), 'bk': jax.random.uniform(ks[5], (HID,), jnp.float32, -s_txt, s_txt), 'Wv': jax.random.uniform(ks[6], (TXT_DIM, HID), jnp.float32, -s_txt, s_txt), 'bv': jax.random.uniform(ks[7], (HID,), jnp.float32, -s_txt, s_txt)}
    _L0_xattn_all = _L0_xattn_setup()
    _L0_xattn_in = {k: v for k, v in _L0_xattn_all.items() if k in ('Wq', 'bq', 'Wk', 'bk', 'Wv', 'bv')}
    del _L0_xattn_all

    def _L0_ffn_setup():
        import jax, jax.numpy as jnp
        import numpy as np
        E = 64
        K = 6
        CAP = 64
        ROUTE_SCALE = 1.0
        key = jax.random.key(seed)
        ks = jax.random.split(key, 9)
        B, S, D, I = (2, 128, 128, 88)
        SI = 2 * I
        s = 0.02
        return {'x': jax.random.normal(ks[0], (B, S, D), jnp.float32), 'gate_w': jax.random.normal(ks[1], (E, D), jnp.float32) * s, 'gate_b': jnp.zeros((E,), jnp.float32), 'w1': jax.random.normal(ks[2], (E, I, D), jnp.float32) * s, 'w2': jax.random.normal(ks[3], (E, D, I), jnp.float32) * s, 'w3': jax.random.normal(ks[4], (E, I, D), jnp.float32) * s, 'ws1': jax.random.normal(ks[5], (SI, D), jnp.float32) * s, 'ws2': jax.random.normal(ks[6], (D, SI), jnp.float32) * s, 'ws3': jax.random.normal(ks[7], (SI, D), jnp.float32) * s}
    _L0_ffn_all = _L0_ffn_setup()
    _L0_ffn_in = {k: v for k, v in _L0_ffn_all.items() if k in ('gate_w', 'gate_b', 'w1', 'w2', 'w3', 'ws1', 'ws2', 'ws3')}
    del _L0_ffn_all

    def _L1_xattn_setup():
        import jax, jax.numpy as jnp
        import numpy as np
        IN_DIM = 128
        CTX_DIM = 96
        NUM_HEADS = 16
        HEAD_DIM = IN_DIM // NUM_HEADS
        SCALE = 1.0 / float(np.sqrt(HEAD_DIM))
        key = jax.random.key(seed)
        ks = jax.random.split(key, 10)
        B, NQ, NKV = (8, 128, 64)
        s_in = 1.0 / float(np.sqrt(IN_DIM))
        s_ctx = 1.0 / float(np.sqrt(CTX_DIM))
        return {'x': jax.random.normal(ks[0], (B, NQ, IN_DIM), dtype=jnp.float32), 'context': jax.random.normal(ks[1], (B, NKV, CTX_DIM), dtype=jnp.float32), 'Wq': jax.random.normal(ks[2], (IN_DIM, IN_DIM), dtype=jnp.float32) * s_in, 'bq': jax.random.normal(ks[3], (IN_DIM,), dtype=jnp.float32) * 0.01, 'Wk': jax.random.normal(ks[4], (IN_DIM, CTX_DIM), dtype=jnp.float32) * s_ctx, 'bk': jax.random.normal(ks[5], (IN_DIM,), dtype=jnp.float32) * 0.01, 'Wv': jax.random.normal(ks[6], (IN_DIM, CTX_DIM), dtype=jnp.float32) * s_ctx, 'bv': jax.random.normal(ks[7], (IN_DIM,), dtype=jnp.float32) * 0.01, 'Wo': jax.random.normal(ks[8], (IN_DIM, IN_DIM), dtype=jnp.float32) * s_in, 'bo': jax.random.normal(ks[9], (IN_DIM,), dtype=jnp.float32) * 0.01}
    _L1_xattn_all = _L1_xattn_setup()
    _L1_xattn_in = {k: v for k, v in _L1_xattn_all.items() if k in ('Wq', 'bq', 'Wk', 'bk', 'Wv', 'bv', 'Wo', 'bo')}
    del _L1_xattn_all

    def _L1_ffn_setup():
        import jax, jax.numpy as jnp
        import numpy as np
        DIM = 128
        N_EXPERTS = 8
        TOPK = 2
        CAPACITY_FACTOR = 1.25
        B, S = (2, 256)

        def _moe(x, Wr, W1, b1, W2, b2):
            Bsz, Sl, D = x.shape
            E = Wr.shape[1]
            T = Bsz * Sl
            capacity = max(1, int(T * CAPACITY_FACTOR / E))
            xt = x.reshape(T, D)
            probs_full = jax.nn.softmax(xt @ Wr, axis=-1)
            topv, topi = jax.lax.top_k(probs_full, TOPK)
            topv = topv / jnp.sum(topv, axis=-1, keepdims=True)
            onehot = jax.nn.one_hot(topi, E, dtype=x.dtype)
            rank = jnp.cumsum(onehot, axis=0)
            keep = (rank <= capacity).astype(x.dtype) * onehot
            w = jnp.einsum('tk,tke->te', topv, keep)
            h = jax.nn.gelu(jnp.einsum('td,edf->etf', xt, W1) + b1[:, None, :], approximate=False)
            y = jnp.einsum('etf,efd->etd', h, W2) + b2[:, None, :]
            out = jnp.einsum('te,etd->td', w, y)
            return out.reshape(Bsz, Sl, D)
        key = jax.random.key(seed)
        ks = jax.random.split(key, 6)
        D, E, F = (DIM, N_EXPERTS, 4 * DIM)
        x = jax.random.normal(ks[0], (B, S, D), dtype=jnp.float32)
        Wr = jax.random.normal(ks[1], (D, E), dtype=jnp.float32) * (1.0 / np.sqrt(D))
        W1 = jax.random.normal(ks[2], (E, D, F), dtype=jnp.float32) * (1.0 / np.sqrt(D))
        b1 = jnp.zeros((E, F), dtype=jnp.float32)
        W2 = jax.random.normal(ks[3], (E, F, D), dtype=jnp.float32) * (1.0 / np.sqrt(F))
        b2 = jnp.zeros((E, D), dtype=jnp.float32)
        return {'x': x, 'Wr': Wr, 'W1': W1, 'b1': b1, 'W2': W2, 'b2': b2}
    _L1_ffn_all = _L1_ffn_setup()
    _L1_ffn_in = {k: v for k, v in _L1_ffn_all.items() if k in ('Wr', 'W1', 'b1', 'W2', 'b2')}
    del _L1_ffn_all
    return {'x': x, 'ctx_768': ctx_768, 'L0_xattn_Wq': _L0_xattn_in['Wq'], 'L0_xattn_bq': _L0_xattn_in['bq'], 'L0_xattn_Wk': _L0_xattn_in['Wk'], 'L0_xattn_bk': _L0_xattn_in['bk'], 'L0_xattn_Wv': _L0_xattn_in['Wv'], 'L0_xattn_bv': _L0_xattn_in['bv'], 'L0_ffn_gate_w': _L0_ffn_in['gate_w'], 'L0_ffn_gate_b': _L0_ffn_in['gate_b'], 'L0_ffn_w1': _L0_ffn_in['w1'], 'L0_ffn_w2': _L0_ffn_in['w2'], 'L0_ffn_w3': _L0_ffn_in['w3'], 'L0_ffn_ws1': _L0_ffn_in['ws1'], 'L0_ffn_ws2': _L0_ffn_in['ws2'], 'L0_ffn_ws3': _L0_ffn_in['ws3'], 'L1_xattn_Wq': _L1_xattn_in['Wq'], 'L1_xattn_bq': _L1_xattn_in['bq'], 'L1_xattn_Wk': _L1_xattn_in['Wk'], 'L1_xattn_bk': _L1_xattn_in['bk'], 'L1_xattn_Wv': _L1_xattn_in['Wv'], 'L1_xattn_bv': _L1_xattn_in['bv'], 'L1_xattn_Wo': _L1_xattn_in['Wo'], 'L1_xattn_bo': _L1_xattn_in['bo'], 'L1_ffn_Wr': _L1_ffn_in['Wr'], 'L1_ffn_W1': _L1_ffn_in['W1'], 'L1_ffn_b1': _L1_ffn_in['b1'], 'L1_ffn_W2': _L1_ffn_in['W2'], 'L1_ffn_b2': _L1_ffn_in['b2']}

def reference(x, ctx_768, L0_xattn_Wq, L0_xattn_bq, L0_xattn_Wk, L0_xattn_bk, L0_xattn_Wv, L0_xattn_bv, L0_ffn_gate_w, L0_ffn_gate_b, L0_ffn_w1, L0_ffn_w2, L0_ffn_w3, L0_ffn_ws1, L0_ffn_ws2, L0_ffn_ws3, L1_xattn_Wq, L1_xattn_bq, L1_xattn_Wk, L1_xattn_bk, L1_xattn_Wv, L1_xattn_bv, L1_xattn_Wo, L1_xattn_bo, L1_ffn_Wr, L1_ffn_W1, L1_ffn_b1, L1_ffn_W2, L1_ffn_b2):
    import jax
    import jax.numpy as jnp

    def _L0_xattn_ref(image_features, text_features, Wq, bq, Wk, bk, Wv, bv):
        import jax, jax.numpy as jnp
        import numpy as np
        IMG_DIM, TXT_DIM, HID = (128, 96, 128)
        B, LQ, LK = (8, 256, 256)
        query = jnp.einsum('bqi,ih->bqh', image_features, Wq) + bq
        key = jnp.einsum('bkt,th->bkh', text_features, Wk) + bk
        value = jnp.einsum('bkt,th->bkh', text_features, Wv) + bv
        scale = 1.0 / jnp.sqrt(jnp.asarray(HID, query.dtype))
        scores = jnp.einsum('bqh,bkh->bqk', query, key) * scale
        weights = jax.nn.softmax(scores, axis=-1)
        attended = jnp.einsum('bqk,bkh->bqh', weights, value)
        return attended

    def _L0_ffn_ref(x, gate_w, gate_b, w1, w2, w3, ws1, ws2, ws3):
        import jax, jax.numpy as jnp
        import numpy as np
        E = 64
        K = 6
        CAP = 64
        ROUTE_SCALE = 1.0
        shape = x.shape
        D = shape[-1]
        xf = x.reshape(-1, D)
        T = xf.shape[0]
        scores = jax.nn.softmax(xf @ gate_w.T, axis=-1)
        _, idx = jax.lax.top_k(scores + gate_b, K)
        weights = jnp.take_along_axis(scores, idx, axis=1) * ROUTE_SCALE
        flat_e = idx.reshape(-1)
        order = jnp.argsort(flat_e)
        se = flat_e[order]
        counts = jnp.bincount(flat_e, length=E)
        starts = jnp.cumsum(counts) - counts
        pos = jnp.arange(T * K) - starts[se]
        tok = order // K
        xb = jnp.zeros((E, CAP, D), xf.dtype).at[se, pos].set(xf[tok], mode='drop')
        h = jax.nn.silu(jnp.einsum('ecd,eid->eci', xb, w1)) * jnp.einsum('ecd,eid->eci', xb, w3)
        yb = jnp.einsum('eci,edi->ecd', h, w2)
        valid = (pos < CAP).astype(xf.dtype)
        contrib = yb[se, jnp.minimum(pos, CAP - 1)]
        wf = weights.reshape(-1)[order] * valid
        y = jnp.zeros_like(xf).at[tok].add(contrib * wf[:, None])
        z = jax.nn.silu(xf @ ws1.T) * (xf @ ws3.T) @ ws2.T
        return (y + z).reshape(shape)

    def _L1_xattn_ref(x, context, Wq, bq, Wk, bk, Wv, bv, Wo, bo):
        import jax, jax.numpy as jnp
        import numpy as np
        IN_DIM = 128
        CTX_DIM = 96
        NUM_HEADS = 16
        HEAD_DIM = IN_DIM // NUM_HEADS
        SCALE = 1.0 / float(np.sqrt(HEAD_DIM))
        q = x @ Wq.T + bq
        k = context @ Wk.T + bk
        v = context @ Wv.T + bv
        B, NQ, _ = q.shape
        NKV = k.shape[1]
        q = q.reshape(B, NQ, NUM_HEADS, HEAD_DIM)
        k = k.reshape(B, NKV, NUM_HEADS, HEAD_DIM)
        v = v.reshape(B, NKV, NUM_HEADS, HEAD_DIM)
        attn = jnp.einsum('bihd,bjhd->bhij', q, k) * SCALE
        attn = jax.nn.softmax(attn, axis=-1)
        out = jnp.einsum('bhij,bjhd->bihd', attn, v)
        out = out.reshape(B, NQ, IN_DIM)
        return out @ Wo.T + bo

    def _L1_ffn_ref(x, Wr, W1, b1, W2, b2):
        import jax, jax.numpy as jnp
        import numpy as np
        DIM = 128
        N_EXPERTS = 8
        TOPK = 2
        CAPACITY_FACTOR = 1.25
        B, S = (2, 256)

        def _moe(x, Wr, W1, b1, W2, b2):
            Bsz, Sl, D = x.shape
            E = Wr.shape[1]
            T = Bsz * Sl
            capacity = max(1, int(T * CAPACITY_FACTOR / E))
            xt = x.reshape(T, D)
            probs_full = jax.nn.softmax(xt @ Wr, axis=-1)
            topv, topi = jax.lax.top_k(probs_full, TOPK)
            topv = topv / jnp.sum(topv, axis=-1, keepdims=True)
            onehot = jax.nn.one_hot(topi, E, dtype=x.dtype)
            rank = jnp.cumsum(onehot, axis=0)
            keep = (rank <= capacity).astype(x.dtype) * onehot
            w = jnp.einsum('tk,tke->te', topv, keep)
            h = jax.nn.gelu(jnp.einsum('td,edf->etf', xt, W1) + b1[:, None, :], approximate=False)
            y = jnp.einsum('etf,efd->etd', h, W2) + b2[:, None, :]
            out = jnp.einsum('te,etd->td', w, y)
            return out.reshape(Bsz, Sl, D)
        return _moe(x, Wr, W1, b1, W2, b2)
    x = x + _L0_xattn_ref(_layernorm(x, axis=-1), ctx_768, L0_xattn_Wq, L0_xattn_bq, L0_xattn_Wk, L0_xattn_bk, L0_xattn_Wv, L0_xattn_bv)
    x = x + _L0_ffn_ref(_layernorm(x, axis=-1), L0_ffn_gate_w, L0_ffn_gate_b, L0_ffn_w1, L0_ffn_w2, L0_ffn_w3, L0_ffn_ws1, L0_ffn_ws2, L0_ffn_ws3)
    x = x + _L1_xattn_ref(_layernorm(x, axis=-1), ctx_768, L1_xattn_Wq, L1_xattn_bq, L1_xattn_Wk, L1_xattn_bk, L1_xattn_Wv, L1_xattn_bv, L1_xattn_Wo, L1_xattn_bo)
    x = x + _L1_ffn_ref(_layernorm(x, axis=-1), L1_ffn_Wr, L1_ffn_W1, L1_ffn_b1, L1_ffn_W2, L1_ffn_b2)
    return x

_drawn_inputs = setup_inputs


def setup_inputs(seed=0):
    import zlib

    import numpy as np

    out = dict(_drawn_inputs(seed))
    spreads = {'L0_ffn_gate_b': (0.0, 0.8), 'L1_ffn_b1': (0.0, 0.1), 'L1_ffn_b2': (0.0, 0.1)}
    factors = {'L0_xattn_bq': 2.715,
     'L0_xattn_bk': 64.0,
     'L0_ffn_gate_w': 8.0,
     'L0_ffn_w1': 8.0,
     'L0_ffn_w2': 8.0,
     'L0_ffn_w3': 8.0,
     'L0_ffn_ws2': 2.81,
     'L1_xattn_bq': 8.897,
     'L1_xattn_bk': 64.0}
    for name, (base, spread) in spreads.items():
        noise = np.random.default_rng([zlib.crc32(name.encode()), seed]).standard_normal(out[name].shape)
        drawn = base * np.exp(spread * noise) if base else spread * noise
        out[name] = jnp.asarray(drawn.astype(out[name].dtype))
    for name, factor in factors.items():
        out[name] = (out[name] * factor).astype(out[name].dtype)
    return out
```

```python
from contextlib import ExitStack

import concourse.bass as bass
from concourse import mybir

F32 = mybir.dt.float32
F32R = mybir.dt.float32r
BF16 = mybir.dt.bfloat16
F16 = mybir.dt.float16
I32 = mybir.dt.int32
U32 = mybir.dt.uint32
ALU = mybir.AluOpType
ACT = mybir.ActivationFunctionType
X = mybir.AxisListType.X

P = 128
T = 1024
NC = T // P
NB = 4
TB = T // NB
KV = 256
CD = 96
EPS = 1e-5

E0, K0, CAP0, I0 = 64, 6, 64, 88
SI = 2 * I0
GE = 8
NG = E0 // GE
GS = GE * CAP0
NPAIR = GS // P
LNSCALE = 4096.0

NH, HD = 16, 8
PARTS_Q = (0, 0, 0, 1, 1, 1, 2, 2)
PARTS_K = (0, 1, 2, 0, 1, 2, 0, 1)
NCOMB = len(PARTS_Q)
KROWS = NCOMB * HD
VW = HD + 1
RING0 = 3
WCOLS = GE * (SI + P)
NPROB = 8
LAG = 26
TAIL_OT, TAIL_ON, TAIL_ONTP, TAIL_ONT, TAIL_OUT, TAIL_X3 = 21, 22, 23, 24, 25, 26
TAIL_STEP = 5
SLOTS = LAG + (NB - 1) * NH + TAIL_X3 + TAIL_STEP + 1
SCALE1 = 1.0 / float(HD) ** 0.5

E1, F1 = 8, 512
RING1 = 3
CAP1 = int(T * 1.25 / E1)
NF = F1 // P

A_WQ0, A_WQ1, A_WO1, A_GATE, A_WS1, A_WS3, A_WR, A_END = 0, 128, 256, 384, 448, 624, 800, 808
B_BQ0, B_BQ1, B_B1, B_B2, B_END = 0, 1, 2, 34, 42


def view(ap, *dims):
    return bass.AP(ap.tensor, ap.offset, [list(ap.ap[0])] + [list(d) for d in dims])


def build(nc, x_in, ctx_in, packa_in, packc_in, bias_in, gateb_in, bo_in, ws2_in, w13_in, w2_in,
          ew1_in, ew2_in, out):
    with ExitStack() as ctx:
        def sb(name, shape, dt=F32):
            return ctx.enter_context(nc.sbuf_tensor(name, shape, dt))

        def sem(name):
            return ctx.enter_context(nc.semaphore(name))

        def sems(name, n):
            return [sem(f"{name}{i}") for i in range(n)]

        bank = [ctx.enter_context(nc.psum_tensor(f"bank{i}", [P, 512], F32)) for i in range(8)]

        ident = sb("ident", [P, P])
        identb = sb("identb", [P, P], BF16)
        tri = sb("tri", [P, P], BF16)
        ones = sb("ones", [P, P], BF16)
        iota_i = sb("iota_i", [P, E0], I32)
        iota_e = sb("iota_e", [P, E0])
        iota_s = sb("iota_s", [P, CAP0], BF16)
        mhalf = sb("mhalf", [P, 4])
        selw = sb("selw", [3 * E1, E1, P], BF16)

        x = sb("x", [P, NC, P])
        ctxT = sb("ctxT", [P, T])
        packa = sb("packa", [P, A_END])
        packc = sb("packc", [CD + 1, 4, P])
        biases = sb("biases", [P, B_END])
        gateb = sb("gateb", [P, E0])
        bo = sb("bo", [P, P])
        ws2 = sb("ws2", [I0, 2, P])
        st = sb("st", [P, NC, 6])
        mv = sb("mv", [P, NC, 2])
        veps = sb("veps", [P, NC])
        rstd = sb("rstd", [P, NC])
        xn = sb("xn", [P, NC, P])
        xnT = sb("xnT", [P, T])

        big = sb("big", [P, NH * T // 2])
        pbuf = sb("pbuf", [P, 2, NC * GS], BF16)
        work = pbuf[:, :, :].rearrange("p a n -> p (a n)").bitcast(F32)
        qbuf, kbuf, vbuf = sb("qbuf", [P, T]), sb("kbuf", [P, T]), sb("vbuf", [P, NC, P])
        frbuf = sb("frbuf", [P, 5120], F32R)
        splits = sb("splits", [P, 4, T], F32R)

        q0T, k0T, v0 = qbuf, kbuf, vbuf
        prob0 = work[:, 0:NC * KV].rearrange("p (c k) -> p c k", c=NC)
        probT0 = work[:, NC * KV:2 * NC * KV].rearrange("p (c k) -> p c k", c=NC)
        nm0, sum0, rs0 = sb("nm0", [P, NC]), sb("sum0", [P, NC]), sb("rs0", [P, NC])

        xh, xl = sb("xh", [P, NC, P], F16), sb("xl", [P, NC, P], F16)
        score, biased = sb("score", [P, NC, E0]), sb("biased", [P, NC, E0])
        ra, rb = sb("ra", [P, 512]), sb("rb", [P, 512])
        nmg, sumg, rsg = sb("nmg", [P, NC]), sb("sumg", [P, NC]), sb("rsg", [P, NC])
        top8 = sb("top8", [P, NC, 8])
        idx8 = sb("idx8", [P, NC, 8], U32)
        idxf = sb("idxf", [P, NC, 8])
        selb = sb("selb", [P, NC, E0], BF16)
        rk = sb("rk", [P, NG, NC, GE, 2], BF16)
        sparts = sb("sparts", [P, NC, E0, 3], BF16)
        sres = sb("sres", [P, NC, E0])
        hs = work[0:I0, 2048:4096].rearrange("p (i t) -> p i t", i=2)
        def w13(e):
            at = (e // GE) % RING0 * WCOLS + (e % GE) * SI
            return big[:, at:at + SI]

        def w2(e):
            at = (e // GE) % RING0 * WCOLS + GE * SI + (e % GE) * P
            return big[0:I0, at:at + P]

        xb = ctxT[:, :].rearrange("p (a s) -> p a s", a=2)
        PTs = splits
        wslot = sb("wslot", [P, 2, NPAIR])
        sil, gv = sb("sil", [P, NPAIR, I0]), sb("gv", [P, NPAIR, I0])
        gT = sb("gT", [I0, NPAIR, P])
        yh = frbuf[:, 0:512].rearrange("p (j d) -> p j d", j=NPAIR)
        yl = frbuf[:, 512:1024].rearrange("p (j d) -> p j d", j=NPAIR)

        ks = sb("ks", [KROWS + 3, NH, T], BF16)
        qs = big[0:KROWS + 3, :].bitcast(BF16).rearrange("p (h t) -> p h t", h=NH)
        parts = sb("parts", [P, 3, T], BF16)
        vaug = sb("vaug", [P, NC, NH, VW])
        nm1, nmr, rden = (score[:, :, :].rearrange("p c e -> p (c e)")[:, i * P:(i + 1) * P]
                          .rearrange("p (c h) -> p c h", c=NC) for i in range(3))
        nmp = sb("nmp", [P, NC, 3, NH], BF16)
        nmT = sb("nmT", [3 * NH, T], BF16)
        prob1 = work.rearrange("p (r n) -> p r n", r=NPROB)
        qf, oun, onrm, onT = qbuf, qbuf, vbuf, kbuf

        ew = sb("ew", [P, RING1, 2, F1])
        xTh, xTl = frbuf[:, 0:T], frbuf[:, T:2 * T]
        w1h, w1l, w2h, w2l = (splits[:, i, :].rearrange("p (a f) -> p a f", a=2)
                              for i in range(4))
        act = work[:, 0:4 * 512].rearrange("p (r n) -> p r n", r=4)
        NA = 3
        acth = frbuf[:, 2 * T:2 * T + NA * 512].rearrange("p (r n) -> p r n", r=NA)
        actl = frbuf[:, 2 * T + NA * 512:2 * T + 2 * NA * 512].rearrange("p (r n) -> p r n", r=NA)
        accT = qbuf
        wbc = vbuf[:, :, :].rearrange("p c d -> p (c d)").rearrange("p (a t) -> p a t", a=2)
        ywt = kbuf[:, :].rearrange("p (a t) -> p a t", a=2)
        rp, rtop, ridxf, wtok, wres = (
            sres[:, :, :].rearrange("p c e -> p (c e)")[:, i * NC * E1:(i + 1) * NC * E1]
            .rearrange("p (c e) -> p c e", c=NC) for i in range(5))
        ridx = sb("ridx", [P, NC, 8], U32)
        roh = sb("roh", [P, NC, 2, E1], BF16)
        rkeep = sres[:, :, :].rearrange("p c e -> p (c e)")[:, 5 * NC * E1:7 * NC * E1].rearrange(
            "p (c k e) -> p c k e", c=NC, k=2)
        rtv, rsum = sb("rtv", [P, NC, 2]), sb("rsum", [P, NC])
        wparts = sb("wparts", [P, NC, 3, E1], BF16)
        wT = biased[0:3 * E1, :, :].rearrange("p c e -> p (c e)").bitcast(BF16)

        scratch = nc.dram_tensor("qk_scratch", [2, 3, P, T], BF16, kind="Internal").ap()

        ld_x, ld_ctx, ld_packa, ld_packc, ld_small = (
            sem("ld_x"), sem("ld_ctx"), sem("ld_packa"), sem("ld_packc"), sem("ld_small"))
        ld_w0, ld_w1 = sems("ld_w0_", NG), sems("ld_w1_", E1)
        c_row, c_all = sem("c_row"), sem("c_all")
        dve_step, pool_step = sem("dve_step"), sem("pool_step")
        ln_var, ln_rstd, ln_out, ln_tps, ln_tsb = (
            sem("ln_var"), sem("ln_rstd"), sem("ln_out"), sem("ln_tps"), sem("ln_tsb"))
        k0_ps, k0_sb, v0_ps, v0_sb = sem("k0_ps"), sem("k0_sb"), sem("v0_ps"), sem("v0_sb")
        k1_ps, k1_hi, k1_res, k1_mid, k1_lo = (
            sem("k1_ps"), sem("k1_hi"), sem("k1_res"), sem("k1_mid"), sem("k1_lo"))
        v1_ps, v1_sb, kd_out, ks_in = sem("v1_ps"), sem("v1_sb"), sem("kd_out"), sem("ks_in")
        q0_ps, q0_sb, s0_ps, m0_sb, p0_sb = (
            sem("q0_ps"), sem("q0_sb"), sem("s0_ps"), sem("m0_sb"), sem("p0_sb"))
        t0_ps, t0_sb, o0_ps, x1_sb = sem("t0_ps"), sem("t0_sb"), sem("o0_ps"), sem("x1_sb")
        g_ps, g_sub, g_exp, g_score, g_sel, g_rank, g_parts = (
            sem("g_ps"), sem("g_sub"), sem("g_exp"), sem("g_score"), sem("g_sel"), sem("g_rank"),
            sem("g_parts"))
        xhl_sb, sh_ps, sh_sil, sh_sb, sh_z = (
            sem("xhl_sb"), sem("sh_ps"), sem("sh_sil"), sem("sh_sb"), sem("sh_z"))
        e_P, e_G, e_xb, e_T, e_PTa, e_PTv = (
            sem("e_P"), sem("e_G"), sem("e_xb"), sem("e_T"), sem("e_PTa"), sem("e_PTv"))
        e_W, e_H, e_sil, e_gv, e_gTp, e_gT = (
            sem("e_W"), sem("e_H"), sem("e_sil"), sem("e_gv"), sem("e_gTp"), sem("e_gT"))
        e_Y, e_yh, e_yl, e_comb = sem("e_Y"), sem("e_yh"), sem("e_yl"), sem("e_comb")
        z_sb, z_T, x2_sb = sem("z_sb"), sem("z_T"), sem("x2_sb")
        q1_ps, q1_f, q1_hi, q1_res, q1_mid, q1_lo = (
            sem("q1_ps"), sem("q1_f"), sem("q1_hi"), sem("q1_res"), sem("q1_mid"), sem("q1_lo"))
        qd_out, qs_in, nm_in = sems("qd_out", 2), sems("qs_in", 2), sems("nm_in", NB)
        a_zero, a_S, a_max, a_nmp, a_nmTp, a_nmT, a_ST, a_exp = (
            sem("a_zero"), sem("a_S"), sem("a_max"), sem("a_nmp"), sem("a_nmTp"), sem("a_nmT"),
            sem("a_ST"), sem("a_exp"))
        a_O, a_oun, a_oT, a_on, a_onTp, a_onT, a_out, x3_sb = (
            sem("a_O"), sem("a_oun"), sem("a_oT"), sem("a_on"), sem("a_onTp"), sem("a_onT"),
            sem("a_out"), sem("x3_sb"))
        r_x, r_ps, r_sub, r_exp, r_oh, r_rank, r_wp, r_wTp, r_wT = (
            sem("r_x"), sem("r_ps"), sem("r_sub"), sem("r_exp"), sem("r_oh"), sem("r_rank"),
            sem("r_wp"), sem("r_wTp"), sem("r_wT"))
        f_split, f_H, f_act, f_hi, f_lo, f_Y, f_bc, f_wbc, f_yw, f_acc = (
            sem("f_split"), sem("f_H"), sem("f_act"), sem("f_hi"), sem("f_lo"), sem("f_Y"),
            sem("f_bc"), sem("f_wbc"), sem("f_yw"), sem("f_acc"))
        f_oT, x4_sb, st_out = sem("f_oT"), sem("x4_sb"), sem("st_out")

        def half(h2):
            return slice(h2 * 512, h2 * 512 + 512)

        def chunk(c):
            return slice(c * P, (c + 1) * P)

        def batch(b):
            return slice(b * TB, (b + 1) * TB)

        LN_BANK = [0, 1, 2, 3, 4, 5, 2, 3]
        NT = 2 * E1 * NF

        def shared_silu(i):
            return gT[:, :, :].rearrange("p j s -> p (j s)") if i % 2 == 0 else kbuf[0:I0, 0:512]

        def tail_chunk(e, at):
            for i in range(2):
                b = (e - at - i * TAIL_STEP) // NH
                if 0 <= b < NB and e == at + i * TAIL_STEP + NH * b:
                    return 2 * b + i
            return None

        block = ctx.enter_context(nc.Block())

        @block.sync
        def _(sp):
            def group_weights(g):
                at = g % RING0 * WCOLS
                es = slice(g * GE, (g + 1) * GE)
                sp.dma_start(big[:, at:at + GE * SI].rearrange("p (e i) -> p e i", e=GE),
                             w13_in[:, es, :]).then_inc(ld_w0[g], 16)
                sp.dma_start(big[0:I0, at + GE * SI:at + WCOLS].rearrange("p (e d) -> p e d", e=GE),
                             w2_in[:, es, :]).then_inc(ld_w0[g], 16)

            def expert_weights(e):
                sp.dma_start(ew[:, e % RING1, 0, :], ew1_in[:, e, :]).then_inc(ld_w1[e], 16)
                sp.dma_start(ew[:, e % RING1, 1, :].rearrange("p (f d) -> p f d", f=NF),
                             ew2_in[:, e, :, :]).then_inc(ld_w1[e], 16)

            sp.dma_start(ctxT[0:CD, :], ctx_in).then_inc(ld_ctx, 16)
            sp.dma_start(packc[:, :, :], packc_in).then_inc(ld_packc, 16)
            sp.dma_start(x[:, :, :], x_in.rearrange("(c p) d -> p c d", p=P)).then_inc(ld_x, 16)
            sp.dma_start(packa[:, :], packa_in).then_inc(ld_packa, 16)
            sp.dma_start(biases[:, :], bias_in).then_inc(ld_small, 16)
            sp.dma_start(gateb[:, :], gateb_in.to_broadcast([P, E0])).then_inc(ld_small, 16)
            sp.dma_start(bo[:, :], bo_in.to_broadcast([P, P])).then_inc(ld_small, 16)
            sp.dma_start(ws2[:, :, :], ws2_in).then_inc(ld_small, 16)
            for g in range(RING0):
                group_weights(g)
            for e in range(RING1):
                expert_weights(e)
            sp.wait_ge(k1_hi, 2)
            sp.wait_ge(k1_mid, 2)
            sp.wait_ge(k1_lo, 2)
            sp.dma_start(scratch[0].rearrange("j p t -> p j t"), parts[:, :, :]).then_inc(kd_out, 16)
            sp.wait_ge(kd_out, 16)
            for i, part in enumerate(PARTS_K):
                sp.dma_start(ks[i * HD:(i + 1) * HD, :, :],
                             scratch[0, part].rearrange("(h d) t -> d h t", d=HD)).then_inc(ks_in, 16)
            for g in range(RING0, NG):
                sp.wait_ge(e_Y, g - RING0 + 1)
                group_weights(g)
            for h2 in range(2):
                sp.wait_ge(q1_hi, h2 + 1)
                sp.wait_ge(q1_mid, h2 + 1)
                sp.wait_ge(q1_lo, h2 + 1)
                sp.dma_start(scratch[1][:, :, half(h2)].rearrange("j p t -> p j t"),
                             parts[:, :, half(h2)]).then_inc(qd_out[h2], 16)
                sp.wait_ge(qd_out[h2], 16)
                for i, part in enumerate(PARTS_Q):
                    sp.dma_start(qs[i * HD:(i + 1) * HD, :, half(h2)],
                                 scratch[1, part][:, half(h2)].rearrange("(h d) t -> d h t", d=HD)
                                 ).then_inc(qs_in[h2], 16)
            for b in range(NB):
                sp.wait_ge(a_nmT, b + 1)
                for part in range(3):
                    sp.dma_start(qs[KROWS + part:KROWS + part + 1, :, batch(b)],
                                 nmT[part * NH:(part + 1) * NH, batch(b)]).then_inc(nm_in[b], 16)
            for e in range(RING1, E1):
                sp.wait_ge(f_split, e - RING1 + 1)
                expert_weights(e)
            for h2 in range(2):
                sp.wait_ge(x4_sb, h2 + 1)
                sp.dma_start(out.rearrange("(c p) d -> p c d", p=P)[:, 4 * h2:4 * h2 + 4, :],
                             x[:, 4 * h2:4 * h2 + 4, :]).then_inc(st_out, 16)
            sp.wait_ge(st_out, 32)

        @block.gpsimd
        def _(pool):
            steps = [0]

            def chained(ins):
                steps[0] += 1
                ins.then_inc(pool_step, 1)
                pool.wait_ge(pool_step, steps[0])

            pool.memset(ctxT[CD:CD + 1, :], 1.0).then_inc(c_row, 1)
            pool.wait_ge(c_row, 1)
            pool.memset(mhalf[:, :], -0.5)
            pool.memset(ident[:, :], 0.0)
            pool.memset(identb[:, :], 0.0)
            chained(pool.memset(ones[:, :], 1.0))
            chained(pool.memset(selw[:, :, :], 0.0))
            pool.affine_select(out=ident[:, :], in_=ident[:, :], compare_op=ALU.not_equal, fill=1.0,
                               base=0, pattern=[[-1, P]], channel_multiplier=1)
            pool.affine_select(out=identb[:, :], in_=identb[:, :], compare_op=ALU.not_equal,
                               fill=1.0, base=0, pattern=[[-1, P]], channel_multiplier=1)
            pool.affine_select(out=tri[:, :], in_=ones[:, :], compare_op=ALU.is_ge, fill=0.0,
                               base=0, pattern=[[1, P]], channel_multiplier=-1)
            chained(pool.iota(iota_i[:, :], pattern=[[1, E0]], base=0, channel_multiplier=0))
            chained(pool.tensor_copy(iota_e[:, :], iota_i[:, :]))
            pool.tensor_scalar(iota_s[:, :], iota_e[:, :], 1.0, None, ALU.add).then_inc(c_all, 1)

            def power(step):
                cs = slice(4 * (step % 2), 4 * (step % 2) + 4)
                pool.wait_ge(ln_var, step + 1)
                if step >= 2:
                    pool.wait_ge(ln_out, step - 1)
                pool.tensor_tensor(out=rstd[:, cs], in0=veps[:, cs], in1=mhalf[:, :],
                                   op=ALU.pow).then_inc(ln_rstd, 1)

            power(0)
            power(1)
            for h2 in range(2):
                pool.wait_ge(k1_res, h2 + 1)
                pool.tensor_copy(parts[:, 1, half(h2)], (ra, rb)[h2][:, :]).then_inc(k1_mid, 1)
            pool.wait_ge(k1_mid, 2)
            for part in range(3):
                chained(pool.affine_select(
                    out=selw[:, :, :], in_=selw[:, :, :], compare_op=ALU.not_equal, fill=1.0,
                    base=-E1 * part, pattern=[[-1, E1], [0, P]], channel_multiplier=1))
            pool.memset(ks[KROWS:KROWS + 3, :, :], 1.0).then_inc(c_all, 1)
            pool.wait_ge(c_all, 2)
            power(2)
            power(3)
            pool.wait_ge(g_score, 1)
            chained(pool.tensor_copy(sparts[:, :, :, 0], score[:, :, :]))
            chained(pool.tensor_tensor(out=sres[:, :, :], in0=score[:, :, :],
                                       in1=sparts[:, :, :, 0], op=ALU.subtract))
            chained(pool.tensor_copy(sparts[:, :, :, 1], sres[:, :, :]))
            pool.tensor_tensor(out=sparts[:, :, :, 2], in0=sres[:, :, :],
                               in1=sparts[:, :, :, 1], op=ALU.subtract).then_inc(g_parts, 1)
            power(4)
            power(5)
            for h2 in range(2):
                pool.wait_ge(q1_res, h2 + 1)
                pool.tensor_copy(parts[:, 1, half(h2)], (ra, rb)[h2][:, :]).then_inc(q1_mid, 1)
            pool.wait_ge(e_comb, NG)
            for e in range(E1):
                if e == 2:
                    power(6)
                    power(7)
                pool.wait_ge(ld_w1[e], 32)
                if e >= 2:
                    pool.wait_ge(f_Y, 2 * NF * (e - 1))
                pool.tensor_copy(w1h[:, e % 2, :], ew[:, e % RING1, 0, :])
                chained(pool.tensor_copy(w2h[:, e % 2, :], ew[:, e % RING1, 1, :]))
                pool.tensor_tensor(out=w1l[:, e % 2, :], in0=ew[:, e % RING1, 0, :],
                                   in1=w1h[:, e % 2, :].bitcast(F32), op=ALU.subtract)
                pool.tensor_tensor(out=w2l[:, e % 2, :], in0=ew[:, e % RING1, 1, :],
                                   in1=w2h[:, e % 2, :].bitcast(F32),
                                   op=ALU.subtract).then_inc(f_split, 1)

        @block.scalar
        def _(a):
            for h2 in range(2):
                a.wait_ge(k0_ps, h2 + 1)
                a.copy(k0T[:, half(h2)], bank[h2][:, :]).then_inc(k0_sb, 1)
            for h2 in range(2):
                a.wait_ge(v0_ps, h2 + 1)
                a.copy(v0[:, 4 * h2:4 * h2 + 4, :],
                       bank[2 + h2][:, :].rearrange("p (c d) -> p c d", c=4)).then_inc(v0_sb, 1)
            for h2 in range(2):
                a.wait_ge(k1_ps, h2 + 1)
                a.copy(parts[:, 0, half(h2)], bank[4 + h2][:, :]).then_inc(k1_hi, 1)
            for h2 in range(2):
                a.wait_ge(v1_ps, h2 + 1)
                for c in range(4):
                    ins = a.copy(vaug[:, 4 * h2 + c, :, 0:HD],
                                 bank[6 + h2][:, chunk(c)].rearrange("p (h d) -> p h d", h=NH))
                ins.then_inc(v1_sb, 1)
            a.wait_ge(c_all, 1)
            a.copy(vaug[:, :, :, HD:HD + 1],
                   ones[:, :].rearrange("p (c h o) -> p c h o", c=NC, h=NH)).then_inc(v1_sb, 1)

            def norm_transposed(step):
                a.wait_ge(ln_tps, step + 1)
                a.copy(xnT[:, half(step % 2)], bank[LN_BANK[step]][:, :]).then_inc(ln_tsb, 1)

            norm_transposed(0)
            norm_transposed(1)

            def exp0(c):
                a.wait_ge(m0_sb, c + 1)
                a.activation(prob0[:, c, :], bank[4 + c % 2][:, 0:KV], ACT.Exp,
                             bias=nm0[:, c:c + 1], accum_out=sum0[:, c:c + 1]).then_inc(p0_sb, 1)

            exp0(0)
            for c in range(NC):
                if c + 1 < NC:
                    exp0(c + 1)
                a.wait_ge(t0_ps, c + 1)
                a.copy(probT0[:, c, :], bank[6 + c % 2][:, 0:KV]).then_inc(t0_sb, 1)

            norm_transposed(2)
            norm_transposed(3)
            a.wait_ge(g_sub, 1)
            a.activation(score[:, :, :], ra[:, :].rearrange("p (c e) -> p c e", c=NC),
                         ACT.Exp).then_inc(g_exp, 1)
            for i in range(4):
                a.wait_ge(sh_ps, i + 1)
                if i >= 2:
                    a.wait_ge(sh_sb, i - 1)
                a.activation(shared_silu(i), bank[(2, 5)[i % 2]][0:I0, :], ACT.Silu
                             ).then_inc(sh_sil, 1)
            for g in range(NG):
                a.wait_ge(e_G, g + 1)
                if g >= 2:
                    a.wait_ge(e_H, 2 * (g - 1))
                a.mul(xb[:, g % 2, :], bank[2][:, :], 1.0 / LNSCALE).then_inc(e_xb, 1)
                for p2 in range(2):
                    a.wait_ge(e_H, 2 * g + p2 + 1)
                    if g >= 1:
                        a.wait_ge(e_gv, g)
                    a.activation(sil[:, 2 * p2:2 * p2 + 2, :],
                                 bank[5 + p2][:, 0:2 * SI].rearrange(
                                     "p (j i) -> p j i", j=2)[:, :, 0:I0],
                                 ACT.Silu).then_inc(e_sil, 1)
                a.wait_ge(e_T, NPAIR * g + 2)
                if g >= 1:
                    a.wait_ge(e_comb, g)
                a.copy(PTs[:, 1, :], bank[4][:, :].bitcast(BF16)).then_inc(e_PTa, 1)
                a.wait_ge(e_gTp, g + 1)
                a.copy(gT[:, :, :], bank[7][0:I0, :].rearrange(
                    "p (j s) -> p j s", j=NPAIR)).then_inc(e_gT, 1)
                a.wait_ge(e_T, NPAIR * g + 4)
                a.copy(PTs[:, 3, :], bank[4][:, :].bitcast(BF16)).then_inc(e_PTa, 1)
                a.wait_ge(e_Y, g + 1)
                a.copy(yh, bank[7][:, :].rearrange("p (j d) -> p j d", j=NPAIR)).then_inc(e_yh, 1)
            a.wait_ge(e_comb, NG)
            for h2 in range(2):
                a.copy(xnT[:, half(h2)], bank[h2][:, :]).then_inc(z_sb, 1)
            a.wait_ge(z_T, 2)
            norm_transposed(4)
            norm_transposed(5)
            a.wait_ge(kd_out, 16)
            for h2 in range(2):
                a.wait_ge(q1_f, h2 + 1)
                a.copy(parts[:, 0, half(h2)], qf[:, half(h2)]).then_inc(q1_hi, 1)

            for s in range(SLOTS):
                m, e = s, s - LAG
                if m % NH == 3 and 1 <= m // NH <= NB:
                    b = m // NH - 1
                    a.wait_ge(a_nmTp, b + 1)
                    a.copy(nmT[:, batch(b)], bank[4][0:3 * NH, :].bitcast(BF16)[:, 0:TB]
                           ).then_inc(a_nmT, 1)
                if 0 <= e < NB * NH:
                    a.wait_ge(a_ST, e + 1)
                    if e >= NPROB:
                        a.wait_ge(a_O, (e - NPROB) // 4 + 1)
                    a.activation(prob1[:, e % NPROB, :], bank[2 + e % 2][:, :],
                                 ACT.Exp).then_inc(a_exp, 1)
                o = (e - 12) // 8
                if e >= 12 and (e - 12) % 8 == 0 and o < 2 * NB:
                    a.wait_ge(a_O, 2 * o + 2)
                    if o >= 2:
                        a.wait_ge(a_oT, 2 * (o // 2))
                    a.copy(oun[:, half(o % 2)], bank[5 + o % 2][:, :]).then_inc(a_oun, 1)
                c = tail_chunk(e, TAIL_ONT)
                if c is not None:
                    a.wait_ge(a_onTp, c + 1)
                    a.copy(onT[:, chunk(c)], bank[7][:, 0:P]).then_inc(a_onT, 1)

            norm_transposed(6)
            norm_transposed(7)
            a.wait_ge(r_sub, 1)
            a.activation(rp[:, :, :], rp[:, :, :], ACT.Exp).then_inc(r_exp, 1)
            a.wait_ge(r_wTp, 1)
            a.copy(wT[:, :], bank[6][0:3 * E1, :].bitcast(BF16)).then_inc(r_wT, 1)
            for n in range(NT):
                q, f = n // NF, n % NF
                e = q // 2
                if f == 0:
                    a.wait_ge(f_bc, q + 1)
                    if q >= 2:
                        a.wait_ge(f_yw, q - 1)
                    a.copy(wbc[:, q % 2, :], bank[5 + q % 2][:, :]).then_inc(f_wbc, 1)
                a.wait_ge(f_H, n + 1)
                if n >= 4:
                    a.wait_ge(f_lo, n - 3)
                bias = biases[:, B_B1 + e * NF + f:B_B1 + e * NF + f + 1]
                a.activation(act[:, n % 4, :], bank[n % 3][:, :], ACT.Gelu,
                             bias=bias).then_inc(f_act, 1)
                if n >= NA:
                    a.wait_ge(f_Y, n - NA + 1)
                a.activation(acth[:, n % NA, :], bank[n % 3][:, :], ACT.Gelu,
                             bias=bias).then_inc(f_hi, 1)

        @block.tensor
        def _(pe):
            def mm(out_, lhsT, rhs, start=True, stop=True):
                return pe.matmul(out_, lhsT, rhs, start=start, stop=stop, skip_group_check=True)

            pe.wait_ge(ld_ctx, 16)
            pe.wait_ge(ld_packc, 16)
            pe.wait_ge(c_row, 1)
            ctxr = ctxT[0:CD + 1, :]
            for first, (wk, wv, k_ps, v_ps) in ((0, (0, 1, k0_ps, v0_ps)), (4, (2, 3, k1_ps, v1_ps))):
                for h2 in range(2):
                    mm(bank[first + h2][:, :], packc[:, wk, :], ctxr[:, half(h2)]).then_inc(k_ps, 1)
                for c in range(NC):
                    ins = mm(bank[first + 2 + c // 4][:, chunk(c % 4)], ctxr[:, chunk(c)],
                             packc[:, wv, :])
                    if c % 4 == 3:
                        ins.then_inc(v_ps, 1)

            def norm_transposes(step):
                pe.wait_ge(ln_out, step + 1)
                for i in range(4):
                    ins = pe.transpose(bank[LN_BANK[step]][:, chunk(i)],
                                       xn[:, 4 * (step % 2) + i, :], ident[:, :])
                ins.then_inc(ln_tps, 1)

            pe.wait_ge(c_all, 1)
            pe.wait_ge(k0_sb, 2)
            norm_transposes(0)
            norm_transposes(1)
            pe.wait_ge(ld_packa, 16)
            pe.wait_ge(v0_sb, 2)
            for h2 in range(2):
                pe.wait_ge(ln_tsb, h2 + 1)
                mm(bank[2 + h2][:, :], packa[:, A_WQ0:A_WQ0 + P], xnT[:, half(h2)]
                   ).then_inc(q0_ps, 1)

            def scores0(c):
                if c % 4 == 0:
                    pe.wait_ge(q0_sb, c // 4 + 1)
                if c >= 2:
                    pe.wait_ge(p0_sb, c - 1)
                mm(bank[4 + c % 2][:, 0:KV], q0T[:, chunk(c)], k0T[:, batch(c // 2)]
                   ).then_inc(s0_ps, 1)

            def values0(c):
                pe.wait_ge(t0_sb, c + 1)
                if c >= 2:
                    pe.wait_ge(x1_sb, c - 1)
                b = c // 2
                mm(bank[c % 2][:, 0:P], probT0[:, c, 0:P], v0[:, 2 * b, :], stop=False)
                mm(bank[c % 2][:, 0:P], probT0[:, c, P:KV], v0[:, 2 * b + 1, :],
                   start=False).then_inc(o0_ps, 1)

            pe.wait_ge(k1_hi, 2)
            pe.wait_ge(k1_res, 2)
            pe.wait_ge(v1_sb, 2)
            scores0(0)
            for c in range(NC):
                if c + 1 < NC:
                    scores0(c + 1)
                pe.wait_ge(p0_sb, c + 1)
                if c >= 2:
                    pe.wait_ge(t0_sb, c - 1)
                pe.transpose(bank[6 + c % 2][:, 0:P], prob0[:, c, 0:P], ident[:, :])
                pe.transpose(bank[6 + c % 2][:, P:KV], prob0[:, c, P:KV], ident[:, :]
                             ).then_inc(t0_ps, 1)
                if c >= 1:
                    values0(c - 1)
            values0(NC - 1)

            norm_transposes(2)
            norm_transposes(3)
            for h2 in range(2):
                pe.wait_ge(ln_tsb, 2 + h2 + 1)
                for i in range(4):
                    c = 4 * h2 + i
                    ins = mm(bank[4][:, c * E0:(c + 1) * E0], xnT[:, chunk(c)],
                             packa[:, A_GATE:A_GATE + E0])
            ins.then_inc(g_ps, 1)
            for i in range(4):
                ih, h2 = i // 2, i % 2
                if i >= 2:
                    pe.wait_ge(sh_sb, i - 1)
                b1, b3 = ((2, 3), (5, 6))[i % 2]
                mm(bank[b1][0:I0, :], packa[:, A_WS1 + ih * I0:A_WS1 + (ih + 1) * I0],
                   xnT[:, half(h2)])
                mm(bank[b3][0:I0, :], packa[:, A_WS3 + ih * I0:A_WS3 + (ih + 1) * I0],
                   xnT[:, half(h2)]).then_inc(sh_ps, 1)
            pe.wait_ge(g_sel, 1)
            for c in range(NC):
                o = bank[4][:, c * E0:(c + 1) * E0]
                for cc in range(c):
                    mm(o, ones[:, :], selb[:, cc, :], start=(cc == 0), stop=False)
                ins = mm(o, tri[:, :], selb[:, c, :], start=(c == 0))
            ins.then_inc(g_rank, 1)
            pe.wait_ge(ld_small, 64)
            pe.wait_ge(x1_sb, NC)
            pe.wait_ge(sh_sb, 4)
            for h2 in range(2):
                for ih in range(2):
                    ins = mm(bank[h2][:, :], ws2[:, ih, :], hs[:, ih, half(h2)],
                             start=(ih == 0), stop=False)
            ins.then_inc(sh_z, 1)

            def onehot(g, c, j):
                return pbuf[:, g % 2, c * GS + j * P:c * GS + (j + 1) * P]

            def gather(g):
                pe.wait_ge(e_P, g + 1)
                if g >= 1:
                    pe.wait_ge(e_xb, g)
                for c in range(NC):
                    for i, part in enumerate((xh, xl)):
                        ins = mm(bank[2][:, :], part[:, c, :],
                                 pbuf[:, g % 2, c * GS:(c + 1) * GS],
                                 start=(c == 0 and i == 0), stop=(c == NC - 1 and i == 1))
                ins.then_inc(e_G, 1)

            def combine(g):
                pe.wait_ge(e_PTa, 2 * (g + 1))
                pe.wait_ge(e_PTv, 2 * (g + 1))
                pe.wait_ge(e_yh, g + 1)
                pe.wait_ge(e_yl, g + 1)
                for j in range(NPAIR):
                    for y in (yh, yl):
                        for h2 in range(2):
                            ins = mm(bank[h2][:, :], y[:, j, :], PTs[:, j, half(h2)], start=False,
                                     stop=(g == NG - 1 and j == NPAIR - 1 and y is yl))
                ins.then_inc(e_comb, 1)

            def slot_weights(g):
                for j in range(NPAIR):
                    for c in range(NC):
                        ins = mm(bank[7][:, 6 * j:6 * j + 6], onehot(g, c, j),
                                 sparts[:, c, g * GE + 2 * j:g * GE + 2 * j + 2, :].rearrange(
                                     "p e k -> p (e k)"), start=(c == 0), stop=(c == NC - 1))
                ins.then_inc(e_W, 1)

            def hidden(g):
                pe.wait_ge(e_xb, g + 1)
                pe.wait_ge(ld_w0[g], 32)
                if g >= 1:
                    pe.wait_ge(e_gv, g)
                for j in range(NPAIR):
                    for s in range(2):
                        ins = mm(bank[5 + j // 2][64 * s:64 * s + 64, (j % 2) * SI:(j % 2 + 1) * SI],
                                 xb[:, g % 2, j * P + 64 * s:j * P + 64 * s + 64],
                                 w13(g * GE + 2 * j + s))
                    if j % 2:
                        ins.then_inc(e_H, 1)

            def dispatch_transposes(g, j):
                if 2 * g + j // 2:
                    pe.wait_ge((e_PTv, e_PTa)[j % 2], 2 * g + j // 2)
                for c in range(NC):
                    ins = pe.transpose(bank[3 + j % 2][:, :].bitcast(BF16)[:, chunk(c)],
                                       onehot(g, c, j), identb[:, :])
                ins.then_inc(e_T, 1)

            def hidden_transposes(g):
                pe.wait_ge(e_gv, g + 1)
                for j in range(NPAIR):
                    ins = pe.transpose(bank[7][0:I0, chunk(j)], gv[:, j, :], ident[:, :])
                ins.then_inc(e_gTp, 1)

            def outputs(g):
                pe.wait_ge(e_gT, g + 1)
                for j in range(NPAIR):
                    for s in range(2):
                        ins = mm(bank[7][64 * s:64 * s + 64, chunk(j)],
                                 gT[:, j, 64 * s:64 * s + 64], w2(g * GE + 2 * j + s))
                ins.then_inc(e_Y, 1)

            pe.wait_ge(xhl_sb, 1)
            pe.wait_ge(g_parts, 1)
            for g in range(NG):
                gather(g)
                if g >= 1:
                    combine(g - 1)
                slot_weights(g)
                hidden(g)
                for j in (0, 1):
                    dispatch_transposes(g, j)
                hidden_transposes(g)
                for j in (2, 3):
                    dispatch_transposes(g, j)
                outputs(g)
            combine(NG - 1)

            for h2 in range(2):
                pe.wait_ge(z_sb, h2 + 1)
                for i in range(4):
                    ins = pe.transpose(bank[2 + h2][:, chunk(i)], xnT[:, chunk(4 * h2 + i)],
                                       ident[:, :])
                ins.then_inc(z_T, 1)
            norm_transposes(4)
            norm_transposes(5)
            for h2 in range(2):
                pe.wait_ge(ln_tsb, 4 + h2 + 1)
                mm(bank[6 + h2][:, :], packa[:, A_WQ1:A_WQ1 + P], xnT[:, half(h2)]
                   ).then_inc(q1_ps, 1)

            transposed = {"maxima": 0, "outputs": 0}

            def max_scores(m):
                c, hp = m // 8, m % 8
                if m >= 2:
                    pe.wait_ge(a_max, m - 1)
                if m % 32 == 0:
                    pe.wait_ge(qs_in[m // 32], 16 * NCOMB)
                for i in range(2):
                    h = 2 * hp + i
                    ins = mm(bank[m % 2][:, i * KV:(i + 1) * KV], qs[0:KROWS, h, chunk(c)],
                             ks[0:KROWS, h, batch(c // 2)])
                ins.then_inc(a_S, 1)

            def maxima_transposes(b):
                pe.wait_ge(a_nmp, b + 1)
                if transposed["outputs"]:
                    pe.wait_ge(a_on, transposed["outputs"])
                transposed["maxima"] += 1
                for i in range(2):
                    ins = pe.transpose(bank[4][0:3 * NH, :].bitcast(BF16)[:, chunk(i)],
                                       nmp[:, 2 * b + i, :, :].rearrange("p j h -> p (j h)"),
                                       identb[:, :])
                ins.then_inc(a_nmTp, 1)

            def exp_scores(e):
                b, h = e // NH, e % NH
                if h == 0:
                    pe.wait_ge(nm_in[b], 48)
                if e >= 2:
                    pe.wait_ge(a_exp, e - 1)
                for kc in range(2):
                    ins = mm(bank[2 + e % 2][:, kc * TB:(kc + 1) * TB],
                             ks[:, h, chunk(2 * b + kc)], qs[:, h, batch(b)])
                ins.then_inc(a_ST, 1)

            def head_values(hg):
                b, g4 = hg // 4, hg % 4
                pe.wait_ge(a_exp, 4 * hg + 4)
                if hg >= 4 and g4 % 2 == 0:
                    pe.wait_ge(a_oun, hg // 2 - 1)
                for kc in range(2):
                    for i in range(4):
                        h = 4 * g4 + i
                        ins = mm(bank[5 + g4 // 2][32 * i:32 * i + VW,
                                                   (g4 % 2) * TB:(g4 % 2 + 1) * TB],
                                 vaug[:, 2 * b + kc, h, :],
                                 prob1[:, (4 * hg + i) % NPROB, kc * TB:(kc + 1) * TB],
                                 start=(kc == 0), stop=(kc == 1))
                ins.then_inc(a_O, 1)

            def output_transposes(c):
                b, i = c // 2, c % 2
                pe.wait_ge(a_oun, 2 * b + 2)
                pe.wait_ge(a_nmT, transposed["maxima"])
                if c >= 1:
                    pe.wait_ge(a_on, c)
                transposed["outputs"] += 1
                for g4 in range(4):
                    at = g4 * TB + i * P
                    ins = pe.transpose(bank[4][:, chunk(g4)], oun[:, at:at + P], ident[:, :])
                ins.then_inc(a_oT, 1)

            def normed_transposes(c):
                pe.wait_ge(a_on, c + 1)
                if c >= 1:
                    pe.wait_ge(x3_sb, c)
                pe.transpose(bank[7][:, 0:P], onrm[:, c, :], ident[:, :]).then_inc(a_onTp, 1)

            def attention_out(c):
                pe.wait_ge(a_onT, c + 1)
                mm(bank[7][:, 0:P], onT[:, chunk(c)], packa[:, A_WO1:A_WO1 + P]).then_inc(a_out, 1)

            pe.wait_ge(a_zero, 1)
            pe.wait_ge(c_all, 2)
            pe.wait_ge(v1_sb, 3)
            pe.wait_ge(ks_in, 16 * NCOMB)
            for s in range(SLOTS):
                m, e = s, s - LAG
                if m < NB * NH:
                    max_scores(m)
                if m % NH == 2 and 1 <= m // NH <= NB:
                    maxima_transposes(m // NH - 1)
                if 0 <= e < NB * NH:
                    exp_scores(e)
                if e >= 6 and (e - 6) % 4 == 0 and (e - 6) // 4 < 4 * NB:
                    head_values((e - 6) // 4)
                for at, step in ((TAIL_OT, output_transposes), (TAIL_ONTP, normed_transposes),
                                 (TAIL_OUT, attention_out)):
                    c = tail_chunk(e, at)
                    if c is not None:
                        step(c)

            norm_transposes(6)
            norm_transposes(7)
            for h2 in range(2):
                pe.wait_ge(ln_tsb, 6 + h2 + 1)
                for i in range(4):
                    c = 4 * h2 + i
                    ins = mm(bank[4][:, c * E1:(c + 1) * E1], xnT[:, chunk(c)],
                             packa[:, A_WR:A_WR + E1])
            ins.then_inc(r_ps, 1)

            def ffn_hidden(n):
                q, f = n // NF, n % NF
                e, h2 = q // 2, q % 2
                if n % (2 * NF) == 0:
                    pe.wait_ge(f_split, e + 1)
                if n >= 3:
                    pe.wait_ge(f_hi, n - 2)
                wh, wl = w1h[:, e % 2, chunk(f)], w1l[:, e % 2, chunk(f)]
                o = bank[n % 3][:, :]
                mm(o, wh, xTh[:, half(h2)], stop=False)
                mm(o, wh, xTl[:, half(h2)], start=False, stop=False)
                mm(o, wl, xTh[:, half(h2)], start=False).then_inc(f_H, 1)

            def ffn_out(n):
                q, f = n // NF, n % NF
                e = q // 2
                if f == 0 and q >= 2:
                    pe.wait_ge(f_yw, q - 1)
                pe.wait_ge(f_hi, n + 1)
                pe.wait_ge(f_lo, n + 1)
                wh, wl = w2h[:, e % 2, chunk(f)], w2l[:, e % 2, chunk(f)]
                o = bank[3 + q % 2][:, :]
                mm(o, wh, acth[:, n % NA, :], start=(f == 0), stop=False)
                mm(o, wh, actl[:, n % NA, :], start=False, stop=False)
                mm(o, wl, acth[:, n % NA, :], start=False, stop=(f == NF - 1)).then_inc(f_Y, 1)

            def weight_rows(q):
                e, h2 = q // 2, q % 2
                if q >= 2:
                    pe.wait_ge(f_wbc, q - 1)
                mm(bank[5 + q % 2][:, :], selw[:, e, :], wT[:, half(h2)]).then_inc(f_bc, 1)

            pe.wait_ge(r_x, 2)
            ffn_hidden(0)
            pe.wait_ge(r_oh, 1)
            for c in range(NC):
                o = bank[5][:, c * 2 * E1:(c + 1) * 2 * E1]
                for cc in range(c):
                    mm(o, ones[:, :], roh[:, cc, :, :].rearrange("p k e -> p (k e)"),
                       start=(cc == 0), stop=False)
                ins = mm(o, tri[:, :], roh[:, c, :, :].rearrange("p k e -> p (k e)"),
                         start=(c == 0))
            ins.then_inc(r_rank, 1)
            pe.wait_ge(r_wp, 1)
            for c in range(NC):
                ins = pe.transpose(bank[6][0:3 * E1, :].bitcast(BF16)[:, chunk(c)],
                                   wparts[:, c, :, :].rearrange("p k e -> p (k e)"), identb[:, :])
            ins.then_inc(r_wTp, 1)
            pe.wait_ge(r_wT, 1)
            for n in range(1, NT + 2):
                if (n - 1) % NF == 0 and (n - 1) // NF < 2 * E1:
                    weight_rows((n - 1) // NF)
                if n < NT:
                    ffn_hidden(n)
                if n >= 2:
                    ffn_out(n - 2)
            for h2 in range(2):
                pe.wait_ge(f_acc, 2 * (E1 - 1) - 1 + h2)
                for i in range(4):
                    ins = pe.transpose(bank[6 + h2][:, chunk(i)], accT[:, chunk(4 * h2 + i)],
                                       ident[:, :])
                ins.then_inc(f_oT, 1)

        @block.vector
        def _(v):
            steps = [0]

            def chained(ins):
                steps[0] += 1
                ins.then_inc(dve_step, 1)
                v.wait_ge(dve_step, steps[0])

            def statistics(step):
                cs = range(4 * (step % 2), 4 * (step % 2) + 4)
                for c in cs:
                    ins = v.bn_stats(st[:, c, :], x[:, c, :])
                chained(ins)
                for c in cs:
                    ins = v.bn_aggr(mv[:, c, :], st[:, c, :])
                chained(ins)
                v.tensor_scalar(veps[:, cs[0]:cs[-1] + 1], mv[:, cs[0]:cs[-1] + 1, 1], EPS, None,
                                ALU.add).then_inc(ln_var, 1)

            def normalise(step):
                v.wait_ge(ln_rstd, step + 1)
                if step >= 2:
                    v.wait_ge(ln_tps, step - 1)
                for c in range(4 * (step % 2), 4 * (step % 2) + 4):
                    ins = v.tensor_scalar(xn[:, c, :], x[:, c, :], mv[:, c, 0:1], rstd[:, c:c + 1],
                                          ALU.subtract, ALU.mult)
                ins.then_inc(ln_out, 1)

            v.wait_ge(ld_x, 16)
            statistics(0)
            statistics(1)
            normalise(0)
            normalise(1)
            for h2 in range(2):
                v.wait_ge(k1_hi, h2 + 1)
                v.tensor_tensor(out=(ra, rb)[h2][:, :], in0=bank[4 + h2][:, :],
                                in1=parts[:, 0, half(h2)], op=ALU.subtract).then_inc(k1_res, 1)
            v.wait_ge(ld_small, 64)
            for h2 in range(2):
                v.wait_ge(q0_ps, h2 + 1)
                v.tensor_scalar(q0T[:, half(h2)], bank[2 + h2][:, :], biases[:, B_BQ0:B_BQ0 + 1],
                                float(P) ** -0.5, ALU.add, ALU.mult).then_inc(q0_sb, 1)
            for h2 in range(2):
                v.wait_ge(k1_mid, h2 + 1)
                v.tensor_tensor(out=parts[:, 2, half(h2)], in0=(ra, rb)[h2][:, :],
                                in1=parts[:, 1, half(h2)], op=ALU.subtract).then_inc(k1_lo, 1)

            def maximum0(c):
                v.wait_ge(s0_ps, c + 1)
                v.tensor_reduce(nm0[:, c:c + 1], bank[4 + c % 2][:, 0:KV], X, ALU.max,
                                negate=True).then_inc(m0_sb, 1)

            def residual1(c):
                v.wait_ge(p0_sb, c + 1)
                chained(v.reciprocal(rs0[:, c:c + 1], sum0[:, c:c + 1]))
                v.wait_ge(o0_ps, c + 1)
                v.scalar_tensor_tensor(out=x[:, c, :], in0=bank[c % 2][:, 0:P],
                                       scalar=rs0[:, c:c + 1], in1=x[:, c, :], op0=ALU.mult,
                                       op1=ALU.add).then_inc(x1_sb, 1)

            maximum0(0)
            for c in range(NC):
                if c + 1 < NC:
                    maximum0(c + 1)
                if c >= 1:
                    residual1(c - 1)
            residual1(NC - 1)

            v.wait_ge(x1_sb, NC)
            statistics(2)
            statistics(3)
            normalise(2)
            normalise(3)
            v.wait_ge(ln_out, 4)
            chained(v.tensor_scalar(xh[:, :, :], xn[:, :, :], LNSCALE, None, ALU.mult))
            v.scalar_tensor_tensor(out=xl[:, :, :], in0=xn[:, :, :], scalar=LNSCALE,
                                   in1=xh[:, :, :], op0=ALU.mult,
                                   op1=ALU.subtract).then_inc(xhl_sb, 1)
            logits = bank[4][:, :].rearrange("p (c e) -> p c e", c=NC)
            v.wait_ge(g_ps, 1)
            chained(v.tensor_reduce(nmg[:, :], logits, X, ALU.max, negate=True))
            v.tensor_tensor(out=ra[:, :].rearrange("p (c e) -> p c e", c=NC), in0=logits,
                            in1=view(nmg[:, :], (1, NC), (0, E0)), op=ALU.add).then_inc(g_sub, 1)

            def shared_product(i):
                ih, h2 = i // 2, i % 2
                v.wait_ge(sh_sil, i + 1)
                v.tensor_tensor(out=hs[:, ih, half(h2)], in0=bank[(3, 6)[i % 2]][0:I0, :],
                                in1=shared_silu(i), op=ALU.mult).then_inc(sh_sb, 1)

            v.wait_ge(g_exp, 1)
            chained(v.reduce_sum(sumg[:, :], score[:, :, :], X))
            chained(v.reciprocal(rsg[:, :], sumg[:, :]))
            v.tensor_tensor(out=score[:, :, :], in0=score[:, :, :],
                            in1=view(rsg[:, :], (1, NC), (0, E0)), op=ALU.mult
                            ).then_inc(g_score, 1)
            v.wait_ge(g_score, 1)
            chained(v.tensor_tensor(out=biased[:, :, :], in0=score[:, :, :],
                                    in1=view(gateb[:, :], (0, NC), (1, E0)), op=ALU.add))
            for c in range(NC):
                ins = v.max(out=top8[:, c, :], in_=biased[:, c, :])
            chained(ins)
            for c in range(NC):
                ins = v.max_index(out=idx8[:, c, :], in_max=top8[:, c, :], in_values=biased[:, c, :])
            chained(ins)
            chained(v.tensor_copy(idxf[:, :, :], idx8[:, :, :]))
            lowest = view(top8[:, 0, K0 - 1:K0], (8, NC), (0, E0))
            lowest_at = view(idxf[:, 0, K0 - 1:K0], (8, NC), (0, E0))
            ra3, rb3 = (t[:, :].rearrange("p (c e) -> p c e", c=NC) for t in (ra, rb))
            v.tensor_tensor(out=ra3, in0=view(iota_e[:, :], (0, NC), (1, E0)), in1=lowest_at,
                            op=ALU.is_le)
            chained(v.tensor_tensor(out=rb3, in0=biased[:, :, :], in1=lowest, op=ALU.is_equal))
            v.tensor_tensor(out=ra3, in0=ra3, in1=rb3, op=ALU.mult)
            chained(v.tensor_tensor(out=biased[:, :, :], in0=biased[:, :, :], in1=lowest,
                                    op=ALU.is_gt))
            v.tensor_tensor(out=selb[:, :, :], in0=ra3, in1=biased[:, :, :],
                            op=ALU.add).then_inc(g_sel, 1)
            for i in range(4):
                shared_product(i)
            v.wait_ge(g_rank, 1)
            for c in range(NC):
                ins = v.tensor_tensor(out=view(rk[:, 0, c, 0, 0:1], (NC * GE * 2, NG), (2, GE), (1, 2)),
                                      in0=view(bank[4][:, c * E0:c * E0 + 1], (GE, NG), (1, GE), (0, 2)),
                                      in1=view(selb[:, c, 0:1], (GE, NG), (1, GE), (0, 2)),
                                      op=ALU.mult)
            chained(ins)

            def dispatch(g):
                if g == 1:
                    v.wait_ge(sh_z, 1)
                if g >= 2:
                    v.wait_ge(e_T, NPAIR * (g - 1))
                v.tensor_tensor(out=view(pbuf[:, g % 2, 0:1], (CAP0, NC * GE), (2, CAP0 // 2), (1, 2)),
                                in0=view(rk[:, g, 0, 0, 0:1], (2, NC * GE), (0, CAP0 // 2), (1, 2)),
                                in1=view(iota_s[:, 0:1], (0, NC * GE), (2, CAP0 // 2), (1, 2)),
                                op=ALU.is_equal).then_inc(e_P, 1)

            dispatch(0)
            dispatch(1)
            for g in range(NG):
                v.wait_ge(e_W, g + 1)
                for s in range(2):
                    ps = slice(64 * s, 64 * s + 64)
                    ins = v.reduce_sum(wslot[ps, g % 2, :],
                                       view(bank[7][ps, 3 * s:3 * s + 1], (6, NPAIR), (1, 3)), X)
                chained(ins)
                v.wait_ge(e_sil, 2 * g + 2)
                if g >= 1:
                    v.wait_ge(e_gTp, g)
                for j in range(NPAIR):
                    at = (j % 2) * SI + I0
                    ins = v.scalar_tensor_tensor(out=gv[:, j, :], in0=bank[5 + j // 2][:, at:at + I0],
                                                 scalar=wslot[:, g % 2, j:j + 1], in1=sil[:, j, :],
                                                 op0=ALU.mult, op1=ALU.mult)
                ins.then_inc(e_gv, 1)
                for i in range(2):
                    v.wait_ge(e_T, NPAIR * g + 2 * i + 1)
                    if g >= 1:
                        v.wait_ge(e_comb, g)
                    v.tensor_copy(PTs[:, 2 * i, :], bank[3][:, :].bitcast(BF16)).then_inc(e_PTv, 1)
                v.wait_ge(e_yh, g + 1)
                v.tensor_tensor(out=yl, in0=bank[7][:, :].rearrange("p (j d) -> p j d", j=NPAIR),
                                in1=yh.bitcast(F32), op=ALU.subtract).then_inc(e_yl, 1)
                if g + 2 < NG:
                    dispatch(g + 2)

            for h2 in range(2):
                v.wait_ge(z_T, h2 + 1)
                xh2 = x[:, 4 * h2:4 * h2 + 4, :]
                v.tensor_tensor(out=xh2, in0=xh2,
                                in1=bank[2 + h2][:, :].rearrange("p (c d) -> p c d", c=4),
                                op=ALU.add).then_inc(x2_sb, 1)
            v.wait_ge(x2_sb, 2)
            statistics(4)
            statistics(5)
            normalise(4)
            normalise(5)
            for h2 in range(2):
                v.wait_ge(q1_ps, h2 + 1)
                v.tensor_scalar(qf[:, half(h2)], bank[6 + h2][:, :], biases[:, B_BQ1:B_BQ1 + 1],
                                SCALE1, ALU.add, ALU.mult).then_inc(q1_f, 1)
            for h2 in range(2):
                v.wait_ge(q1_hi, h2 + 1)
                v.tensor_tensor(out=(ra, rb)[h2][:, :], in0=qf[:, half(h2)],
                                in1=parts[:, 0, half(h2)], op=ALU.subtract).then_inc(q1_res, 1)
            v.tensor_tensor(out=x[:, :, :], in0=x[:, :, :], in1=view(bo[:, :], (0, NC), (1, P)),
                            op=ALU.add).then_inc(x2_sb, 1)
            for h2 in range(2):
                v.wait_ge(q1_mid, h2 + 1)
                v.tensor_tensor(out=parts[:, 2, half(h2)], in0=(ra, rb)[h2][:, :],
                                in1=parts[:, 1, half(h2)], op=ALU.subtract).then_inc(q1_lo, 1)
            v.wait_ge(ln_tsb, 6)
            v.memset(bank[5][:, :], 0.0)
            v.memset(bank[6][:, :], 0.0).then_inc(a_zero, 1)

            for s in range(SLOTS):
                m, e = s, s - LAG
                if m < NB * NH:
                    c, hp = m // 8, m % 8
                    v.wait_ge(a_S, m + 1)
                    v.tensor_reduce(nm1[:, c, 2 * hp:2 * hp + 2],
                                    bank[m % 2][:, :].rearrange("p (h k) -> p h k", h=2), X,
                                    ALU.max, negate=True).then_inc(a_max, 1)
                    if m % NH == NH - 1:
                        cs = slice(c - 1, c + 1)
                        v.wait_ge(a_max, m + 1)
                        chained(v.tensor_copy(nmp[:, cs, 0, :], nm1[:, cs, :]))
                        chained(v.tensor_tensor(out=nmr[:, cs, :], in0=nm1[:, cs, :],
                                                in1=nmp[:, cs, 0, :], op=ALU.subtract))
                        chained(v.tensor_copy(nmp[:, cs, 1, :], nmr[:, cs, :]))
                        v.tensor_tensor(out=nmp[:, cs, 2, :], in0=nmr[:, cs, :],
                                        in1=nmp[:, cs, 1, :], op=ALU.subtract).then_inc(a_nmp, 1)
                c = tail_chunk(e, TAIL_ON)
                if c is not None:
                    v.wait_ge(a_oT, c + 1)
                    chained(v.reciprocal(rden[:, c, :], view(bank[4][:, HD:HD + 1], (32, NH))))
                    v.tensor_tensor(out=onrm[:, c, :].rearrange("p (h d) -> p h d", h=NH),
                                    in0=view(bank[4][:, 0:1], (32, NH), (1, HD)),
                                    in1=view(rden[:, c, :], (1, NH), (0, HD)),
                                    op=ALU.mult).then_inc(a_on, 1)
                c = tail_chunk(e, TAIL_X3)
                if c is not None:
                    v.wait_ge(a_out, c + 1)
                    if c == 0:
                        v.wait_ge(x2_sb, 3)
                    v.tensor_tensor(out=x[:, c, :], in0=x[:, c, :], in1=bank[7][:, 0:P],
                                    op=ALU.add).then_inc(x3_sb, 1)

            v.wait_ge(x3_sb, NC)
            statistics(6)
            statistics(7)
            normalise(6)
            normalise(7)
            for h2 in range(2):
                v.wait_ge(ln_tsb, 6 + h2 + 1)
                chained(v.tensor_copy(xTh[:, half(h2)], xnT[:, half(h2)]))
                v.tensor_tensor(out=xTl[:, half(h2)], in0=xnT[:, half(h2)],
                                in1=xTh[:, half(h2)].bitcast(F32), op=ALU.subtract
                                ).then_inc(r_x, 1)
            logits = bank[4][:, 0:NC * E1].rearrange("p (c e) -> p c e", c=NC)
            v.wait_ge(r_ps, 1)
            chained(v.tensor_reduce(rsum[:, :], logits, X, ALU.max, negate=True))
            v.tensor_tensor(out=rp[:, :, :], in0=logits, in1=view(rsum[:, :], (1, NC), (0, E1)),
                            op=ALU.add).then_inc(r_sub, 1)
            v.wait_ge(r_exp, 1)
            for c in range(NC):
                ins = v.max(out=rtop[:, c, :], in_=rp[:, c, :])
            chained(ins)
            for c in range(NC):
                ins = v.max_index(out=ridx[:, c, :], in_max=rtop[:, c, :], in_values=rp[:, c, :])
            chained(ins)
            chained(v.tensor_copy(ridxf[:, :, :], ridx[:, :, :]))
            v.tensor_tensor(out=roh[:, :, :, :], in0=view(iota_e[:, :], (0, NC), (0, 2), (1, E1)),
                            in1=view(ridxf[:, 0, 0:1], (8, NC), (1, 2), (0, E1)),
                            op=ALU.is_equal).then_inc(r_oh, 1)
            v.wait_ge(r_oh, 1)
            chained(v.tensor_tensor(out=rsum[:, :], in0=rtop[:, :, 0], in1=rtop[:, :, 1],
                                    op=ALU.add))
            chained(v.reciprocal(rsum[:, :], rsum[:, :]))
            chained(v.tensor_tensor(out=rtv[:, :, :], in0=rtop[:, :, 0:2],
                                    in1=view(rsum[:, :], (1, NC), (0, 2)), op=ALU.mult))
            v.wait_ge(r_rank, 1)
            chained(v.scalar_tensor_tensor(
                out=rkeep[:, :, :, :].rearrange("p c k e -> p (c k e)"),
                in0=bank[5][:, 0:NC * 2 * E1], scalar=float(CAP1),
                in1=roh[:, :, :, :].rearrange("p c k e -> p (c k e)"),
                op0=ALU.is_le, op1=ALU.mult))
            chained(v.tensor_tensor(out=rkeep[:, :, :, :], in0=rkeep[:, :, :, :],
                                    in1=view(rtv[:, 0, 0:1], (2, NC), (1, 2), (0, E1)),
                                    op=ALU.mult))
            chained(v.tensor_tensor(out=wtok[:, :, :], in0=rkeep[:, :, 0, :],
                                    in1=rkeep[:, :, 1, :], op=ALU.add))
            chained(v.tensor_copy(wparts[:, :, 0, :], wtok[:, :, :]))
            chained(v.tensor_tensor(out=wres[:, :, :], in0=wtok[:, :, :], in1=wparts[:, :, 0, :],
                                    op=ALU.subtract))
            chained(v.tensor_copy(wparts[:, :, 1, :], wres[:, :, :]))
            v.tensor_tensor(out=wparts[:, :, 2, :], in0=wres[:, :, :], in1=wparts[:, :, 1, :],
                            op=ALU.subtract).then_inc(r_wp, 1)

            def weighted(q):
                e, h2 = q // 2, q % 2
                v.wait_ge(f_Y, NF * (q + 1))
                v.wait_ge(f_wbc, q + 1)
                dst = accT[:, half(h2)] if e == 0 else ywt[:, h2, :]
                v.scalar_tensor_tensor(out=dst, in0=bank[3 + q % 2][:, :],
                                       scalar=biases[:, B_B2 + e:B_B2 + e + 1],
                                       in1=wbc[:, q % 2, :], op0=ALU.add,
                                       op1=ALU.mult).then_inc(f_yw, 1)
                if e >= 1:
                    v.wait_ge(f_yw, q + 1)
                    if e >= 2:
                        v.wait_ge(f_acc, q - 3)
                    v.tensor_tensor(out=accT[:, half(h2)], in0=accT[:, half(h2)], in1=dst,
                                    op=ALU.add).then_inc(f_acc, 1)

            for n in range(NT):
                v.wait_ge(f_act, n + 1)
                v.wait_ge(f_hi, n + 1)
                if n >= NA:
                    v.wait_ge(f_Y, n - NA + 1)
                v.tensor_tensor(out=actl[:, n % NA, :], in0=act[:, n % 4, :],
                                in1=acth[:, n % NA, :].bitcast(F32), op=ALU.subtract
                                ).then_inc(f_lo, 1)
                if n % NF == 1 and n > NF:
                    weighted(n // NF - 1)
            weighted(2 * E1 - 1)
            for h2 in range(2):
                v.wait_ge(f_oT, h2 + 1)
                xh2 = x[:, 4 * h2:4 * h2 + 4, :]
                v.tensor_tensor(out=xh2, in0=xh2,
                                in1=bank[6 + h2][:, :].rearrange("p (c d) -> p c d", c=4),
                                op=ALU.add).then_inc(x4_sb, 1)


def kernel(**inputs):
    import numpy as np
    import concourse.bacc as bacc
    from concourse.bass_utils import run_bass_kernel_spmd

    a = {k: np.asarray(v) for k, v in inputs.items()}
    cat = np.concatenate
    arrays = {
        "x": a["x"].reshape(T, P),
        "ctxT": a["ctx_768"].reshape(T, CD).T,
        "packa": cat([a["L0_xattn_Wq"], a["L1_xattn_Wq"].T, a["L1_xattn_Wo"].T,
                      a["L0_ffn_gate_w"].T, a["L0_ffn_ws1"].T, a["L0_ffn_ws3"].T,
                      a["L1_ffn_Wr"]], axis=1),
        "packc": cat([cat([a["L0_xattn_Wk"], a["L0_xattn_bk"][None]], 0)[:, None],
                      cat([a["L0_xattn_Wv"], a["L0_xattn_bv"][None]], 0)[:, None],
                      cat([a["L1_xattn_Wk"].T, a["L1_xattn_bk"][None]], 0)[:, None],
                      cat([a["L1_xattn_Wv"].T, a["L1_xattn_bv"][None]], 0)[:, None]], axis=1),
        "biases": cat([a["L0_xattn_bq"][:, None], a["L1_xattn_bq"][:, None],
                       a["L1_ffn_b1"].reshape(E1, NF, P).transpose(2, 0, 1).reshape(P, E1 * NF),
                       a["L1_ffn_b2"].T], axis=1),
        "gateb": a["L0_ffn_gate_b"][None],
        "bo": a["L1_xattn_bo"][None],
        "ws2": a["L0_ffn_ws2"].T.reshape(2, I0, P).transpose(1, 0, 2),
        "w13": cat([a["L0_ffn_w1"], a["L0_ffn_w3"]], axis=1).transpose(2, 0, 1),
        "w2": a["L0_ffn_w2"].transpose(2, 0, 1),
        "ew1": a["L1_ffn_W1"].transpose(1, 0, 2),
        "ew2": a["L1_ffn_W2"].reshape(E1, NF, P, P).transpose(2, 0, 1, 3),
    }
    arrays = {f"in_{k}": np.ascontiguousarray(v) for k, v in arrays.items()}
    nc = bacc.Bacc("TRN2", target_bir_lowering=False, num_devices=1)
    args = [nc.dram_tensor(k, v.shape, mybir.dt.from_np(v.dtype), kind="ExternalInput").ap()
            for k, v in arrays.items()]
    args.append(nc.dram_tensor("out_x", (T, P), F32, kind="ExternalOutput").ap())
    build(nc, *args)
    r = run_bass_kernel_spmd(nc, [arrays], core_ids=[0])
    return r.results[0]["out_x"].reshape(a["x"].shape)
```

```python
from contextlib import ExitStack

import concourse.bass as bass
from concourse import mybir

F32 = mybir.dt.float32
F32R = mybir.dt.float32r
BF16 = mybir.dt.bfloat16
F16 = mybir.dt.float16
I32 = mybir.dt.int32
U32 = mybir.dt.uint32
ALU = mybir.AluOpType
ACT = mybir.ActivationFunctionType
X = mybir.AxisListType.X

P = 128
T = 1024
NC = T // P
NB = 4
TB = T // NB
KV = 256
CD = 96
EPS = 1e-5

E0, K0, CAP0, I0 = 64, 6, 64, 88
SI = 2 * I0
GE = 8
NG = E0 // GE
GS = GE * CAP0
NPAIR = GS // P
LNSCALE = 4096.0

NH, HD = 16, 8
PARTS_Q = (0, 1, 2, 0, 1, 2, 0, 1)
PARTS_K = (0, 0, 0, 1, 1, 1, 2, 2)
NCOMB = len(PARTS_Q)
KROWS = NCOMB * HD
VW = HD + 1
RING0 = 3
WCOLS = GE * (SI + P)
NPROB = 8
LAG = 16

TAIL_AT = {"transposes": 21, "division": 22, "normed transposes": 23, "normed copy": 24,
           "output": 25, "residual": 26}
TAIL_STEP = 6
TAIL_LAST = {6: dict(zip(TAIL_AT, (65, 65, 66, 66, 67, 67))),
             7: dict(zip(TAIL_AT, (66, 66, 68, 68, 69, 69)))}
STATISTICS, NORMALISE, NORM_T, NORMED, OPERANDS = (49, 69), (50, 70), (51, 71), (52, 71), (52, 71)
ROUTER_LOGITS, ROUTER_SUB, ROUTER_EXP, ROUTER_CHOICES = (53, 72), (54, 72), (55, 73), (55, 73)
ROUTER_RANKS, ROUTER_WEIGHTS, ROUTER_T, ROUTER_WT = (57, 74), (57, 74), (59, 76), (60, 76)
ROUTER_BANK, ROUTER_BANK_T, SUM_BANK = (1, 7), (0, 7), (7, 1)
TILE0 = NB * NH
QS = [(0, 0), (1, 0), (0, 1), (1, 1)] + [(e, h2) for e in range(2, 8) for h2 in range(2)]


def rows_at(q):
    return min(4 * q + 5, 63)


SCALE1 = 1.0 / float(HD) ** 0.5
SLOTS = LAG + 64 + 64 + 2

E1, F1 = 8, 512
RING1 = 3
CAP1 = int(T * 1.25 / E1)
NF = F1 // P

A_WQ0, A_WQ1, A_WO1, A_GATE, A_WS1, A_WS3, A_WR, A_END = 0, 128, 256, 384, 448, 624, 800, 808
B_BQ0, B_BQ1, B_B1, B_B2, B_END = 0, 1, 2, 34, 42


def view(ap, *dims):
    return bass.AP(ap.tensor, ap.offset, [list(ap.ap[0])] + [list(d) for d in dims])


def build(nc, x_in, ctx_in, packa_in, packc_in, bias_in, gateb_in, bo_in, ws2_in, w13_in, w2_in,
          ew1_in, ew2_in, out):
    with ExitStack() as ctx:
        def sb(name, shape, dt=F32):
            return ctx.enter_context(nc.sbuf_tensor(name, shape, dt))

        def sem(name):
            return ctx.enter_context(nc.semaphore(name))

        def sems(name, n):
            return [sem(f"{name}{i}") for i in range(n)]

        bank = [ctx.enter_context(nc.psum_tensor(f"bank{i}", [P, 512], F32)) for i in range(8)]

        ident = sb("ident", [P, P])
        identb = sb("identb", [P, P], BF16)
        tri = sb("tri", [P, P], BF16)
        ones = sb("ones", [P, P], BF16)
        iota_i = sb("iota_i", [P, E0], I32)
        iota_e = sb("iota_e", [P, E0])
        iota_s = sb("iota_s", [P, CAP0], BF16)
        mhalf = sb("mhalf", [P, 4])
        selw = sb("selw", [3 * E1, E1, P], BF16)

        x = sb("x", [P, NC, P])
        ctxT = sb("ctxT", [P, T])
        packa = sb("packa", [P, A_END])
        packc = sb("packc", [CD + 1, 4, P])
        biases = sb("biases", [P, B_END])
        gateb = sb("gateb", [P, E0])
        bo = sb("bo", [P, P])
        ws2 = sb("ws2", [I0, 2, P])
        st = sb("st", [P, NC, 6])
        mv = sb("mv", [P, NC, 2])
        veps = sb("veps", [P, NC])
        rstd = sb("rstd", [P, NC])
        xn = sb("xn", [P, NC, P])
        xnT = sb("xnT", [P, T])

        big = sb("big", [P, NH * T // 2])
        pbuf = sb("pbuf", [P, 2, NC * GS], BF16)
        work = pbuf[:, :, :].rearrange("p a n -> p (a n)").bitcast(F32)
        qbuf, kbuf, vbuf = sb("qbuf", [P, T]), sb("kbuf", [P, T]), sb("vbuf", [P, NC, P])
        frbuf = sb("frbuf", [P, 5120], F32R)
        splits = sb("splits", [P, 4, T], F32R)

        q0T, k0T, v0 = qbuf, kbuf, vbuf
        prob0 = work[:, 0:NC * KV].rearrange("p (c k) -> p c k", c=NC)
        probT0 = work[:, NC * KV:2 * NC * KV].rearrange("p (c k) -> p c k", c=NC)
        nm0, sum0, rs0 = sb("nm0", [P, NC]), sb("sum0", [P, NC]), sb("rs0", [P, NC])

        xh, xl = sb("xh", [P, NC, P], F16), sb("xl", [P, NC, P], F16)
        score, biased = sb("score", [P, NC, E0]), sb("biased", [P, NC, E0])
        ra, rb = sb("ra", [P, 512]), sb("rb", [P, 512])
        nmg, sumg, rsg = sb("nmg", [P, NC]), sb("sumg", [P, NC]), sb("rsg", [P, NC])
        top8 = sb("top8", [P, NC, 8])
        idx8 = sb("idx8", [P, NC, 8], U32)
        idxf = sb("idxf", [P, NC, 8])
        selb = sb("selb", [P, NC, E0], BF16)
        rk = sb("rk", [P, NG, NC, GE, 2], BF16)
        sparts = sb("sparts", [P, NC, E0, 3], BF16)
        sres = sb("sres", [P, NC, E0])
        hs = [qbuf[0:I0, :], kbuf[0:I0, :]]
        SH_BANKS = [(2, 3), (5, 6), (0, 1), (5, 6)]
        W_AT = 2 * SI
        def w13(e):
            at = (e // GE) % RING0 * WCOLS + (e % GE) * SI
            return big[:, at:at + SI]

        def w2(e):
            at = (e // GE) % RING0 * WCOLS + GE * SI + (e % GE) * P
            return big[0:I0, at:at + P]

        xb = ctxT[:, :].rearrange("p (a s) -> p a s", a=2)
        PTs = splits
        wslot = sb("wslot", [P, 2, NPAIR])
        sil, gv = sb("sil", [P, NPAIR, I0]), sb("gv", [P, NPAIR, I0])
        gT = sb("gT", [I0, NPAIR, P])
        yh = frbuf[:, 0:512].rearrange("p (j d) -> p j d", j=NPAIR)
        yl = frbuf[:, 512:1024].rearrange("p (j d) -> p j d", j=NPAIR)

        ks = sb("ks", [P, NH, T], BF16)
        qs = big[:, :].bitcast(BF16).rearrange("p (b h t) -> p b h t", b=NB, h=NH)
        parts = sb("parts", [P, 3, T], BF16)
        vaug = sb("vaug", [P, NC, NH, VW])
        nm1, nmr, rden = (score[:, :, :].rearrange("p c e -> p (c e)")[:, i * P:(i + 1) * P]
                          .rearrange("p (c h) -> p c h", c=NC) for i in range(3))
        nmp = sb("nmp", [P, NC, 2, 3, NH // 2], BF16)
        nmT = [t[0:24, :, :].rearrange("p c d -> p (c d)").bitcast(BF16) for t in (xh, xl)]
        prob1 = work.rearrange("p (r n) -> p r n", r=NPROB)
        qf, oun, onrm, onT = qbuf, qbuf, vbuf, kbuf

        ew = sb("ew", [P, RING1, 2, F1])
        xTh, xTl = frbuf[:, 0:T], frbuf[:, T:2 * T]
        w1h, w1l, w2h, w2l = (splits[:, i, :].rearrange("p (a f) -> p a f", a=2)
                              for i in range(4))
        act = work[:, 0:4 * 512].rearrange("p (r n) -> p r n", r=4)
        NA = 3
        acth = frbuf[:, 2 * T:2 * T + NA * 512].rearrange("p (r n) -> p r n", r=NA)
        actl = frbuf[:, 2 * T + NA * 512:2 * T + 2 * NA * 512].rearrange("p (r n) -> p r n", r=NA)
        accT = qbuf
        wbc = vbuf[:, :, :].rearrange("p c d -> p (c d)").rearrange("p (a t) -> p a t", a=2)
        ywt = kbuf[:, :].rearrange("p (a t) -> p a t", a=2)
        rp, rtop, ridxf, wtok, wres = (
            sres[:, :, :].rearrange("p c e -> p (c e)")[:, i * NC * E1:(i + 1) * NC * E1]
            .rearrange("p (c e) -> p c e", c=NC) for i in range(5))
        ridx = sb("ridx", [P, NC, 8], U32)
        roh = sb("roh", [P, NC, 2, E1], BF16)
        rkeep = sres[:, :, :].rearrange("p c e -> p (c e)")[:, 5 * NC * E1:7 * NC * E1].rearrange(
            "p (c k e) -> p c k e", c=NC, k=2)
        rtv, rsum = sb("rtv", [P, NC, 2]), sb("rsum", [P, NC])
        wparts = sb("wparts", [P, NC, 3, E1], BF16)
        wT = biased[0:3 * E1, :, :].rearrange("p c e -> p (c e)").bitcast(BF16)

        kscratch = nc.dram_tensor("k_parts", [3, P, T], BF16, kind="Internal").ap()
        qscratch = nc.dram_tensor("q_parts", [NB, 3, P, TB], BF16, kind="Internal").ap()

        ld_x, ld_ctx, ld_packa, ld_packc, ld_small = (
            sem("ld_x"), sem("ld_ctx"), sem("ld_packa"), sem("ld_packc"), sem("ld_small"))
        ld_w0, ld_w1 = sems("ld_w0_", NG), sems("ld_w1_", E1)
        c_row, c_all = sem("c_row"), sem("c_all")
        dve_step, pool_step = sem("dve_step"), sem("pool_step")
        ln_var, ln_rstd, ln_out, ln_tps, ln_tsb = (
            sem("ln_var"), sem("ln_rstd"), sem("ln_out"), sem("ln_tps"), sem("ln_tsb"))
        k0_ps, k0_sb, v0_ps, v0_sb = sem("k0_ps"), sem("k0_sb"), sem("v0_ps"), sem("v0_sb")
        k1_ps, k1_hi, k1_res, k1_mid, k1_lo = (
            sem("k1_ps"), sem("k1_hi"), sem("k1_res"), sem("k1_mid"), sem("k1_lo"))
        v1_ps, v1_sb, kd_out, ks_in = sem("v1_ps"), sem("v1_sb"), sem("kd_out"), sem("ks_in")
        q0_ps, q0_sb, s0_ps, m0_sb, p0_sb = (
            sem("q0_ps"), sem("q0_sb"), sem("s0_ps"), sem("m0_sb"), sem("p0_sb"))
        t0_ps, t0_sb, o0_ps, x1_sb = sem("t0_ps"), sem("t0_sb"), sem("o0_ps"), sem("x1_sb")
        g_ps, g_sub, g_exp, g_score, g_sel, g_rank, g_parts = (
            sem("g_ps"), sem("g_sub"), sem("g_exp"), sem("g_score"), sem("g_sel"), sem("g_rank"),
            sem("g_parts"))
        xhl_sb, sh_ps, sh_sil, sh_sb = sem("xhl_sb"), sem("sh_ps"), sem("sh_sil"), sem("sh_sb")
        e_P, e_G, e_xb, e_T, e_PTa, e_PTv = (
            sem("e_P"), sem("e_G"), sem("e_xb"), sem("e_T"), sem("e_PTa"), sem("e_PTv"))
        e_H, e_ws, e_sil, e_gv, e_gTp, e_gT = (
            sem("e_H"), sem("e_ws"), sem("e_sil"), sem("e_gv"), sem("e_gTp"), sem("e_gT"))
        e_Y, e_yh, e_yl, e_comb = sem("e_Y"), sem("e_yh"), sem("e_yl"), sem("e_comb")
        z_sb, z_T, x2_sb = sem("z_sb"), sem("z_T"), sem("x2_sb")
        q1_ps, q1_f, q1_hi, q1_res, q1_mid, q1_lo = (
            sem("q1_ps"), sem("q1_f"), sem("q1_hi"), sem("q1_res"), sem("q1_mid"), sem("q1_lo"))
        qd_out, qs_in, nm_in = sems("qd_out", 2), sems("qs_in", NB), sems("nm_in", 2 * NB)
        a_zero, a_S, a_max, a_nmp, a_nmTp, a_nmT, a_ST, a_exp = (
            sem("a_zero"), sem("a_S"), sem("a_max"), sem("a_nmp"), sem("a_nmTp"), sem("a_nmT"),
            sem("a_ST"), sem("a_exp"))
        a_O, a_oun, a_oT, a_on, a_onTp, a_onT, a_out, x3_sb = (
            sem("a_O"), sem("a_oun"), sem("a_oT"), sem("a_on"), sem("a_onTp"), sem("a_onT"),
            sem("a_out"), sem("x3_sb"))
        r_x, r_ps, r_sub, r_exp, r_oh, r_rank, r_wp, r_wTp, r_wT = (
            sem("r_x"), sem("r_ps"), sem("r_sub"), sem("r_exp"), sem("r_oh"), sem("r_rank"),
            sem("r_wp"), sem("r_wTp"), sem("r_wT"))
        f_split, f_H, f_act, f_hi, f_lo, f_Y, f_bc, f_wbc, f_yw, f_acc = (
            sem("f_split"), sem("f_H"), sem("f_act"), sem("f_hi"), sem("f_lo"), sem("f_Y"),
            sem("f_bc"), sem("f_wbc"), sem("f_yw"), sem("f_acc"))
        f_oT, x4_sb, st_out = sem("f_oT"), sem("x4_sb"), sem("st_out")

        def half(h2):
            return slice(h2 * 512, h2 * 512 + 512)

        def chunk(c):
            return slice(c * P, (c + 1) * P)

        def batch(b):
            return slice(b * TB, (b + 1) * TB)

        LN_BANK = [0, 1, 2, 3, 4, 5, 0, 7]
        NT = 2 * E1 * NF

        def shared_silu(i):
            return xb[0:I0, i % 2, :]

        def tail_chunk(step, e):
            for c in range(NC):
                if TAIL_LAST[c][step] == e if c in TAIL_LAST else (
                        NH * (c // 2) + TAIL_AT[step] + TAIL_STEP * (c % 2) == e):
                    return c
            return None

        block = ctx.enter_context(nc.Block())

        @block.sync
        def _(sp):
            def group_weights(g):
                at = g % RING0 * WCOLS
                es = slice(g * GE, (g + 1) * GE)
                sp.dma_start(big[:, at:at + GE * SI].rearrange("p (e i) -> p e i", e=GE),
                             w13_in[:, es, :]).then_inc(ld_w0[g], 16)
                sp.dma_start(big[0:I0, at + GE * SI:at + WCOLS].rearrange("p (e d) -> p e d", e=GE),
                             w2_in[:, es, :]).then_inc(ld_w0[g], 16)

            def expert_weights(e):
                sp.dma_start(ew[:, e % RING1, 0, :], ew1_in[:, e, :]).then_inc(ld_w1[e], 16)
                sp.dma_start(ew[:, e % RING1, 1, :].rearrange("p (f d) -> p f d", f=NF),
                             ew2_in[:, e, :, :]).then_inc(ld_w1[e], 16)

            sp.dma_start(ctxT[0:CD, :], ctx_in).then_inc(ld_ctx, 16)
            sp.dma_start(packc[:, :, :], packc_in).then_inc(ld_packc, 16)
            sp.dma_start(x[:, :, :], x_in.rearrange("(c p) d -> p c d", p=P)).then_inc(ld_x, 16)
            sp.dma_start(packa[:, :], packa_in).then_inc(ld_packa, 16)
            sp.dma_start(biases[:, :], bias_in).then_inc(ld_small, 16)
            sp.dma_start(gateb[:, :], gateb_in.to_broadcast([P, E0])).then_inc(ld_small, 16)
            sp.dma_start(bo[:, :], bo_in.to_broadcast([P, P])).then_inc(ld_small, 16)
            sp.dma_start(ws2[:, :, :], ws2_in).then_inc(ld_small, 16)
            for g in range(RING0):
                group_weights(g)
            for e in range(RING1):
                expert_weights(e)
            sp.wait_ge(k1_hi, 2)
            sp.wait_ge(k1_mid, 2)
            sp.wait_ge(k1_lo, 2)
            sp.dma_start(kscratch.rearrange("j p t -> p j t"), parts[:, :, :]).then_inc(kd_out, 16)
            sp.wait_ge(kd_out, 16)
            for i, part in enumerate(PARTS_K):
                sp.dma_start(ks[i * HD:(i + 1) * HD, :, :],
                             kscratch[part].rearrange("(d h) t -> d h t", d=HD)).then_inc(ks_in, 16)
            for g in range(RING0, NG):
                sp.wait_ge(e_Y, g - RING0 + 1)
                group_weights(g)
            for h2 in range(2):
                for part, ready in enumerate((q1_hi, q1_mid, q1_lo)):
                    sp.wait_ge(ready, h2 + 1)
                    sp.dma_start(
                        qscratch[2 * h2:2 * h2 + 2, part].rearrange("b p t -> p b t"),
                        parts[:, part, half(h2)].rearrange("p (b t) -> p b t", b=2)
                    ).then_inc(qd_out[h2], 16)
                sp.wait_ge(qd_out[h2], 48)
                for b in (2 * h2, 2 * h2 + 1):
                    rows = qscratch[b].rearrange("j (d h) t -> (j d) h t", d=HD)
                    for i in range(0, NCOMB, 3):
                        n = min(3, NCOMB - i)
                        sp.dma_start(qs[i * HD:(i + n) * HD, b, :, :],
                                     rows[0:n * HD]).then_inc(qs_in[b], 16)
            sp.wait_ge(c_all, 2)
            for k in range(2 * NB):
                b, hs8 = k // 2, slice(k % 2 * 8, k % 2 * 8 + 8)
                sp.wait_ge(a_nmT, k + 1)
                for part in range(3):
                    sp.dma_start(qs[KROWS + part:KROWS + part + 1, b, hs8, :],
                                 nmT[k % 2][part * 8:(part + 1) * 8, batch(b)]
                                 ).then_inc(nm_in[k], 16)
            for e in range(RING1, E1):
                sp.wait_ge(f_split, e - RING1 + 1)
                expert_weights(e)
            for h2 in range(2):
                sp.wait_ge(x4_sb, h2 + 1)
                sp.dma_start(out.rearrange("(c p) d -> p c d", p=P)[:, 4 * h2:4 * h2 + 4, :],
                             x[:, 4 * h2:4 * h2 + 4, :]).then_inc(st_out, 16)
            sp.wait_ge(st_out, 32)

        @block.gpsimd
        def _(pool):
            steps = [0]

            def chained(ins):
                steps[0] += 1
                ins.then_inc(pool_step, 1)
                pool.wait_ge(pool_step, steps[0])

            pool.memset(ctxT[CD:CD + 1, :], 1.0).then_inc(c_row, 1)
            pool.wait_ge(c_row, 1)
            pool.memset(mhalf[:, :], -0.5)
            pool.memset(ident[:, :], 0.0)
            pool.memset(identb[:, :], 0.0)
            chained(pool.memset(ones[:, :], 1.0))
            chained(pool.memset(selw[:, :, :], 0.0))
            pool.affine_select(out=ident[:, :], in_=ident[:, :], compare_op=ALU.not_equal, fill=1.0,
                               base=0, pattern=[[-1, P]], channel_multiplier=1)
            pool.affine_select(out=identb[:, :], in_=identb[:, :], compare_op=ALU.not_equal,
                               fill=1.0, base=0, pattern=[[-1, P]], channel_multiplier=1)
            pool.affine_select(out=tri[:, :], in_=ones[:, :], compare_op=ALU.is_ge, fill=0.0,
                               base=0, pattern=[[1, P]], channel_multiplier=-1)
            chained(pool.iota(iota_i[:, :], pattern=[[1, E0]], base=0, channel_multiplier=0))
            chained(pool.tensor_copy(iota_e[:, :], iota_i[:, :]))
            pool.tensor_scalar(iota_s[:, :], iota_e[:, :], 1.0, None, ALU.add).then_inc(c_all, 1)

            def power(step):
                cs = slice(4 * (step % 2), 4 * (step % 2) + 4)
                pool.wait_ge(ln_var, step + 1)
                if step >= 2:
                    pool.wait_ge(ln_out, step - 1)
                pool.tensor_tensor(out=rstd[:, cs], in0=veps[:, cs], in1=mhalf[:, :],
                                   op=ALU.pow).then_inc(ln_rstd, 1)

            power(0)
            power(1)
            for h2 in range(2):
                pool.wait_ge(k1_res, h2 + 1)
                pool.tensor_copy(parts[:, 1, half(h2)], (ra, rb)[h2][:, :]).then_inc(k1_mid, 1)
            power(2)
            power(3)
            pool.wait_ge(g_score, 1)
            chained(pool.tensor_copy(sparts[:, :, :, 0], score[:, :, :]))
            chained(pool.tensor_tensor(out=sres[:, :, :], in0=score[:, :, :],
                                       in1=sparts[:, :, :, 0], op=ALU.subtract))
            chained(pool.tensor_copy(sparts[:, :, :, 1], sres[:, :, :]))
            pool.tensor_tensor(out=sparts[:, :, :, 2], in0=sres[:, :, :],
                               in1=sparts[:, :, :, 1], op=ALU.subtract).then_inc(g_parts, 1)
            pool.wait_ge(g_parts, 1)
            for part in range(3):
                chained(pool.affine_select(
                    out=selw[:, :, :], in_=selw[:, :, :], compare_op=ALU.not_equal, fill=1.0,
                    base=-E1 * part, pattern=[[-1, E1], [0, P]], channel_multiplier=1))
            chained(pool.memset(ks[KROWS:P, :, :].bitcast(F32), 0.0))
            chained(pool.memset(ks[KROWS:KROWS + 3, :, :], 1.0))
            pool.wait_ge(e_Y, NG)
            pool.memset(big[KROWS:P, :], 0.0).then_inc(c_all, 1)
            pool.wait_ge(c_all, 2)
            power(4)
            power(5)
            pool.wait_ge(e_comb, NG + 1)
            for e in range(E1):
                if e == 2:
                    power(6)
                    power(7)
                pool.wait_ge(ld_w1[e], 32)
                if e >= 2:
                    pool.wait_ge(f_Y, NF * (1 + max(QS.index((e - 2, h2)) for h2 in range(2))))
                pool.tensor_copy(w1h[:, e % 2, :], ew[:, e % RING1, 0, :])
                chained(pool.tensor_copy(w2h[:, e % 2, :], ew[:, e % RING1, 1, :]))
                pool.tensor_tensor(out=w1l[:, e % 2, :], in0=ew[:, e % RING1, 0, :],
                                   in1=w1h[:, e % 2, :].bitcast(F32), op=ALU.subtract)
                pool.tensor_tensor(out=w2l[:, e % 2, :], in0=ew[:, e % RING1, 1, :],
                                   in1=w2h[:, e % 2, :].bitcast(F32),
                                   op=ALU.subtract).then_inc(f_split, 1)

        @block.scalar
        def _(a):
            for h2 in range(2):
                a.wait_ge(k0_ps, h2 + 1)
                a.copy(k0T[:, half(h2)], bank[h2][:, :]).then_inc(k0_sb, 1)
            for h2 in range(2):
                a.wait_ge(v0_ps, h2 + 1)
                a.copy(v0[:, 4 * h2:4 * h2 + 4, :],
                       bank[2 + h2][:, :].rearrange("p (c d) -> p c d", c=4)).then_inc(v0_sb, 1)
            for h2 in range(2):
                a.wait_ge(k1_ps, h2 + 1)
                a.copy(parts[:, 0, half(h2)], bank[4 + h2][:, :]).then_inc(k1_hi, 1)
            for h2 in range(2):
                a.wait_ge(v1_ps, h2 + 1)
                for c in range(4):
                    ins = a.copy(vaug[:, 4 * h2 + c, :, 0:HD],
                                 bank[6 + h2][:, chunk(c)].rearrange("p (h d) -> p h d", h=NH))
                ins.then_inc(v1_sb, 1)
            a.wait_ge(c_all, 1)
            a.copy(vaug[:, :, :, HD:HD + 1],
                   ones[:, :].rearrange("p (c h o) -> p c h o", c=NC, h=NH)).then_inc(v1_sb, 1)

            def norm_transposed(step):
                a.wait_ge(ln_tps, step + 1)
                a.copy(xnT[:, half(step % 2)], bank[LN_BANK[step]][:, :]).then_inc(ln_tsb, 1)

            norm_transposed(0)
            norm_transposed(1)

            def exp0(c):
                a.wait_ge(m0_sb, c + 1)
                a.activation(prob0[:, c, :], bank[4 + c % 2][:, 0:KV], ACT.Exp,
                             bias=nm0[:, c:c + 1], accum_out=sum0[:, c:c + 1]).then_inc(p0_sb, 1)

            exp0(0)
            for c in range(NC):
                if c + 1 < NC:
                    exp0(c + 1)
                a.wait_ge(t0_ps, c + 1)
                a.copy(probT0[:, c, :], bank[6 + c % 2][:, 0:KV]).then_inc(t0_sb, 1)
                if c == NC - 1:
                    norm_transposed(2)
            norm_transposed(3)
            a.wait_ge(g_sub, 1)
            a.activation(score[:, :, :], ra[:, :].rearrange("p (c e) -> p c e", c=NC),
                         ACT.Exp).then_inc(g_exp, 1)
            for i in range(4):
                a.wait_ge(sh_ps, i + 1)
                if i >= 2:
                    a.wait_ge(sh_sb, i - 1)
                a.activation(shared_silu(i), bank[SH_BANKS[i][0]][0:I0, :], ACT.Silu
                             ).then_inc(sh_sil, 1)
            def gathered(g):
                a.wait_ge(e_G, g + 1)
                if g >= 2:
                    a.wait_ge(e_H, 2 * (g - 1))
                a.mul(xb[:, g % 2, :], bank[2][:, :], 1.0 / LNSCALE).then_inc(e_xb, 1)

            gathered(0)
            for g in range(NG):
                a.wait_ge(e_ws, g + 1)
                for p2 in range(2):
                    a.wait_ge(e_H, 2 * g + p2 + 1)
                    if g >= 1:
                        a.wait_ge(e_gv, g)
                    a.activation(sil[:, 2 * p2:2 * p2 + 2, :],
                                 bank[5 + p2][:, 0:2 * SI].rearrange(
                                     "p (j i) -> p j i", j=2)[:, :, 0:I0],
                                 ACT.Silu).then_inc(e_sil, 1)
                a.wait_ge(e_T, NPAIR * g + 2)
                if g >= 1:
                    a.wait_ge(e_comb, g)
                a.copy(PTs[:, 1, :], bank[4][:, :].bitcast(BF16)).then_inc(e_PTa, 1)
                if g + 1 < NG:
                    gathered(g + 1)
                a.wait_ge(e_gTp, g + 1)
                a.copy(gT[:, :, :], bank[7][0:I0, :].rearrange(
                    "p (j s) -> p j s", j=NPAIR)).then_inc(e_gT, 1)
                a.wait_ge(e_T, NPAIR * g + 4)
                a.copy(PTs[:, 3, :], bank[4][:, :].bitcast(BF16)).then_inc(e_PTa, 1)
                a.wait_ge(e_Y, g + 1)
                a.copy(yh, bank[7][:, :].rearrange("p (j d) -> p j d", j=NPAIR)).then_inc(e_yh, 1)
            for h2 in range(2):
                a.wait_ge(e_comb, NG + h2)
                a.copy(xnT[:, half(h2)], bank[h2][:, :]).then_inc(z_sb, 1)
            a.wait_ge(z_T, 2)
            norm_transposed(4)
            norm_transposed(5)
            a.wait_ge(kd_out, 16)
            for h2 in range(2):
                a.wait_ge(q1_f, h2 + 1)
                a.copy(parts[:, 0, half(h2)], qf[:, half(h2)]).then_inc(q1_hi, 1)
                a.wait_ge(q1_res, h2 + 1)
                a.copy(parts[:, 1, half(h2)], (ra, rb)[h2][:, :]).then_inc(q1_mid, 1)

            for s in range(SLOTS):
                m, e = s, s - LAG
                if m % 8 == 2 and 1 <= m // 8 <= 2 * NB:
                    k = m // 8 - 1
                    a.wait_ge(a_nmTp, k + 1)
                    a.copy(nmT[k % 2][:, batch(k // 2)], bank[4][0:24, :].bitcast(BF16)[:, 0:TB]
                           ).then_inc(a_nmT, 1)
                for h2 in range(2):
                    if e == NORMED[h2]:
                        norm_transposed(6 + h2)
                    if e == ROUTER_EXP[h2]:
                        a.wait_ge(r_sub, h2 + 1)
                        a.activation(rp[:, 4 * h2:4 * h2 + 4, :], rp[:, 4 * h2:4 * h2 + 4, :],
                                     ACT.Exp).then_inc(r_exp, 1)
                    if e == ROUTER_WT[h2]:
                        a.wait_ge(r_wTp, h2 + 1)
                        a.copy(wT[:, half(h2)], bank[ROUTER_BANK_T[h2]][0:3 * E1, :].bitcast(
                            BF16)[:, half(h2)]).then_inc(r_wT, 1)
                if 0 <= e < NB * NH:
                    a.wait_ge(a_ST, e + 1)
                    if e >= NPROB:
                        a.wait_ge(a_O, (e - NPROB) // 4 + 1)
                    a.activation(prob1[:, e % NPROB, :], bank[2 + e % 2][:, :],
                                 ACT.Exp).then_inc(a_exp, 1)
                for o in range(2 * NB):
                    if e == min(8 * o + 12, NB * NH):
                        a.wait_ge(a_O, 2 * o + 2)
                        if o >= 2:
                            a.wait_ge(a_oT, 2 * (o // 2))
                        a.copy(oun[:, half(o % 2)], bank[5 + o % 2][:, :]).then_inc(a_oun, 1)
                c = tail_chunk("normed copy", e)
                if c is not None:
                    a.wait_ge(a_onTp, c + 1)
                    a.copy(onT[:, chunk(c)], bank[7][:, 0:P]).then_inc(a_onT, 1)
                n = e - TILE0
                if not 0 <= n < NT:
                    continue
                q, f = n // NF, n % NF
                expert = QS[q][0]
                a.wait_ge(f_H, n + 1)
                if n == 0:
                    a.wait_ge(a_O, 4 * NB - 1)
                if n >= 4:
                    a.wait_ge(f_lo, n - 3)
                bias = biases[:, B_B1 + expert * NF + f:B_B1 + expert * NF + f + 1]
                a.activation(act[:, n % 4, :], bank[n % 3][:, :], ACT.Gelu,
                             bias=bias).then_inc(f_act, 1)
                if n >= NA:
                    a.wait_ge(f_Y, n - NA + 1)
                a.activation(acth[:, n % NA, :], bank[n % 3][:, :], ACT.Gelu,
                             bias=bias).then_inc(f_hi, 1)
                for q in range(2 * E1):
                    if n == rows_at(q):
                        a.wait_ge(f_bc, q + 1)
                        if q >= 2:
                            a.wait_ge(f_yw, q - 1)
                        a.copy(wbc[:, q % 2, :], bank[5 + q % 2][:, :]).then_inc(f_wbc, 1)

        @block.tensor
        def _(pe):
            def mm(out_, lhsT, rhs, start=True, stop=True):
                return pe.matmul(out_, lhsT, rhs, start=start, stop=stop, skip_group_check=True)

            pe.wait_ge(ld_ctx, 16)
            pe.wait_ge(ld_packc, 16)
            pe.wait_ge(c_row, 1)
            ctxr = ctxT[0:CD + 1, :]
            for first, (wk, wv, k_ps, v_ps) in ((0, (0, 1, k0_ps, v0_ps)), (4, (2, 3, k1_ps, v1_ps))):
                for h2 in range(2):
                    mm(bank[first + h2][:, :], packc[:, wk, :], ctxr[:, half(h2)]).then_inc(k_ps, 1)
                for c in range(NC):
                    ins = mm(bank[first + 2 + c // 4][:, chunk(c % 4)], ctxr[:, chunk(c)],
                             packc[:, wv, :])
                    if c % 4 == 3:
                        ins.then_inc(v_ps, 1)

            def norm_transposes(step):
                pe.wait_ge(ln_out, step + 1)
                if step == 6:
                    pe.wait_ge(a_max, NB * NH)
                for i in range(4):
                    ins = pe.transpose(bank[LN_BANK[step]][:, chunk(i)],
                                       xn[:, 4 * (step % 2) + i, :], ident[:, :])
                ins.then_inc(ln_tps, 1)

            pe.wait_ge(c_all, 1)
            pe.wait_ge(k0_sb, 2)
            norm_transposes(0)
            norm_transposes(1)
            pe.wait_ge(ld_packa, 16)
            pe.wait_ge(v0_sb, 2)
            for h2 in range(2):
                pe.wait_ge(ln_tsb, h2 + 1)
                mm(bank[2 + h2][:, :], packa[:, A_WQ0:A_WQ0 + P], xnT[:, half(h2)]
                   ).then_inc(q0_ps, 1)

            def scores0(c):
                if c % 4 == 0:
                    pe.wait_ge(q0_sb, c // 4 + 1)
                if c >= 2:
                    pe.wait_ge(p0_sb, c - 1)
                mm(bank[4 + c % 2][:, 0:KV], q0T[:, chunk(c)], k0T[:, batch(c // 2)]
                   ).then_inc(s0_ps, 1)

            def values0(c):
                pe.wait_ge(t0_sb, c + 1)
                if c >= 2:
                    pe.wait_ge(x1_sb, c - 1)
                b = c // 2
                mm(bank[c % 2][:, 0:P], probT0[:, c, 0:P], v0[:, 2 * b, :], stop=False)
                mm(bank[c % 2][:, 0:P], probT0[:, c, P:KV], v0[:, 2 * b + 1, :],
                   start=False).then_inc(o0_ps, 1)

            pe.wait_ge(k1_hi, 2)
            pe.wait_ge(k1_res, 2)
            pe.wait_ge(v1_sb, 2)
            scores0(0)
            for c in range(NC):
                if c + 1 < NC:
                    scores0(c + 1)
                pe.wait_ge(p0_sb, c + 1)
                if c >= 2:
                    pe.wait_ge(t0_sb, c - 1)
                pe.transpose(bank[6 + c % 2][:, 0:P], prob0[:, c, 0:P], ident[:, :])
                pe.transpose(bank[6 + c % 2][:, P:KV], prob0[:, c, P:KV], ident[:, :]
                             ).then_inc(t0_ps, 1)
                if c == NC - 1:
                    norm_transposes(2)
                if c >= 1:
                    values0(c - 1)
            values0(NC - 1)

            norm_transposes(3)
            for h2 in range(2):
                pe.wait_ge(ln_tsb, 2 + h2 + 1)
                for i in range(4):
                    c = 4 * h2 + i
                    ins = mm(bank[4][:, c * E0:(c + 1) * E0], xnT[:, chunk(c)],
                             packa[:, A_GATE:A_GATE + E0])
            ins.then_inc(g_ps, 1)
            def shared_hidden(i):
                ih, h2 = i // 2, i % 2
                b1, b3 = SH_BANKS[i]
                mm(bank[b1][0:I0, :], packa[:, A_WS1 + ih * I0:A_WS1 + (ih + 1) * I0],
                   xnT[:, half(h2)])
                mm(bank[b3][0:I0, :], packa[:, A_WS3 + ih * I0:A_WS3 + (ih + 1) * I0],
                   xnT[:, half(h2)]).then_inc(sh_ps, 1)

            def shared_outputs():
                pe.wait_ge(ld_small, 64)
                pe.wait_ge(sh_sb, 4)
                for h2 in range(2):
                    for ih in range(2):
                        mm(bank[h2][:, :], ws2[:, ih, :], hs[ih][:, half(h2)],
                           start=(ih == 0), stop=False)

            shared_hidden(0)
            shared_hidden(1)
            pe.wait_ge(x1_sb, NC)
            shared_hidden(2)
            pe.wait_ge(g_sel, 1)
            for c in range(NC):
                o = bank[4][:, c * E0:(c + 1) * E0]
                for cc in range(c):
                    mm(o, ones[:, :], selb[:, cc, :], start=(cc == 0), stop=False)
                ins = mm(o, tri[:, :], selb[:, c, :], start=(c == 0))
            ins.then_inc(g_rank, 1)
            pe.wait_ge(sh_sb, 2)
            shared_hidden(3)

            def onehot(g, c, j):
                return pbuf[:, g % 2, c * GS + j * P:c * GS + (j + 1) * P]

            def gather(g):
                pe.wait_ge(e_P, g + 1)
                if g >= 1:
                    pe.wait_ge(e_xb, g)
                for c in range(NC):
                    for i, part in enumerate((xh, xl)):
                        ins = mm(bank[2][:, :], part[:, c, :],
                                 pbuf[:, g % 2, c * GS:(c + 1) * GS],
                                 start=(c == 0 and i == 0), stop=(c == NC - 1 and i == 1))
                ins.then_inc(e_G, 1)

            def combine(g):
                pe.wait_ge(e_PTa, 2 * (g + 1))
                pe.wait_ge(e_PTv, 2 * (g + 1))
                pe.wait_ge(e_yh, g + 1)
                pe.wait_ge(e_yl, g + 1)
                for h2 in range(2):
                    for j in range(NPAIR):
                        for y in (yh, yl):
                            ins = mm(bank[h2][:, :], y[:, j, :], PTs[:, j, half(h2)], start=False,
                                     stop=(g == NG - 1 and j == NPAIR - 1 and y is yl))
                    if h2 == 1 or g == NG - 1:
                        ins.then_inc(e_comb, 1)

            def slot_weights(g):
                if g >= 1:
                    pe.wait_ge(e_gv, g)
                for j in range(NPAIR):
                    for c in range(NC):
                        ins = mm(bank[5][:, W_AT + 6 * j:W_AT + 6 * j + 6], onehot(g, c, j),
                                 sparts[:, c, g * GE + 2 * j:g * GE + 2 * j + 2, :].rearrange(
                                     "p e k -> p (e k)"), start=(c == 0), stop=(c == NC - 1))

            def hidden(g):
                pe.wait_ge(e_xb, g + 1)
                pe.wait_ge(ld_w0[g], 32)
                for j in range(NPAIR):
                    for s in range(2):
                        ins = mm(bank[5 + j // 2][64 * s:64 * s + 64, (j % 2) * SI:(j % 2 + 1) * SI],
                                 xb[:, g % 2, j * P + 64 * s:j * P + 64 * s + 64],
                                 w13(g * GE + 2 * j + s))
                    if j % 2:
                        ins.then_inc(e_H, 1)

            def dispatch_transposes(g, j):
                if 2 * g + j // 2:
                    pe.wait_ge((e_PTv, e_PTa)[j % 2], 2 * g + j // 2)
                for c in range(NC):
                    ins = pe.transpose(bank[3 + j % 2][:, :].bitcast(BF16)[:, chunk(c)],
                                       onehot(g, c, j), identb[:, :])
                ins.then_inc(e_T, 1)

            def hidden_transposes(g):
                pe.wait_ge(e_gv, g + 1)
                if g >= 1:
                    pe.wait_ge(e_yl, g)
                for j in range(NPAIR):
                    ins = pe.transpose(bank[7][0:I0, chunk(j)], gv[:, j, :], ident[:, :])
                ins.then_inc(e_gTp, 1)

            def outputs(g):
                pe.wait_ge(e_gT, g + 1)
                for j in range(NPAIR):
                    for s in range(2):
                        ins = mm(bank[7][64 * s:64 * s + 64, chunk(j)],
                                 gT[:, j, 64 * s:64 * s + 64], w2(g * GE + 2 * j + s))
                ins.then_inc(e_Y, 1)

            pe.wait_ge(xhl_sb, 1)
            pe.wait_ge(g_parts, 1)
            gather(0)
            shared_outputs()
            for g in range(NG):
                slot_weights(g)
                hidden(g)
                if g >= 1:
                    combine(g - 1)
                dispatch_transposes(g, 0)
                dispatch_transposes(g, 1)
                if g + 1 < NG:
                    gather(g + 1)
                hidden_transposes(g)
                dispatch_transposes(g, 2)
                dispatch_transposes(g, 3)
                outputs(g)
            combine(NG - 1)

            for h2 in range(2):
                pe.wait_ge(z_sb, h2 + 1)
                for i in range(4):
                    ins = pe.transpose(bank[2 + h2][:, chunk(i)], xnT[:, chunk(4 * h2 + i)],
                                       ident[:, :])
                ins.then_inc(z_T, 1)
            norm_transposes(4)
            norm_transposes(5)
            for h2 in range(2):
                pe.wait_ge(ln_tsb, 4 + h2 + 1)
                mm(bank[6 + h2][:, :], packa[:, A_WQ1:A_WQ1 + P], xnT[:, half(h2)]
                   ).then_inc(q1_ps, 1)

            transposed = {"maxima": 0, "outputs": 0}

            def max_scores(m):
                b, hp, i = m // NH, m % NH // 2, m % 2
                if m >= 2:
                    pe.wait_ge(a_max, m - 1)
                if m % NH == 0:
                    pe.wait_ge(qs_in[b], 48)
                for j in range(2):
                    h = 2 * hp + j
                    ins = mm(bank[m % 2][:, j * KV:(j + 1) * KV], qs[:, b, h, chunk(i)],
                             ks[:, h, batch(b)])
                ins.then_inc(a_S, 1)

            def maxima_transposes(k):
                pe.wait_ge(a_nmp, k + 1)
                if transposed["outputs"]:
                    pe.wait_ge(a_on, transposed["outputs"])
                transposed["maxima"] += 1
                for i in range(2):
                    ins = pe.transpose(bank[4][0:24, :].bitcast(BF16)[:, chunk(i)],
                                       nmp[:, 2 * (k // 2) + i, k % 2, :, :].rearrange(
                                           "p j h -> p (j h)"),
                                       identb[:, :])
                ins.then_inc(a_nmTp, 1)

            def exp_scores(e):
                b, h = e // NH, e % NH
                if h % 8 == 0:
                    pe.wait_ge(nm_in[e // 8], 48)
                if e >= 2:
                    pe.wait_ge(a_exp, e - 1)
                for kc in range(2):
                    ins = mm(bank[2 + e % 2][:, kc * TB:(kc + 1) * TB],
                             ks[:, h, chunk(2 * b + kc)], qs[:, b, h, :])
                ins.then_inc(a_ST, 1)

            def head_values(hg):
                b, g4 = hg // 4, hg % 4
                pe.wait_ge(a_exp, 4 * hg + 4)
                if hg >= 4 and g4 % 2 == 0:
                    pe.wait_ge(a_oun, hg // 2 - 1)
                for kc in range(2):
                    for i in range(4):
                        h = 4 * g4 + i
                        ins = mm(bank[5 + g4 // 2][32 * i:32 * i + VW,
                                                   (g4 % 2) * TB:(g4 % 2 + 1) * TB],
                                 vaug[:, 2 * b + kc, h, :],
                                 prob1[:, (4 * hg + i) % NPROB, kc * TB:(kc + 1) * TB],
                                 start=(kc == 0), stop=(kc == 1))
                ins.then_inc(a_O, 1)

            def output_transposes(c):
                b, i = c // 2, c % 2
                pe.wait_ge(a_oun, 2 * b + 2)
                pe.wait_ge(a_nmT, transposed["maxima"])
                if c >= 1:
                    pe.wait_ge(a_on, c)
                transposed["outputs"] += 1
                for g4 in range(4):
                    at = g4 * TB + i * P
                    ins = pe.transpose(bank[4][:, chunk(g4)], oun[:, at:at + P], ident[:, :])
                ins.then_inc(a_oT, 1)

            def normed_transposes(c):
                pe.wait_ge(a_on, c + 1)
                if c >= 1:
                    pe.wait_ge(x3_sb, c)
                pe.transpose(bank[7][:, 0:P], onrm[:, c, :], ident[:, :]).then_inc(a_onTp, 1)

            def attention_out(c):
                pe.wait_ge(a_onT, c + 1)
                mm(bank[7][:, 0:P], onT[:, chunk(c)], packa[:, A_WO1:A_WO1 + P]).then_inc(a_out, 1)

            pe.wait_ge(a_zero, 1)
            pe.wait_ge(c_all, 2)
            pe.wait_ge(v1_sb, 3)
            pe.wait_ge(ks_in, 16 * NCOMB)
            def router_logits(h2):
                pe.wait_ge(ln_tsb, 6 + h2 + 1)
                if h2 == 0:
                    pe.wait_ge(a_max, NB * NH)
                for c in range(4 * h2, 4 * h2 + 4):
                    ins = mm(bank[ROUTER_BANK[h2]][:, c * E1:(c + 1) * E1], xnT[:, chunk(c)],
                             packa[:, A_WR:A_WR + E1])
                ins.then_inc(r_ps, 1)

            def router_ranks(h2):
                pe.wait_ge(r_oh, h2 + 1)
                for c in range(4 * h2, 4 * h2 + 4):
                    o = bank[ROUTER_BANK[h2]][:, c * 2 * E1:(c + 1) * 2 * E1]
                    for cc in range(c):
                        mm(o, ones[:, :], roh[:, cc, :, :].rearrange("p k e -> p (k e)"),
                           start=(cc == 0), stop=False)
                    ins = mm(o, tri[:, :], roh[:, c, :, :].rearrange("p k e -> p (k e)"),
                             start=(c == 0))
                ins.then_inc(r_rank, 1)

            def router_transposes(h2):
                pe.wait_ge(r_wp, h2 + 1)
                for c in range(4 * h2, 4 * h2 + 4):
                    ins = pe.transpose(
                        bank[ROUTER_BANK_T[h2]][0:3 * E1, :].bitcast(BF16)[:, chunk(c)],
                        wparts[:, c, :, :].rearrange("p k e -> p (k e)"), identb[:, :])
                ins.then_inc(r_wTp, 1)

            def ffn_hidden(n):
                q, f = n // NF, n % NF
                e, h2 = QS[q]
                if f == 0:
                    pe.wait_ge(f_split, e + 1)
                    pe.wait_ge(r_x, h2 + 1)
                if n == 0:
                    pe.wait_ge(r_wT, 1)
                if n == 2:
                    pe.wait_ge(a_exp, NB * NH - 1)
                if n >= 3:
                    pe.wait_ge(f_hi, n - 2)
                wh, wl = w1h[:, e % 2, chunk(f)], w1l[:, e % 2, chunk(f)]
                o = bank[n % 3][:, :]
                mm(o, wh, xTh[:, half(h2)], stop=False)
                mm(o, wh, xTl[:, half(h2)], start=False, stop=False)
                mm(o, wl, xTh[:, half(h2)], start=False).then_inc(f_H, 1)

            def ffn_out(n):
                q, f = n // NF, n % NF
                e = QS[q][0]
                if n == 0:
                    pe.wait_ge(a_exp, NB * NH)
                if n == NF:
                    pe.wait_ge(a_on, NC)
                if f == 0 and q >= 2:
                    pe.wait_ge(f_yw, q - 1)
                pe.wait_ge(f_hi, n + 1)
                pe.wait_ge(f_lo, n + 1)
                wh, wl = w2h[:, e % 2, chunk(f)], w2l[:, e % 2, chunk(f)]
                o = bank[3 + q % 2][:, :]
                mm(o, wh, acth[:, n % NA, :], start=(f == 0), stop=False)
                mm(o, wh, actl[:, n % NA, :], start=False, stop=False)
                mm(o, wl, acth[:, n % NA, :], start=False, stop=(f == NF - 1)).then_inc(f_Y, 1)

            def weight_rows(q):
                e, h2 = QS[q]
                pe.wait_ge(r_wT, h2 + 1)
                if q < 2:
                    pe.wait_ge(a_oun, 2 * NB)
                else:
                    pe.wait_ge(f_wbc, q - 1)
                mm(bank[5 + q % 2][:, :], selw[:, e, :], wT[:, half(h2)]).then_inc(f_bc, 1)

            def sum_transposes(h2):
                pe.wait_ge(f_acc, 2 * (E1 - 1) - 1 + h2)
                if h2 == 0:
                    pe.wait_ge(r_wT, 2)
                for i in range(4):
                    ins = pe.transpose(bank[SUM_BANK[h2]][:, chunk(i)],
                                       accT[:, chunk(4 * h2 + i)], ident[:, :])
                ins.then_inc(f_oT, 1)

            tail_steps = {"transposes": output_transposes, "normed transposes": normed_transposes,
                          "output": attention_out}
            for s in range(SLOTS):
                m, e = s, s - LAG
                if m < NB * NH:
                    max_scores(m)
                if m % 8 == 1 and 1 <= m // 8 <= 2 * NB:
                    maxima_transposes(m // 8 - 1)
                if 0 <= e < NB * NH:
                    exp_scores(e)
                for name in ("normed transposes", "output", "transposes"):
                    c = tail_chunk(name, e)
                    if c is not None:
                        tail_steps[name](c)
                for h2 in range(2):
                    for at, step in ((NORM_T, norm_transposes), (ROUTER_LOGITS, router_logits),
                                     (ROUTER_RANKS, router_ranks),
                                     (ROUTER_T, router_transposes)):
                        if e == at[h2]:
                            step(6 + h2 if step is norm_transposes else h2)
                n = e - TILE0
                if 0 <= n < NT:
                    ffn_hidden(n)
                for hg in range(4 * NB):
                    if e == min(4 * hg + 6, NB * NH):
                        head_values(hg)
                for q in range(2 * E1):
                    if n == rows_at(q):
                        weight_rows(q)
                if n == NT + 1:
                    sum_transposes(0)
                if 2 <= n < NT + 2:
                    ffn_out(n - 2)
            sum_transposes(1)

        @block.vector
        def _(v):
            steps = [0]

            def chained(ins):
                steps[0] += 1
                ins.then_inc(dve_step, 1)
                v.wait_ge(dve_step, steps[0])

            def statistics(step):
                cs = range(4 * (step % 2), 4 * (step % 2) + 4)
                for c in cs:
                    ins = v.bn_stats(st[:, c, :], x[:, c, :])
                chained(ins)
                for c in cs:
                    ins = v.bn_aggr(mv[:, c, :], st[:, c, :])
                chained(ins)
                v.tensor_scalar(veps[:, cs[0]:cs[-1] + 1], mv[:, cs[0]:cs[-1] + 1, 1], EPS, None,
                                ALU.add).then_inc(ln_var, 1)

            def normalise(step):
                v.wait_ge(ln_rstd, step + 1)
                if step >= 2:
                    v.wait_ge(ln_tps, step - 1)
                for c in range(4 * (step % 2), 4 * (step % 2) + 4):
                    ins = v.tensor_scalar(xn[:, c, :], x[:, c, :], mv[:, c, 0:1], rstd[:, c:c + 1],
                                          ALU.subtract, ALU.mult)
                ins.then_inc(ln_out, 1)

            v.wait_ge(ld_x, 16)
            statistics(0)
            statistics(1)
            normalise(0)
            normalise(1)
            for h2 in range(2):
                v.wait_ge(k1_hi, h2 + 1)
                v.tensor_tensor(out=(ra, rb)[h2][:, :], in0=bank[4 + h2][:, :],
                                in1=parts[:, 0, half(h2)], op=ALU.subtract).then_inc(k1_res, 1)
            v.wait_ge(ld_small, 64)
            for h2 in range(2):
                v.wait_ge(q0_ps, h2 + 1)
                v.tensor_scalar(q0T[:, half(h2)], bank[2 + h2][:, :], biases[:, B_BQ0:B_BQ0 + 1],
                                float(P) ** -0.5, ALU.add, ALU.mult).then_inc(q0_sb, 1)
            for h2 in range(2):
                v.wait_ge(k1_mid, h2 + 1)
                v.tensor_tensor(out=parts[:, 2, half(h2)], in0=(ra, rb)[h2][:, :],
                                in1=parts[:, 1, half(h2)], op=ALU.subtract).then_inc(k1_lo, 1)

            def maximum0(c):
                v.wait_ge(s0_ps, c + 1)
                v.tensor_reduce(nm0[:, c:c + 1], bank[4 + c % 2][:, 0:KV], X, ALU.max,
                                negate=True).then_inc(m0_sb, 1)

            def residual1(c):
                v.wait_ge(p0_sb, c + 1)
                chained(v.reciprocal(rs0[:, c:c + 1], sum0[:, c:c + 1]))
                v.wait_ge(o0_ps, c + 1)
                v.scalar_tensor_tensor(out=x[:, c, :], in0=bank[c % 2][:, 0:P],
                                       scalar=rs0[:, c:c + 1], in1=x[:, c, :], op0=ALU.mult,
                                       op1=ALU.add).then_inc(x1_sb, 1)

            maximum0(0)
            for c in range(NC):
                if c + 1 < NC:
                    maximum0(c + 1)
                if c >= 1:
                    residual1(c - 1)
                if c == 5:
                    v.wait_ge(x1_sb, 4)
                    statistics(2)
                if c == 6:
                    normalise(2)
            residual1(NC - 1)

            v.wait_ge(x1_sb, NC)
            statistics(3)
            normalise(3)
            v.wait_ge(ln_out, 4)
            chained(v.tensor_scalar(xh[:, :, :], xn[:, :, :], LNSCALE, None, ALU.mult))
            v.scalar_tensor_tensor(out=xl[:, :, :], in0=xn[:, :, :], scalar=LNSCALE,
                                   in1=xh[:, :, :], op0=ALU.mult,
                                   op1=ALU.subtract).then_inc(xhl_sb, 1)
            logits = bank[4][:, :].rearrange("p (c e) -> p c e", c=NC)
            v.wait_ge(g_ps, 1)
            chained(v.tensor_reduce(nmg[:, :], logits, X, ALU.max, negate=True))
            v.tensor_tensor(out=ra[:, :].rearrange("p (c e) -> p c e", c=NC), in0=logits,
                            in1=view(nmg[:, :], (1, NC), (0, E0)), op=ALU.add).then_inc(g_sub, 1)

            def shared_product(i):
                ih, h2 = i // 2, i % 2
                v.wait_ge(sh_sil, i + 1)
                v.tensor_tensor(out=hs[ih][:, half(h2)], in0=bank[SH_BANKS[i][1]][0:I0, :],
                                in1=shared_silu(i), op=ALU.mult).then_inc(sh_sb, 1)

            v.wait_ge(g_exp, 1)
            chained(v.reduce_sum(sumg[:, :], score[:, :, :], X))
            chained(v.reciprocal(rsg[:, :], sumg[:, :]))
            v.tensor_tensor(out=score[:, :, :], in0=score[:, :, :],
                            in1=view(rsg[:, :], (1, NC), (0, E0)), op=ALU.mult
                            ).then_inc(g_score, 1)
            v.wait_ge(g_score, 1)
            chained(v.tensor_tensor(out=biased[:, :, :], in0=score[:, :, :],
                                    in1=view(gateb[:, :], (0, NC), (1, E0)), op=ALU.add))
            for c in range(NC):
                ins = v.max(out=top8[:, c, :], in_=biased[:, c, :])
            chained(ins)
            for c in range(NC):
                ins = v.max_index(out=idx8[:, c, :], in_max=top8[:, c, :], in_values=biased[:, c, :])
            chained(ins)
            chained(v.tensor_copy(idxf[:, :, :], idx8[:, :, :]))
            lowest = view(top8[:, 0, K0 - 1:K0], (8, NC), (0, E0))
            lowest_at = view(idxf[:, 0, K0 - 1:K0], (8, NC), (0, E0))
            ra3, rb3 = (t[:, :].rearrange("p (c e) -> p c e", c=NC) for t in (ra, rb))
            v.tensor_tensor(out=ra3, in0=view(iota_e[:, :], (0, NC), (1, E0)), in1=lowest_at,
                            op=ALU.is_le)
            chained(v.tensor_tensor(out=rb3, in0=biased[:, :, :], in1=lowest, op=ALU.is_equal))
            v.tensor_tensor(out=ra3, in0=ra3, in1=rb3, op=ALU.mult)
            chained(v.tensor_tensor(out=biased[:, :, :], in0=biased[:, :, :], in1=lowest,
                                    op=ALU.is_gt))
            v.tensor_tensor(out=selb[:, :, :], in0=ra3, in1=biased[:, :, :],
                            op=ALU.add).then_inc(g_sel, 1)
            for i in range(3):
                shared_product(i)
            v.wait_ge(g_rank, 1)
            for c in range(NC):
                ins = v.tensor_tensor(out=view(rk[:, 0, c, 0, 0:1], (NC * GE * 2, NG), (2, GE), (1, 2)),
                                      in0=view(bank[4][:, c * E0:c * E0 + 1], (GE, NG), (1, GE), (0, 2)),
                                      in1=view(selb[:, c, 0:1], (GE, NG), (1, GE), (0, 2)),
                                      op=ALU.mult)
            chained(ins)

            def dispatch(g):
                if g >= 2:
                    v.wait_ge(e_T, NPAIR * (g - 1))
                v.tensor_tensor(out=view(pbuf[:, g % 2, 0:1], (CAP0, NC * GE), (2, CAP0 // 2), (1, 2)),
                                in0=view(rk[:, g, 0, 0, 0:1], (2, NC * GE), (0, CAP0 // 2), (1, 2)),
                                in1=view(iota_s[:, 0:1], (0, NC * GE), (2, CAP0 // 2), (1, 2)),
                                op=ALU.is_equal).then_inc(e_P, 1)

            dispatch(0)
            shared_product(3)
            dispatch(1)
            for g in range(NG):
                v.wait_ge(e_H, 2 * g + 1)
                for s in range(2):
                    ps = slice(64 * s, 64 * s + 64)
                    ins = v.reduce_sum(wslot[ps, g % 2, :],
                                       view(bank[5][ps, W_AT + 3 * s:W_AT + 3 * s + 1],
                                            (6, NPAIR), (1, 3)), X)
                ins.then_inc(e_ws, 1)
                v.wait_ge(e_ws, g + 1)
                v.wait_ge(e_sil, 2 * g + 2)
                if g >= 1:
                    v.wait_ge(e_gTp, g)
                for j in range(NPAIR):
                    at = (j % 2) * SI + I0
                    ins = v.scalar_tensor_tensor(out=gv[:, j, :], in0=bank[5 + j // 2][:, at:at + I0],
                                                 scalar=wslot[:, g % 2, j:j + 1], in1=sil[:, j, :],
                                                 op0=ALU.mult, op1=ALU.mult)
                ins.then_inc(e_gv, 1)
                for i in range(2):
                    v.wait_ge(e_T, NPAIR * g + 2 * i + 1)
                    if g >= 1:
                        v.wait_ge(e_comb, g)
                    v.tensor_copy(PTs[:, 2 * i, :], bank[3][:, :].bitcast(BF16)).then_inc(e_PTv, 1)
                v.wait_ge(e_yh, g + 1)
                v.tensor_tensor(out=yl, in0=bank[7][:, :].rearrange("p (j d) -> p j d", j=NPAIR),
                                in1=yh.bitcast(F32), op=ALU.subtract).then_inc(e_yl, 1)
                if g + 2 < NG:
                    dispatch(g + 2)

            for h2 in range(2):
                v.wait_ge(z_T, h2 + 1)
                xh2 = x[:, 4 * h2:4 * h2 + 4, :]
                v.tensor_tensor(out=xh2, in0=xh2,
                                in1=bank[2 + h2][:, :].rearrange("p (c d) -> p c d", c=4),
                                op=ALU.add).then_inc(x2_sb, 1)
                v.wait_ge(x2_sb, h2 + 1)
                statistics(4 + h2)
            normalise(4)
            normalise(5)
            def queries(h2):
                v.wait_ge(q1_ps, h2 + 1)
                v.tensor_scalar(qf[:, half(h2)], bank[6 + h2][:, :], biases[:, B_BQ1:B_BQ1 + 1],
                                SCALE1, ALU.add, ALU.mult).then_inc(q1_f, 1)
                v.wait_ge(q1_hi, h2 + 1)
                v.tensor_tensor(out=(ra, rb)[h2][:, :], in0=qf[:, half(h2)],
                                in1=parts[:, 0, half(h2)], op=ALU.subtract).then_inc(q1_res, 1)

            def queries_low(h2):
                v.wait_ge(q1_mid, h2 + 1)
                v.tensor_tensor(out=parts[:, 2, half(h2)], in0=(ra, rb)[h2][:, :],
                                in1=parts[:, 1, half(h2)], op=ALU.subtract).then_inc(q1_lo, 1)

            queries(0)
            queries_low(0)
            queries(1)
            queries_low(1)
            v.tensor_tensor(out=x[:, :, :], in0=x[:, :, :], in1=view(bo[:, :], (0, NC), (1, P)),
                            op=ALU.add).then_inc(x2_sb, 1)
            v.wait_ge(ln_tsb, 6)
            v.memset(bank[5][:, :], 0.0)
            v.memset(bank[6][:, :], 0.0).then_inc(a_zero, 1)

            def operands(h2):
                v.wait_ge(ln_tsb, 6 + h2 + 1)
                chained(v.tensor_copy(xTh[:, half(h2)], xnT[:, half(h2)]))
                v.tensor_tensor(out=xTl[:, half(h2)], in0=xnT[:, half(h2)],
                                in1=xTh[:, half(h2)].bitcast(F32), op=ALU.subtract
                                ).then_inc(r_x, 1)

            def router_less_maximum(h2):
                cs = slice(4 * h2, 4 * h2 + 4)
                logits = bank[ROUTER_BANK[h2]][:, h2 * 4 * E1:(h2 + 1) * 4 * E1].rearrange(
                    "p (c e) -> p c e", c=4)
                v.wait_ge(r_ps, h2 + 1)
                chained(v.tensor_reduce(rsum[:, cs], logits, X, ALU.max, negate=True))
                v.tensor_tensor(out=rp[:, cs, :], in0=logits, in1=view(rsum[:, cs], (1, 4), (0, E1)),
                                op=ALU.add).then_inc(r_sub, 1)

            def router_choices(h2):
                cs, first = slice(4 * h2, 4 * h2 + 4), 4 * h2
                v.wait_ge(r_exp, h2 + 1)
                for c in range(first, first + 4):
                    ins = v.max(out=rtop[:, c, :], in_=rp[:, c, :])
                chained(ins)
                for c in range(first, first + 4):
                    ins = v.max_index(out=ridx[:, c, :], in_max=rtop[:, c, :],
                                      in_values=rp[:, c, :])
                chained(ins)
                chained(v.tensor_copy(ridxf[:, cs, :], ridx[:, cs, :]))
                v.tensor_tensor(out=roh[:, cs, :, :],
                                in0=view(iota_e[:, :], (0, 4), (0, 2), (1, E1)),
                                in1=view(ridxf[:, first, 0:1], (8, 4), (1, 2), (0, E1)),
                                op=ALU.is_equal).then_inc(r_oh, 1)
                v.wait_ge(r_oh, h2 + 1)
                chained(v.tensor_tensor(out=rsum[:, cs], in0=rtop[:, cs, 0], in1=rtop[:, cs, 1],
                                        op=ALU.add))
                chained(v.reciprocal(rsum[:, cs], rsum[:, cs]))
                chained(v.tensor_tensor(out=rtv[:, cs, :], in0=rtop[:, cs, 0:2],
                                        in1=view(rsum[:, cs], (1, 4), (0, 2)), op=ALU.mult))

            def router_weights(h2):
                cs, first, n = slice(4 * h2, 4 * h2 + 4), 4 * h2, 4 * 2 * E1
                v.wait_ge(r_rank, h2 + 1)
                chained(v.scalar_tensor_tensor(
                    out=rkeep[:, cs, :, :].rearrange("p c k e -> p (c k e)"),
                    in0=bank[ROUTER_BANK[h2]][:, h2 * n:(h2 + 1) * n], scalar=float(CAP1),
                    in1=roh[:, cs, :, :].rearrange("p c k e -> p (c k e)"),
                    op0=ALU.is_le, op1=ALU.mult))
                chained(v.tensor_tensor(out=rkeep[:, cs, :, :], in0=rkeep[:, cs, :, :],
                                        in1=view(rtv[:, first, 0:1], (2, 4), (1, 2), (0, E1)),
                                        op=ALU.mult))
                chained(v.tensor_tensor(out=wtok[:, cs, :], in0=rkeep[:, cs, 0, :],
                                        in1=rkeep[:, cs, 1, :], op=ALU.add))
                chained(v.tensor_copy(wparts[:, cs, 0, :], wtok[:, cs, :]))
                chained(v.tensor_tensor(out=wres[:, cs, :], in0=wtok[:, cs, :],
                                        in1=wparts[:, cs, 0, :], op=ALU.subtract))
                chained(v.tensor_copy(wparts[:, cs, 1, :], wres[:, cs, :]))
                v.tensor_tensor(out=wparts[:, cs, 2, :], in0=wres[:, cs, :],
                                in1=wparts[:, cs, 1, :], op=ALU.subtract).then_inc(r_wp, 1)

            sums = [0]

            def weighted(q):
                e, h2 = QS[q]
                v.wait_ge(f_Y, NF * (q + 1))
                v.wait_ge(f_wbc, q + 1)
                dst = accT[:, half(h2)] if e == 0 else ywt[:, h2, :]
                v.scalar_tensor_tensor(out=dst, in0=bank[3 + q % 2][:, :],
                                       scalar=biases[:, B_B2 + e:B_B2 + e + 1],
                                       in1=wbc[:, q % 2, :], op0=ALU.add,
                                       op1=ALU.mult).then_inc(f_yw, 1)
                if e >= 1:
                    v.wait_ge(f_yw, q + 1)
                    if sums[0]:
                        v.wait_ge(f_acc, sums[0])
                    sums[0] += 1
                    v.tensor_tensor(out=accT[:, half(h2)], in0=accT[:, half(h2)], in1=dst,
                                    op=ALU.add).then_inc(f_acc, 1)

            for s in range(SLOTS):
                m, e = s, s - LAG
                if m < NB * NH:
                    c, hp = 2 * (m // NH) + m % 2, m % NH // 2
                    v.wait_ge(a_S, m + 1)
                    v.tensor_reduce(nm1[:, c, 2 * hp:2 * hp + 2],
                                    bank[m % 2][:, :].rearrange("p (h k) -> p h k", h=2), X,
                                    ALU.max, negate=True).then_inc(a_max, 1)
                    if m % 8 == 7:
                        k = m // 8
                        cs, h8 = slice(2 * (k // 2), 2 * (k // 2) + 2), slice(k % 2 * 8, k % 2 * 8 + 8)
                        v.wait_ge(a_max, m + 1)
                        chained(v.tensor_copy(nmp[:, cs, k % 2, 0, :], nm1[:, cs, h8]))
                        chained(v.tensor_tensor(out=nmr[:, cs, h8], in0=nm1[:, cs, h8],
                                                in1=nmp[:, cs, k % 2, 0, :], op=ALU.subtract))
                        chained(v.tensor_copy(nmp[:, cs, k % 2, 1, :], nmr[:, cs, h8]))
                        v.tensor_tensor(out=nmp[:, cs, k % 2, 2, :], in0=nmr[:, cs, h8],
                                        in1=nmp[:, cs, k % 2, 1, :],
                                        op=ALU.subtract).then_inc(a_nmp, 1)
                c = tail_chunk("division", e)
                if c is not None:
                    v.wait_ge(a_oT, c + 1)
                    chained(v.reciprocal(rden[:, c, :], view(bank[4][:, HD:HD + 1], (32, NH))))
                    v.tensor_tensor(out=onrm[:, c, :].rearrange("p (h d) -> p h d", h=NH),
                                    in0=view(bank[4][:, 0:1], (32, NH), (1, HD)),
                                    in1=view(rden[:, c, :], (1, NH), (0, HD)),
                                    op=ALU.mult).then_inc(a_on, 1)
                c = tail_chunk("residual", e)
                if c is not None:
                    v.wait_ge(a_out, c + 1)
                    if c == 0:
                        v.wait_ge(x2_sb, 3)
                    v.tensor_tensor(out=x[:, c, :], in0=x[:, c, :], in1=bank[7][:, 0:P],
                                    op=ALU.add).then_inc(x3_sb, 1)
                for h2 in range(2):
                    if e == STATISTICS[h2]:
                        v.wait_ge(x3_sb, 4 * h2 + 4)
                        statistics(6 + h2)
                    if e == NORMALISE[h2]:
                        normalise(6 + h2)
                    if e == OPERANDS[h2]:
                        operands(h2)
                    if e == ROUTER_SUB[h2]:
                        router_less_maximum(h2)
                    if e == ROUTER_CHOICES[h2]:
                        router_choices(h2)
                    if e == ROUTER_WEIGHTS[h2]:
                        router_weights(h2)
                n = e - TILE0
                if not 0 <= n < NT:
                    continue
                v.wait_ge(f_act, n + 1)
                v.wait_ge(f_hi, n + 1)
                if n >= NA:
                    v.wait_ge(f_Y, n - NA + 1)
                v.tensor_tensor(out=actl[:, n % NA, :], in0=act[:, n % 4, :],
                                in1=acth[:, n % NA, :].bitcast(F32), op=ALU.subtract
                                ).then_inc(f_lo, 1)
                for q in range(2 * E1 - 1):
                    if n == min(rows_at(q) + 1, NT - 1):
                        weighted(q)
            weighted(2 * E1 - 1)
            for h2 in range(2):
                v.wait_ge(f_oT, h2 + 1)
                xh2 = x[:, 4 * h2:4 * h2 + 4, :]
                v.tensor_tensor(out=xh2, in0=xh2,
                                in1=bank[SUM_BANK[h2]][:, :].rearrange("p (c d) -> p c d", c=4),
                                op=ALU.add).then_inc(x4_sb, 1)


def kernel(**inputs):
    import numpy as np
    import concourse.bacc as bacc
    from concourse.bass_utils import run_bass_kernel_spmd

    a = {k: np.asarray(v) for k, v in inputs.items()}
    cat = np.concatenate

    def by_feature(w):
        return w.reshape(-1, NH, HD).transpose(0, 2, 1).reshape(-1, P)

    arrays = {
        "x": a["x"].reshape(T, P),
        "ctxT": a["ctx_768"].reshape(T, CD).T,
        "packa": cat([a["L0_xattn_Wq"], by_feature(a["L1_xattn_Wq"].T), a["L1_xattn_Wo"].T,
                      a["L0_ffn_gate_w"].T, a["L0_ffn_ws1"].T, a["L0_ffn_ws3"].T,
                      a["L1_ffn_Wr"]], axis=1),
        "packc": cat([cat([a["L0_xattn_Wk"], a["L0_xattn_bk"][None]], 0)[:, None],
                      cat([a["L0_xattn_Wv"], a["L0_xattn_bv"][None]], 0)[:, None],
                      by_feature(cat([a["L1_xattn_Wk"].T, a["L1_xattn_bk"][None]], 0))[:, None],
                      cat([a["L1_xattn_Wv"].T, a["L1_xattn_bv"][None]], 0)[:, None]], axis=1),
        "biases": cat([a["L0_xattn_bq"][:, None], by_feature(a["L1_xattn_bq"]).T,
                       a["L1_ffn_b1"].reshape(E1, NF, P).transpose(2, 0, 1).reshape(P, E1 * NF),
                       a["L1_ffn_b2"].T], axis=1),
        "gateb": a["L0_ffn_gate_b"][None],
        "bo": a["L1_xattn_bo"][None],
        "ws2": a["L0_ffn_ws2"].T.reshape(2, I0, P).transpose(1, 0, 2),
        "w13": cat([a["L0_ffn_w1"], a["L0_ffn_w3"]], axis=1).transpose(2, 0, 1),
        "w2": a["L0_ffn_w2"].transpose(2, 0, 1),
        "ew1": a["L1_ffn_W1"].transpose(1, 0, 2),
        "ew2": a["L1_ffn_W2"].reshape(E1, NF, P, P).transpose(2, 0, 1, 3),
    }
    arrays = {f"in_{k}": np.ascontiguousarray(v) for k, v in arrays.items()}
    nc = bacc.Bacc("TRN2", target_bir_lowering=False, num_devices=1)
    args = [nc.dram_tensor(k, v.shape, mybir.dt.from_np(v.dtype), kind="ExternalInput").ap()
            for k, v in arrays.items()]
    args.append(nc.dram_tensor("out_x", (T, P), F32, kind="ExternalOutput").ap())
    build(nc, *args)
    r = run_bass_kernel_spmd(nc, [arrays], core_ids=[0])
    return r.results[0]["out_x"].reshape(a["x"].shape)
```

```python
from contextlib import ExitStack

import concourse.bass as bass
from concourse import mybir

F32 = mybir.dt.float32
F32R = mybir.dt.float32r
BF16 = mybir.dt.bfloat16
I32 = mybir.dt.int32
U32 = mybir.dt.uint32
ALU = mybir.AluOpType
ACT = mybir.ActivationFunctionType
X = mybir.AxisListType.X

P = 128
T = 1024
NC = T // P
NB = 4
TB = T // NB
KV = TB
CD = 96
EPS = 1e-5

E0, K0, CAP0, I0 = 64, 6, 64, 88
SI = 2 * I0
GE = 8
NG = E0 // GE
GS = GE * CAP0
NPAIR = GS // P

NH, HD = 16, 8
PARTS_Q = (0, 1, 2, 0, 1, 2, 0, 1)
PARTS_K = (0, 0, 0, 1, 1, 1, 2, 2)
NCOMB = len(PARTS_Q)
KROWS = NCOMB * HD
VW = HD + 1
RING0 = 3
WCOLS = GE * (SI + P)
NPROB = 8
LAG = 17

TAIL_AT = {"transposes": 22, "division": 22, "normed transposes": 24, "normed copy": 24,
           "output": 26, "residual": 26}
TAIL_STEP = 6
TAIL_LAST = {6: dict(zip(TAIL_AT, (65, 65, 66, 66, 67, 67))),
             7: dict(zip(TAIL_AT, (66, 66, 67, 67, 68, 68)))}
NORMED_BANK = [7] * 7 + [4]
STATISTICS, NORMALISE, NORM_T, NORMED, OPERANDS = (48, 68), (49, 70), (54, 70), (54, 70), (54, 71)
ROUTER_LOGITS, ROUTER_SUB, ROUTER_EXP, ROUTER_CHOICES = (56, 72), (56, 72), (57, 73), (58, 73)
ROUTER_RANKS, ROUTER_WEIGHTS, ROUTER_T, ROUTER_WT = (60, 74), (60, 75), (63, 76), (63, 76)
ROUTER_BANK, ROUTER_BANK_T, SUM_BANK = (1, 7), (0, 7), (7, 1, 2)
LAST_CHUNKS = ((0, 4), (4, 2), (6, 2))
TILE0 = NB * NH
QS = [(0, 0), (1, 0), (0, 1), (1, 1)] + [(e, h2) for e in range(2, 8) for h2 in range(2)]


def rows_at(q):
    return min(4 * q + 5, 62)


SCALE1 = 1.0 / float(HD) ** 0.5
SLOTS = LAG + 64 + 64 + 2

E1, F1 = 8, 512
RING1 = 3
CAP1 = int(T * 1.25 / E1)
NF = F1 // P

A_WQ0, A_WQ1, A_WO1, A_GATE, A_WS1, A_WS3, A_WR, A_END = 0, 128, 256, 384, 448, 624, 800, 808
B_BQ0, B_BQ1, B_B1, B_B2, B_END = 0, 1, 2, 34, 42


def view(ap, *dims):
    return bass.AP(ap.tensor, ap.offset, [list(ap.ap[0])] + [list(d) for d in dims])


def build(nc, x_in, ctx_in, packa_in, packc_in, bias_in, gateb_in, bo_in, ws2_in, w13_in, w2_in,
          ew1_in, ew2_in, out):
    with ExitStack() as ctx:
        def sb(name, shape, dt=F32):
            return ctx.enter_context(nc.sbuf_tensor(name, shape, dt))

        def sem(name):
            return ctx.enter_context(nc.semaphore(name))

        def sems(name, n):
            return [sem(f"{name}{i}") for i in range(n)]

        bank = [ctx.enter_context(nc.psum_tensor(f"bank{i}", [P, 512], F32)) for i in range(8)]

        ident = sb("ident", [P, P])
        identb = sb("identb", [P, P], BF16)
        tri = sb("tri", [P, P], BF16)
        ones = sb("ones", [P, P], BF16)
        iota_i = sb("iota_i", [P, E0], I32)
        iota_e = sb("iota_e", [P, E0])
        iota_s = sb("iota_s", [P, CAP0], BF16)
        mhalf = sb("mhalf", [P, 4])
        zero = sb("zero", [P, 1])
        selw = sb("selw", [3 * E1, E1, P], BF16)

        x = sb("x", [P, NC, P])
        ctxT = sb("ctxT", [P, T])
        packa = sb("packa", [P, A_END])
        packc = sb("packc", [CD + 1, 4, P])
        biases = sb("biases", [P, B_END])
        gateb = sb("gateb", [P, E0])
        bo = sb("bo", [P, P])
        ws2 = sb("ws2", [I0, 2, P])
        st = sb("st", [P, NC, 6])
        mv = sb("mv", [P, NC, 2])
        veps = sb("veps", [P, NC])
        rstd = sb("rstd", [P, NC])
        xn = sb("xn", [P, NC, P])
        xnT = sb("xnT", [P, T])

        big = sb("big", [P, NH * T // 2])
        pbuf = sb("pbuf", [P, 2, NC * GS], BF16)
        work = pbuf[:, :, :].rearrange("p a n -> p (a n)").bitcast(F32)
        qbuf, kbuf, vbuf = sb("qbuf", [P, T]), sb("kbuf", [P, T]), sb("vbuf", [P, NC, P])
        frbuf = sb("frbuf", [P, 5120], F32R)
        splits = sb("splits", [P, 4, T], F32R)

        ew = sb("ew", [P, RING1, 2, F1])
        onehots = [pbuf[:, 0, :], pbuf[:, 1, :],
                   ew[:, :, :, :].rearrange("p r i f -> p (r i f)")[:, 0:2048].bitcast(BF16)]

        q0T, k0T, v0 = qbuf, kbuf, vbuf
        prob0 = work[:, 0:NC * KV].rearrange("p (c k) -> p c k", c=NC)
        probT0 = work[:, NC * KV:2 * NC * KV].rearrange("p (c k) -> p c k", c=NC)
        nm0, sum0, rs0 = sb("nm0", [P, NC]), sb("sum0", [P, NC]), sb("rs0", [P, NC])

        score, biased = sb("score", [P, NC, E0]), sb("biased", [P, NC, E0])
        ra, rb = sb("ra", [P, 512]), sb("rb", [P, 512])
        nmg, sumg, rsg = sb("nmg", [P, NC]), sb("sumg", [P, NC]), sb("rsg", [P, NC])
        top8 = sb("top8", [P, NC, 8])
        idx8 = sb("idx8", [P, NC, 8], U32)
        selb = sb("selb", [P, NC, E0], BF16)
        equal, before = (ra[:, :].bitcast(BF16).rearrange("p (h a c e) -> p a h c e", h=2, a=2,
                                                          c=4)[:, i] for i in range(2))
        rk = sb("rk", [P, NG, NC, GE, 2], BF16)
        NW = 5
        sparts = sb("sparts", [P, NC, E0, NW], BF16)
        sres = sb("sres", [P, NC, E0])
        hs = [qbuf[0:I0, :], kbuf[0:I0, :]]
        SH_BANKS = [(6, 5), (0, 1), (6, 5), (0, 1)]
        GATE_BANK = [4, 7]
        def w13(e):
            at = (e // GE) % RING0 * WCOLS + (e % GE) * SI
            return big[:, at:at + SI]

        def w2(e):
            at = (e // GE) % RING0 * WCOLS + GE * SI + (e % GE) * P
            return big[0:I0, at:at + P]

        xb = ctxT[:, :].rearrange("p (a s) -> p a s", a=2)
        PTs = splits
        wslot = sb("wslot", [P, 3, NPAIR])
        slot_token = sb("slot_token", [P, 3, NPAIR], U32)
        token_f = sb("token_f", [P, NPAIR])
        token_i = sb("token_i", [P, NC, 2], I32)
        xg = sb("xg", [P, 2, NPAIR, P])
        sil, gv = sb("sil", [P, NPAIR, I0]), sb("gv", [P, NPAIR, I0])
        gT = sb("gT", [I0, NPAIR, P])
        yh = frbuf[:, 0:512].rearrange("p (j d) -> p j d", j=NPAIR)
        yl = frbuf[:, 512:1024].rearrange("p (j d) -> p j d", j=NPAIR)

        ks = sb("ks", [P, NH, T], BF16)
        qs = big[:, :].bitcast(BF16).rearrange("p (b h t) -> p b h t", b=NB, h=NH)
        parts = sb("parts", [P, 3, T], BF16)
        vaug = sb("vaug", [P, NC, NH, VW])
        nm1, nmr, rden = (score[:, :, :].rearrange("p c e -> p (c e)")[:, i * P:(i + 1) * P]
                          .rearrange("p (c h) -> p c h", c=NC) for i in range(3))
        nmp = sb("nmp", [P, NC, 2, 3, NH // 2], BF16)
        nmT = [xg[0:24, i, :, :].rearrange("p j d -> p (j d)").bitcast(BF16) for i in range(2)]
        prob1 = work.rearrange("p (r n) -> p r n", r=NPROB)
        qf, oun, onrm, onT = qbuf, qbuf, vbuf, kbuf

        xTh, xTl = frbuf[:, 0:T], frbuf[:, T:2 * T]
        w1h, w1l, w2h, w2l = (splits[:, i, :].rearrange("p (a f) -> p a f", a=2)
                              for i in range(4))
        act = work[:, 0:4 * 512].rearrange("p (r n) -> p r n", r=4)
        NA = 3
        acth = frbuf[:, 2 * T:2 * T + NA * 512].rearrange("p (r n) -> p r n", r=NA)
        actl = frbuf[:, 2 * T + NA * 512:2 * T + 2 * NA * 512].rearrange("p (r n) -> p r n", r=NA)
        accT = qbuf
        wbc = vbuf[:, :, :].rearrange("p c d -> p (c d)").rearrange("p (a t) -> p a t", a=2)
        ywt = kbuf[:, :].rearrange("p (a t) -> p a t", a=2)
        rp, rtop, ridxf, wtok, wres = (
            sres[:, :, :].rearrange("p c e -> p (c e)")[:, i * NC * E1:(i + 1) * NC * E1]
            .rearrange("p (c e) -> p c e", c=NC) for i in range(5))
        ridx = sb("ridx", [P, NC, 8], U32)
        roh = sb("roh", [P, NC, 2, E1], BF16)
        rkeep = sres[:, :, :].rearrange("p c e -> p (c e)")[:, 5 * NC * E1:7 * NC * E1].rearrange(
            "p (c k e) -> p c k e", c=NC, k=2)
        rtv, rsum = sb("rtv", [P, NC, 2]), sb("rsum", [P, NC])
        wparts = sb("wparts", [P, NC, 3, E1], BF16)
        wT = biased[0:3 * E1, :, :].rearrange("p c e -> p (c e)").bitcast(BF16)

        xn_dram = nc.dram_tensor("normalised", [T, P], F32, kind="Internal").ap()
        kscratch = nc.dram_tensor("k_parts", [3, P, T], BF16, kind="Internal").ap()
        qscratch = nc.dram_tensor("q_parts", [NB, 3, P, TB], BF16, kind="Internal").ap()

        ld_x, ld_ctx, ld_packa, ld_packc, ld_small = (
            sem("ld_x"), sem("ld_ctx"), sem("ld_packa"), sem("ld_packc"), sem("ld_small"))
        ld_w0, ld_w1 = sems("ld_w0_", NG), sems("ld_w1_", E1)
        c_row, c_all = sem("c_row"), sem("c_all")
        dve_step, pool_step = sem("dve_step"), sem("pool_step")
        ln_var, ln_rstd, ln_out, ln_tps, ln_tsb = (
            sem("ln_var"), sem("ln_rstd"), sem("ln_out"), sem("ln_tps"), sem("ln_tsb"))
        k0_ps, k0_sb, v0_ps, v0_sb = sem("k0_ps"), sem("k0_sb"), sem("v0_ps"), sem("v0_sb")
        k1_ps, k1_hi, k1_res, k1_mid, k1_lo = (
            sem("k1_ps"), sem("k1_hi"), sem("k1_res"), sem("k1_mid"), sem("k1_lo"))
        v1_ps, v1_sb, kd_out, ks_in = sem("v1_ps"), sem("v1_sb"), sem("kd_out"), sem("ks_in")
        q0_ps, q0_sb, s0_ps, m0_sb, p0_sb = (
            sem("q0_ps"), sem("q0_sb"), sem("s0_ps"), sem("m0_sb"), sem("p0_sb"))
        t0_ps, t0_sb, o0_ps, x1_sb = sem("t0_ps"), sem("t0_sb"), sem("o0_ps"), sem("x1_sb")
        g_ps, g_sub, g_exp, g_score, g_sel, g_rank, g_parts = (
            sem("g_ps"), sem("g_sub"), sem("g_exp"), sem("g_score"), sem("g_sel"), sem("g_rank"),
            sem("g_parts"))
        sh_ps, sh_sil, sh_sb = sem("sh_ps"), sem("sh_sil"), sem("sh_sb")
        e_P, e_W, e_id, e_xb, e_xgT, e_T, e_PTa, e_PTv = (
            sem("e_P"), sem("e_W"), sem("e_id"), sem("e_xb"), sem("e_xgT"), sem("e_T"),
            sem("e_PTa"), sem("e_PTv"))
        xn_out, e_xg = sem("xn_out"), sems("e_xg", NG)
        e_H, e_sil, e_gv, e_gTp, e_gT = (
            sem("e_H"), sem("e_sil"), sem("e_gv"), sem("e_gTp"), sem("e_gT"))
        e_Y, e_yh, e_yl, e_comb = sem("e_Y"), sem("e_yh"), sem("e_yl"), sem("e_comb")
        z_sb, z_T, x2_sb = sem("z_sb"), sem("z_T"), sem("x2_sb")
        q1_ps, q1_f, q1_hi, q1_res, q1_mid, q1_lo = (
            sem("q1_ps"), sem("q1_f"), sem("q1_hi"), sem("q1_res"), sem("q1_mid"), sem("q1_lo"))
        qd_out, qs_in, nm_in = sems("qd_out", NB), sems("qs_in", NB), sems("nm_in", 2 * NB)
        a_zeros, a_S, a_max, a_nmp, a_nmTp, a_nmT, a_ST, a_exp = (
            sem("a_zeros"), sem("a_S"), sem("a_max"), sem("a_nmp"), sem("a_nmTp"), sem("a_nmT"),
            sem("a_ST"), sem("a_exp"))
        a_O, a_oun, a_oT, a_on, a_onTp, a_onT, a_out, x3_sb = (
            sem("a_O"), sem("a_oun"), sem("a_oT"), sem("a_on"), sem("a_onTp"), sem("a_onT"),
            sem("a_out"), sem("x3_sb"))
        r_x, r_ps, r_sub, r_exp, r_oh, r_rank, r_wp, r_wTp, r_wT = (
            sem("r_x"), sem("r_ps"), sem("r_sub"), sem("r_exp"), sem("r_oh"), sem("r_rank"),
            sem("r_wp"), sem("r_wTp"), sem("r_wT"))
        f_w1, f_w2, f_H, f_act, f_hi, f_lo, f_Y, f_bc, f_wbc, f_yw, f_acc = (
            sem("f_w1"), sem("f_w2"), sem("f_H"), sem("f_act"), sem("f_hi"), sem("f_lo"),
            sem("f_Y"),
            sem("f_bc"), sem("f_wbc"), sem("f_yw"), sem("f_acc"))
        f_oT, x4_sb, st_out = sem("f_oT"), sem("x4_sb"), sem("st_out")

        def half(h2):
            return slice(h2 * 512, h2 * 512 + 512)

        def chunk(c):
            return slice(c * P, (c + 1) * P)

        def batch(b):
            return slice(b * TB, (b + 1) * TB)

        LN_CHUNKS = ([range(0, 4), range(4, 8)] * 2 + [range(2 * b, 2 * b + 2) for b in range(NB)]
                     + [range(0, 4), range(4, 8)])
        LN_BANK = [0, 1, 2, 3, 4, 5, 4, 5, 0, 7]
        Z_BANK = [2, 3, 0, 1]

        def ln_before(step):
            return max([s + 1 for s in range(step) if set(LN_CHUNKS[s]) & set(LN_CHUNKS[step])],
                       default=0)

        NT = 2 * E1 * NF

        def query_rest(b):
            return (ra, rb)[b // 2][:, b % 2 * TB:(b % 2 + 1) * TB]

        def shared_silu(i):
            return xb[0:I0, i % 2, :]

        def tail_chunk(step, e):
            for c in range(NC):
                if TAIL_LAST[c][step] == e if c in TAIL_LAST else (
                        NH * (c // 2) + TAIL_AT[step] + TAIL_STEP * (c % 2) == e):
                    return c
            return None

        VALUES1_AT = (3, 5)
        block = ctx.enter_context(nc.Block())

        @block.sync
        def _(sp):

            def group_weights(g):
                at = g % RING0 * WCOLS
                es = slice(g * GE, (g + 1) * GE)
                sp.dma_start(big[:, at:at + GE * SI].rearrange("p (e i) -> p e i", e=GE),
                             w13_in[:, es, :]).then_inc(ld_w0[g], 16)
                sp.dma_start(big[0:I0, at + GE * SI:at + WCOLS].rearrange("p (e d) -> p e d", e=GE),
                             w2_in[:, es, :]).then_inc(ld_w0[g], 16)

            def expert_weights(e):
                sp.dma_start(ew[:, e % RING1, 0, :], ew1_in[:, e, :]).then_inc(ld_w1[e], 16)
                sp.dma_start(ew[:, e % RING1, 1, :].rearrange("p (f d) -> p f d", f=NF),
                             ew2_in[:, e, :, :]).then_inc(ld_w1[e], 16)

            sp.dma_start(ctxT[0:CD, :], ctx_in).then_inc(ld_ctx, 16)
            sp.dma_start(packc[:, :, :], packc_in).then_inc(ld_packc, 16)
            sp.dma_start(x[:, :, :], x_in.rearrange("(c p) d -> p c d", p=P)).then_inc(ld_x, 16)
            sp.dma_start(packa[:, :], packa_in).then_inc(ld_packa, 16)
            sp.dma_start(biases[:, :], bias_in).then_inc(ld_small, 16)
            sp.dma_start(gateb[:, :], gateb_in.to_broadcast([P, E0])).then_inc(ld_small, 16)
            sp.dma_start(bo[:, :], bo_in.to_broadcast([P, P])).then_inc(ld_small, 16)
            sp.dma_start(ws2[:, :, :], ws2_in).then_inc(ld_small, 16)
            for g in range(RING0):
                group_weights(g)
            sp.wait_ge(k1_hi, 2)
            sp.wait_ge(k1_mid, 2)
            sp.wait_ge(k1_lo, 2)
            sp.dma_start(kscratch.rearrange("j p t -> p j t"), parts[:, :, :]).then_inc(kd_out, 16)
            sp.wait_ge(kd_out, 16)
            for i, part in enumerate(PARTS_K):
                sp.dma_start(ks[i * HD:(i + 1) * HD, :, :],
                             kscratch[part].rearrange("(d h) t -> d h t", d=HD)).then_inc(ks_in, 16)
            for h2 in range(2):
                sp.wait_ge(ln_out, 3 + h2)
                sp.dma_start(xn_dram.rearrange("(c p) d -> p c d", p=P)[:, 4 * h2:4 * h2 + 4, :],
                             xn[:, 4 * h2:4 * h2 + 4, :]).then_inc(xn_out, 16)
            for g in range(RING0, NG):
                sp.wait_ge(e_Y, g - RING0 + 1)
                group_weights(g)
            sp.wait_ge(e_T, NPAIR * (NG - NG % 3))
            for e in range(RING1):
                expert_weights(e)

            def queries_stacked(b):
                sp.wait_ge(q1_hi, b + 1)
                sp.wait_ge(q1_mid, b + 1)
                sp.dma_start(qscratch[b, 0:2].rearrange("j p t -> p j t"),
                             parts[:, 0:2, batch(b)]).then_inc(qd_out[b], 16)
                sp.wait_ge(q1_lo, b + 1)
                sp.dma_start(qscratch[b, 2], parts[:, 2, batch(b)]).then_inc(qd_out[b], 16)
                sp.wait_ge(qd_out[b], 32)
                rows = qscratch[b].rearrange("j (d h) t -> (j d) h t", d=HD)
                for i in range(0, NCOMB, 3):
                    n = min(3, NCOMB - i)
                    sp.dma_start(qs[i * HD:(i + n) * HD, b, :, :], rows[0:n * HD]
                                 ).then_inc(qs_in[b], 16)

            def maxima_stacked(k):
                b, hs8 = k // 2, slice(k % 2 * 8, k % 2 * 8 + 8)
                sp.wait_ge(a_nmT, k + 1)
                for part in range(3):
                    sp.dma_start(qs[KROWS + part:KROWS + part + 1, b, hs8, :],
                                 nmT[k % 2][part * 8:(part + 1) * 8, batch(b)]
                                 ).then_inc(nm_in[k], 16)

            queries_stacked(0)
            queries_stacked(1)
            sp.wait_ge(c_all, 1 + NB)
            for k in range(2 * NB):
                maxima_stacked(k)
                if k < 2:
                    queries_stacked(2 + k)
            for e in range(RING1, E1):
                sp.wait_ge(f_w2, e - RING1 + 1)
                expert_weights(e)
            for i, (c, n) in enumerate(LAST_CHUNKS):
                sp.wait_ge(x4_sb, i + 1)
                sp.dma_start(out.rearrange("(c p) d -> p c d", p=P)[:, c:c + n, :],
                             x[:, c:c + n, :]).then_inc(st_out, 16)
            sp.wait_ge(st_out, 16 * len(LAST_CHUNKS))

        @block.gpsimd
        def _(pool):
            steps = [0]

            def chained(ins):
                steps[0] += 1
                ins.then_inc(pool_step, 1)
                pool.wait_ge(pool_step, steps[0])

            pool.memset(ctxT[CD:CD + 1, :], 1.0).then_inc(c_row, 1)
            pool.wait_ge(c_row, 1)
            pool.memset(mhalf[:, :], -0.5)
            pool.memset(zero[:, :], 0.0)
            pool.memset(ident[:, :], 0.0)
            pool.memset(identb[:, :], 0.0)
            chained(pool.memset(ones[:, :], 1.0))
            chained(pool.memset(selw[:, :, :], 0.0))
            pool.affine_select(out=ident[:, :], in_=ident[:, :], compare_op=ALU.not_equal, fill=1.0,
                               base=0, pattern=[[-1, P]], channel_multiplier=1)
            pool.affine_select(out=identb[:, :], in_=identb[:, :], compare_op=ALU.not_equal,
                               fill=1.0, base=0, pattern=[[-1, P]], channel_multiplier=1)
            pool.affine_select(out=tri[:, :], in_=ones[:, :], compare_op=ALU.is_ge, fill=0.0,
                               base=0, pattern=[[1, P]], channel_multiplier=-1)
            chained(pool.iota(iota_i[:, :], pattern=[[1, E0]], base=0, channel_multiplier=0))
            chained(pool.tensor_copy(iota_e[:, :], iota_i[:, :]))
            pool.tensor_scalar(iota_s[:, :], iota_e[:, :], 1.0, None, ALU.add).then_inc(c_all, 1)

            def power(step):
                n = len(LN_CHUNKS[step])
                cs = slice(LN_CHUNKS[step][0], LN_CHUNKS[step][0] + n)
                pool.wait_ge(ln_var, step + 1)
                if ln_before(step):
                    pool.wait_ge(ln_out, ln_before(step))
                pool.tensor_tensor(out=rstd[:, cs], in0=veps[:, cs], in1=mhalf[:, 0:n],
                                   op=ALU.pow).then_inc(ln_rstd, 1)

            power(0)
            power(1)
            pool.wait_ge(ln_rstd, 2)
            pool.iota(token_i[:, :, 0], pattern=[[P, NC]], base=0, channel_multiplier=0)
            chained(pool.iota(token_i[:, :, 1], pattern=[[0, NC]], base=0, channel_multiplier=1))
            chained(pool.tensor_copy(sparts[:, :, :, 3:5],
                                     view(token_i[:, 0, 0:1], (2, NC), (0, E0), (1, 2))))
            for part in range(3):
                chained(pool.affine_select(
                    out=selw[:, :, :], in_=selw[:, :, :], compare_op=ALU.not_equal, fill=1.0,
                    base=-E1 * part, pattern=[[-1, E1], [0, P]], channel_multiplier=1))

            for h2 in range(2):
                pool.wait_ge(k1_res, h2 + 1)
                pool.tensor_copy(parts[:, 1, half(h2)], (ra, rb)[h2][:, :]).then_inc(k1_mid, 1)
            pool.wait_ge(k1_mid, 2)
            chained(pool.memset(ks[KROWS:P, :, :].bitcast(F32), 0.0))
            power(2)
            power(3)
            pool.wait_ge(ln_rstd, 4)
            for h2 in range(2):
                cs = slice(4 * h2, 4 * h2 + 4)
                pool.wait_ge(g_score, h2 + 1)
                chained(pool.tensor_copy(sparts[:, cs, :, 0], score[:, cs, :]))
                chained(pool.tensor_tensor(out=sres[:, cs, :], in0=score[:, cs, :],
                                           in1=sparts[:, cs, :, 0], op=ALU.subtract))
                chained(pool.tensor_copy(sparts[:, cs, :, 1], sres[:, cs, :]))
                pool.tensor_tensor(out=sparts[:, cs, :, 2], in0=sres[:, cs, :],
                                   in1=sparts[:, cs, :, 1], op=ALU.subtract).then_inc(g_parts, 1)
            pool.wait_ge(g_parts, 2)
            for i in range(4):
                part = hs[i // 2][:, half(i % 2)]
                pool.wait_ge(sh_sil, i + 1)
                pool.tensor_tensor(out=part, in0=part, in1=shared_silu(i),
                                   op=ALU.mult).then_inc(sh_sb, 1)
            pool.wait_ge(sh_sb, 4)
            pool.wait_ge(xn_out, 32)
            for g in range(NG):
                pool.wait_ge(e_id, g + 1)
                if g >= 2:
                    pool.wait_ge(e_xgT, g - 1)
                for j in range(NPAIR):
                    pool.indirect_dma_start(
                        out=xg[:, g % 2, j, :], out_offset=None, in_=xn_dram,
                        in_offset=bass.IndirectOffsetOnAxis(
                            ap=slot_token[:, g % 3, j:j + 1], axis=0)).then_inc(e_xg[g], 16)
            ones_pair = 0x3F803F80
            chained(pool.memset(ks[KROWS:KROWS + 3, :, :].bitcast(I32), ones_pair))

            def query_zeros(b):
                n = NH * TB // 2
                pool.memset(big[KROWS:P, b * n:(b + 1) * n], 0.0).then_inc(c_all, 1)

            pool.wait_ge(e_Y, NG - 2)
            query_zeros(3)
            pool.wait_ge(e_Y, NG)
            for b in range(3):
                query_zeros(b)
            pool.wait_ge(c_all, 1 + NB)
            for step in range(4, 8):
                power(step)
            pool.wait_ge(ln_out, 8)
            pool.wait_ge(ld_small, 64)
            pool.tensor_tensor(out=x[:, :, :], in0=x[:, :, :], in1=view(bo[:, :], (0, NC), (1, P)),
                               op=ALU.add).then_inc(x2_sb, 1)

            def maxima_parts(k):
                cs, h8 = slice(2 * (k // 2), 2 * (k // 2) + 2), slice(k % 2 * 8, k % 2 * 8 + 8)
                pool.wait_ge(a_max, 8 * (k + 1))
                chained(pool.tensor_copy(nmp[:, cs, k % 2, 0, :], nm1[:, cs, h8]))
                chained(pool.tensor_tensor(out=nmr[:, cs, h8], in0=nm1[:, cs, h8],
                                           in1=nmp[:, cs, k % 2, 0, :], op=ALU.subtract))
                chained(pool.tensor_copy(nmp[:, cs, k % 2, 1, :], nmr[:, cs, h8]))
                pool.tensor_tensor(out=nmp[:, cs, k % 2, 2, :], in0=nmr[:, cs, h8],
                                   in1=nmp[:, cs, k % 2, 1, :],
                                   op=ALU.subtract).then_inc(a_nmp, 1)

            def split_weights(e, i):
                high, low, done, split = ((w1h, w1l, f_H, f_w1), (w2h, w2l, f_Y, f_w2))[i]
                pool.wait_ge(ld_w1[e], 32)
                if e >= 2:
                    pool.wait_ge(done, NF * (1 + max(QS.index((e - 2, h2)) for h2 in range(2))))
                chained(pool.tensor_copy(high[:, e % 2, :], ew[:, e % RING1, i, :]))
                pool.tensor_tensor(out=low[:, e % 2, :], in0=ew[:, e % RING1, i, :],
                                   in1=high[:, e % 2, :].bitcast(F32),
                                   op=ALU.subtract).then_inc(split, 1)

            pool.wait_ge(e_comb, NG - 1 + NB)
            for k in range(2 * NB):
                maxima_parts(k)
                if k < 4:
                    split_weights(k // 2, k % 2)
            power(8)
            power(9)
            for e in range(2, E1):
                for i in range(2):
                    split_weights(e, i)

        @block.scalar
        def _(a):
            for h2 in range(2):
                a.wait_ge(k0_ps, h2 + 1)
                a.copy(k0T[:, half(h2)], bank[h2][:, :]).then_inc(k0_sb, 1)
            for h2 in range(2):
                a.wait_ge(v0_ps, h2 + 1)
                a.copy(v0[:, 4 * h2:4 * h2 + 4, :],
                       bank[2 + h2][:, :].rearrange("p (c d) -> p c d", c=4)).then_inc(v0_sb, 1)

            def first_keys1(h2):
                a.wait_ge(k1_ps, h2 + 1)
                a.copy(parts[:, 0, half(h2)], bank[h2][:, :]).then_inc(k1_hi, 1)

            def values1(h2):
                a.wait_ge(v1_ps, h2 + 1)
                for c in range(4):
                    ins = a.copy(vaug[:, 4 * h2 + c, :, 0:HD],
                                 bank[2 + h2][:, chunk(c)].rearrange("p (h d) -> p h d", h=NH))
                ins.then_inc(v1_sb, 1)

            def norm_transposed(step):
                a.wait_ge(ln_tps, step + 1)
                at, n = LN_CHUNKS[step][0] * P, len(LN_CHUNKS[step]) * P
                a.copy(xnT[:, at:at + n], bank[LN_BANK[step]][:, 0:n]).then_inc(ln_tsb, 1)

            norm_transposed(0)
            norm_transposed(1)

            def exp0(c):
                a.wait_ge(m0_sb, c + 1)
                a.activation(prob0[:, c, :], bank[4 + c % 2][:, 0:KV], ACT.Exp,
                             bias=nm0[:, c:c + 1], accum_out=sum0[:, c:c + 1]).then_inc(p0_sb, 1)

            exp0(0)
            first_keys1(0)
            first_keys1(1)
            for c in range(NC):
                if c + 1 < NC:
                    exp0(c + 1)
                if c - 1 in VALUES1_AT:
                    values1(VALUES1_AT.index(c - 1))
                a.wait_ge(t0_ps, c + 1)
                a.copy(probT0[:, c, :], bank[6 + c % 2][:, 0:KV]).then_inc(t0_sb, 1)
                if c == NC - 1:
                    norm_transposed(2)

            def shared_activation(i):
                a.wait_ge(sh_ps, i + 1)
                if i >= 2:
                    a.wait_ge(sh_sb, i - 1)
                a.activation(shared_silu(i), bank[SH_BANKS[i][0]][0:I0, :], ACT.Silu)
                a.copy(hs[i // 2][:, half(i % 2)], bank[SH_BANKS[i][1]][0:I0, :]
                       ).then_inc(sh_sil, 1)

            a.wait_ge(c_all, 1)
            a.copy(vaug[:, :, :, HD:HD + 1],
                   ones[:, :].rearrange("p (c h o) -> p c h o", c=NC, h=NH)).then_inc(v1_sb, 1)
            for h2 in range(2):
                if h2 == 1:
                    norm_transposed(3)
                a.wait_ge(g_sub, h2 + 1)
                a.activation(score[:, 4 * h2:4 * h2 + 4, :],
                             ra[:, h2 * 256:(h2 + 1) * 256].rearrange("p (c e) -> p c e", c=4),
                             ACT.Exp).then_inc(g_exp, 1)
            for i in range(4):
                shared_activation(i)

            def gathered(g):
                a.wait_ge(e_xgT, g + 1)
                if g >= 2:
                    a.wait_ge(e_H, 2 * (g - 1))
                a.copy(xb[:, g % 2, :], bank[7][:, :]).then_inc(e_xb, 1)

            def dispatch_odd(g, j):
                a.wait_ge(e_T, NPAIR * g + j + 1)
                if g >= 1:
                    a.wait_ge(e_comb, g)
                a.copy(PTs[:, j, :], bank[4][:, :].bitcast(BF16)).then_inc(e_PTa, 1)

            dispatch_odd(0, 1)
            gathered(0)
            for g in range(NG):
                for p2 in range(2):
                    a.wait_ge(e_H, 2 * g + p2 + 1)
                    if g >= 1:
                        a.wait_ge(e_gv, g)
                    a.activation(sil[:, 2 * p2:2 * p2 + 2, :],
                                 bank[5 + p2][:, 0:2 * SI].rearrange(
                                     "p (j i) -> p j i", j=2)[:, :, 0:I0],
                                 ACT.Silu).then_inc(e_sil, 1)
                if g + 1 < NG:
                    gathered(g + 1)
                if g >= 1:
                    dispatch_odd(g, 1)
                a.wait_ge(e_gTp, g + 1)
                a.copy(gT[:, :, :], bank[7][0:I0, :].rearrange(
                    "p (j s) -> p j s", j=NPAIR)).then_inc(e_gT, 1)
                dispatch_odd(g, 3)
                a.wait_ge(e_Y, g + 1)
                a.copy(yh, bank[7][:, :].rearrange("p (j d) -> p j d", j=NPAIR)).then_inc(e_yh, 1)
            for b in range(NB):
                a.wait_ge(e_comb, NG + b)
                a.copy(xnT[:, batch(b)], bank[b % 2][:, b // 2 * TB:(b // 2 + 1) * TB]
                       ).then_inc(z_sb, 1)

            def query_parts(b):
                a.wait_ge(q1_f, b + 1)
                a.copy(parts[:, 0, batch(b)], qf[:, batch(b)]).then_inc(q1_hi, 1)
                a.wait_ge(q1_res, b + 1)
                a.copy(parts[:, 1, batch(b)], query_rest(b)).then_inc(q1_mid, 1)

            a.wait_ge(kd_out, 16)
            a.wait_ge(z_T, 1)
            norm_transposed(4)
            a.wait_ge(z_T, 2)
            norm_transposed(5)
            query_parts(0)
            a.wait_ge(z_T, 3)
            norm_transposed(6)
            query_parts(1)
            a.wait_ge(z_T, 4)
            norm_transposed(7)
            query_parts(2)
            query_parts(3)
            a.wait_ge(ln_tsb, 8)
            a.wait_ge(q1_f, NB)
            for i in (5, 6):
                a.copy(bank[i][:, :], view(zero[:, :], (0, 512))).then_inc(a_zeros, 1)

            for s in range(SLOTS):
                m, e = s, s - LAG
                if m % 8 == 3 and 1 <= m // 8 <= 2 * NB:
                    k = m // 8 - 1
                    a.wait_ge(a_nmTp, k + 1)
                    a.copy(nmT[k % 2][:, batch(k // 2)], bank[4][0:24, :].bitcast(BF16)[:, 0:TB]
                           ).then_inc(a_nmT, 1)
                for h2 in range(2):
                    if e == NORMED[h2]:
                        norm_transposed(8 + h2)
                    if e == ROUTER_EXP[h2]:
                        a.wait_ge(r_sub, h2 + 1)
                        a.activation(rp[:, 4 * h2:4 * h2 + 4, :], rp[:, 4 * h2:4 * h2 + 4, :],
                                     ACT.Exp).then_inc(r_exp, 1)
                    if e == ROUTER_WT[h2]:
                        a.wait_ge(r_wTp, h2 + 1)
                        a.copy(wT[:, half(h2)], bank[ROUTER_BANK_T[h2]][0:3 * E1, :].bitcast(
                            BF16)[:, half(h2)]).then_inc(r_wT, 1)
                if 0 <= e < NB * NH:
                    a.wait_ge(a_ST, e + 1)
                    if e >= NPROB:
                        a.wait_ge(a_O, (e - NPROB) // 4 + 1)
                    a.activation(prob1[:, e % NPROB, :], bank[2 + e % 2][:, :],
                                 ACT.Exp).then_inc(a_exp, 1)
                for o in range(2 * NB):
                    if e == min(8 * o + 12, NB * NH):
                        a.wait_ge(a_O, 2 * o + 2)
                        if o >= 2:
                            a.wait_ge(a_oT, 2 * (o // 2))
                        a.copy(oun[:, half(o % 2)], bank[5 + o % 2][:, :]).then_inc(a_oun, 1)
                c = tail_chunk("normed copy", e)
                if c is not None:
                    a.wait_ge(a_onTp, c + 1)
                    a.copy(onT[:, chunk(c)], bank[NORMED_BANK[c]][:, 0:P]).then_inc(a_onT, 1)
                n = e - TILE0
                if not 0 <= n < NT:
                    continue
                q, f = n // NF, n % NF
                expert = QS[q][0]
                a.wait_ge(f_H, n + 1)
                if n == 0:
                    a.wait_ge(a_O, 4 * NB - 1)
                bias = biases[:, B_B1 + expert * NF + f:B_B1 + expert * NF + f + 1]
                if n >= NA:
                    a.wait_ge(f_Y, n - NA + 1)
                a.activation(acth[:, n % NA, :], bank[n % 3][:, :], ACT.Gelu,
                             bias=bias).then_inc(f_hi, 1)
                if n >= 4:
                    a.wait_ge(f_lo, n - 3)
                a.activation(act[:, n % 4, :], bank[n % 3][:, :], ACT.Gelu,
                             bias=bias).then_inc(f_act, 1)
        @block.tensor
        def _(pe):

            def mm(out_, lhsT, rhs, start=True, stop=True):
                return pe.matmul(out_, lhsT, rhs, start=start, stop=stop, skip_group_check=True)

            pe.wait_ge(ld_ctx, 16)
            pe.wait_ge(ld_packc, 16)
            pe.wait_ge(c_row, 1)
            ctxr = ctxT[0:CD + 1, :]

            def context_keys(first, w, done):
                for h2 in range(2):
                    mm(bank[first + h2][:, :], packc[:, w, :], ctxr[:, half(h2)]).then_inc(done, 1)

            def context_values(first, w, done, chunks=range(NC)):
                for c in chunks:
                    ins = mm(bank[first + c // 4][:, chunk(c % 4)], ctxr[:, chunk(c)],
                             packc[:, w, :])
                    if c % 4 == 3:
                        ins.then_inc(done, 1)

            context_keys(0, 0, k0_ps)
            context_values(2, 1, v0_ps)

            def norm_transposes(step):
                pe.wait_ge(ln_out, step + 1)
                if step in (2, 3):
                    pe.wait_ge(v1_sb, step - 1)
                if step == 8:
                    pe.wait_ge(a_max, NB * NH)
                for i, c in enumerate(LN_CHUNKS[step]):
                    ins = pe.transpose(bank[LN_BANK[step]][:, chunk(i)], xn[:, c, :], ident[:, :])
                ins.then_inc(ln_tps, 1)

            pe.wait_ge(c_all, 1)
            pe.wait_ge(k0_sb, 2)
            norm_transposes(0)
            norm_transposes(1)
            pe.wait_ge(ld_packa, 16)
            pe.wait_ge(v0_sb, 2)
            for h2 in range(2):
                pe.wait_ge(ln_tsb, h2 + 1)
                mm(bank[2 + h2][:, :], packa[:, A_WQ0:A_WQ0 + P], xnT[:, half(h2)]
                   ).then_inc(q0_ps, 1)

            def scores0(c):
                if c % 4 == 0:
                    pe.wait_ge(q0_sb, c // 4 + 1)
                if c >= 2:
                    pe.wait_ge(p0_sb, c - 1)
                mm(bank[4 + c % 2][:, 0:KV], q0T[:, chunk(c)], k0T[:, batch(c // 2)]
                   ).then_inc(s0_ps, 1)

            def values0(c):
                pe.wait_ge(t0_sb, c + 1)
                if c >= 2:
                    pe.wait_ge(x1_sb, c - 1)
                else:
                    pe.wait_ge(k1_res, c + 1)
                b = c // 2
                mm(bank[c % 2][:, 0:P], probT0[:, c, 0:P], v0[:, 2 * b, :], stop=False)
                mm(bank[c % 2][:, 0:P], probT0[:, c, P:KV], v0[:, 2 * b + 1, :],
                   start=False).then_inc(o0_ps, 1)

            scores0(0)
            context_keys(0, 2, k1_ps)
            for c in range(NC):
                if c + 1 < NC:
                    scores0(c + 1)
                if c in VALUES1_AT:
                    pe.wait_ge(q0_sb, 2)
                    h2 = VALUES1_AT.index(c)
                    context_values(2, 3, v1_ps, range(4 * h2, 4 * h2 + 4))
                pe.wait_ge(p0_sb, c + 1)
                if c >= 2:
                    pe.wait_ge(t0_sb, c - 1)
                pe.transpose(bank[6 + c % 2][:, 0:P], prob0[:, c, 0:P], ident[:, :])
                pe.transpose(bank[6 + c % 2][:, P:KV], prob0[:, c, P:KV], ident[:, :]
                             ).then_inc(t0_ps, 1)
                if c >= 1:
                    values0(c - 1)
            values0(NC - 1)
            norm_transposes(2)

            def gate_logits(h2):
                pe.wait_ge(ln_tsb, 2 + h2 + 1)
                for c in range(4 * h2, 4 * h2 + 4):
                    ins = mm(bank[GATE_BANK[h2]][:, c * E0:(c + 1) * E0], xnT[:, chunk(c)],
                             packa[:, A_GATE:A_GATE + E0])
                ins.then_inc(g_ps, 1)

            def gate_ranks(h2):
                pe.wait_ge(g_sel, h2 + 1)
                for c in range(4 * h2, 4 * h2 + 4):
                    o = bank[GATE_BANK[h2]][:, c * E0:(c + 1) * E0]
                    for cc in range(c):
                        mm(o, ones[:, :], selb[:, cc, :], start=(cc == 0), stop=False)
                    ins = mm(o, tri[:, :], selb[:, c, :], start=(c == 0))
                ins.then_inc(g_rank, 1)

            def shared_hidden(i):
                ih, h2 = i // 2, i % 2
                b1, b3 = SH_BANKS[i]
                if i == 0:
                    pe.wait_ge(p0_sb, NC)
                    pe.wait_ge(t0_sb, NC)
                mm(bank[b1][0:I0, :], packa[:, A_WS1 + ih * I0:A_WS1 + (ih + 1) * I0],
                   xnT[:, half(h2)])
                mm(bank[b3][0:I0, :], packa[:, A_WS3 + ih * I0:A_WS3 + (ih + 1) * I0],
                   xnT[:, half(h2)]).then_inc(sh_ps, 1)

            def two_batches(tokens, i):
                return view(tokens[:, batch(i)], (2 * TB, 2), (1, TB))

            def shared_outputs(i):
                for ih in range(2):
                    mm(bank[i][:, :], ws2[:, ih, :], two_batches(hs[ih], i),
                       start=(ih == 0), stop=False)

            gate_logits(0)
            shared_hidden(0)
            norm_transposes(3)
            gate_logits(1)
            gate_ranks(0)
            pe.wait_ge(x1_sb, NC)
            shared_hidden(1)
            pe.wait_ge(sh_sil, 1)
            shared_hidden(2)
            gate_ranks(1)
            pe.wait_ge(sh_sil, 2)
            shared_hidden(3)

            def onehot(g, c, j):
                return onehots[g % 3][:, c * GS + j * P:c * GS + (j + 1) * P]

            def gathered_transposes(g):
                pe.wait_ge(e_xg[g], 16 * NPAIR)
                if g >= 2:
                    pe.wait_ge(e_yl, g - 1)
                for j in range(NPAIR):
                    ins = pe.transpose(bank[7][:, chunk(j)], xg[:, g % 2, j, :], ident[:, :])
                ins.then_inc(e_xgT, 1)

            def combine(g, b=None):
                pe.wait_ge(e_PTa, 2 * (g + 1))
                pe.wait_ge(e_PTv, 2 * (g + 1))
                for i in range(2) if b is None else [b % 2]:
                    for y, ready in ((yh, e_yh), (yl, e_yl)):
                        pe.wait_ge(ready, g + 1)
                        for j in range(NPAIR):
                            if b is None:
                                out_, slots = bank[i][:, :], two_batches(PTs[:, j, :], i)
                            else:
                                out_ = bank[i][:, b // 2 * TB:(b // 2 + 1) * TB]
                                slots = PTs[:, j, batch(b)]
                            ins = mm(out_, y[:, j, :], slots, start=False,
                                     stop=(g == NG - 1 and j == NPAIR - 1 and y is yl))
                ins.then_inc(e_comb, 1)

            def slot_numbers(g):
                pe.wait_ge(e_P, NC * (g + 1))
                if g >= 1:
                    pe.wait_ge(e_id, g)
                for j in range(NPAIR):
                    for c in range(NC):
                        ins = mm(bank[2][:, 2 * NW * j:2 * NW * (j + 1)], onehot(g, c, j),
                                 sparts[:, c, g * GE + 2 * j:g * GE + 2 * j + 2, :].rearrange(
                                     "p e k -> p (e k)"), start=(c == 0), stop=(c == NC - 1))
                ins.then_inc(e_W, 1)

            def hidden(g):
                pe.wait_ge(e_xb, g + 1)
                pe.wait_ge(ld_w0[g], 32)
                if g >= 1:
                    pe.wait_ge(e_gv, g)
                for j in range(NPAIR):
                    for s in range(2):
                        ins = mm(bank[5 + j // 2][64 * s:64 * s + 64,
                                                  (j % 2) * SI:(j % 2 + 1) * SI],
                                 xb[:, g % 2, j * P + 64 * s:j * P + 64 * s + 64],
                                 w13(g * GE + 2 * j + s))
                    if j % 2:
                        ins.then_inc(e_H, 1)

            def dispatch_transposes(g, j):
                if 2 * g + j // 2:
                    pe.wait_ge((e_PTv, e_PTa)[j % 2], 2 * g + j // 2)
                for c in range(NC):
                    ins = pe.transpose(bank[3 + j % 2][:, :].bitcast(BF16)[:, chunk(c)],
                                       onehot(g, c, j), identb[:, :])
                ins.then_inc(e_T, 1)

            def hidden_transposes(g):
                pe.wait_ge(e_gv, g + 1)
                if g + 1 < NG:
                    pe.wait_ge(e_xb, g + 2)
                else:
                    pe.wait_ge(e_yl, g)
                for j in range(NPAIR):
                    ins = pe.transpose(bank[7][0:I0, chunk(j)], gv[:, j, :], ident[:, :])
                ins.then_inc(e_gTp, 1)

            def outputs(g):
                pe.wait_ge(e_gT, g + 1)
                for j in range(NPAIR):
                    for s in range(2):
                        ins = mm(bank[7][64 * s:64 * s + 64, chunk(j)],
                                 gT[:, j, 64 * s:64 * s + 64], w2(g * GE + 2 * j + s))
                ins.then_inc(e_Y, 1)

            pe.wait_ge(g_parts, 2)
            slot_numbers(0)
            dispatch_transposes(0, 0)
            dispatch_transposes(0, 1)
            pe.wait_ge(ld_small, 64)
            pe.wait_ge(sh_sb, 4)
            shared_outputs(0)
            slot_numbers(1)
            shared_outputs(1)
            gathered_transposes(0)
            for g in range(NG):
                hidden(g)
                if g >= 1:
                    dispatch_transposes(g, 0)
                    combine(g - 1)
                if g + 1 < NG:
                    gathered_transposes(g + 1)
                if g >= 1:
                    dispatch_transposes(g, 1)
                if g + 2 < NG:
                    slot_numbers(g + 2)
                hidden_transposes(g)
                dispatch_transposes(g, 2)
                dispatch_transposes(g, 3)
                outputs(g)

            def sum_transposes0(b):
                pe.wait_ge(z_sb, b + 1)
                for i in range(2):
                    ins = pe.transpose(bank[Z_BANK[b]][:, chunk(i)], xnT[:, chunk(2 * b + i)],
                                       ident[:, :])
                ins.then_inc(z_T, 1)

            for b in range(NB):
                if b >= 2:
                    pe.wait_ge(z_sb, b - 1)
                combine(NG - 1, b)
                if b >= 1:
                    sum_transposes0(b - 1)
            sum_transposes0(NB - 1)

            def queries1(b):
                pe.wait_ge(ln_tsb, 4 + b + 1)
                if b >= 2:
                    pe.wait_ge(q1_f, b - 1)
                mm(bank[6 + b % 2][:, 0:TB], packa[:, A_WQ1:A_WQ1 + P], xnT[:, batch(b)]
                   ).then_inc(q1_ps, 1)

            norm_transposes(4)
            norm_transposes(5)
            queries1(0)
            queries1(1)
            for b in (2, 3):
                norm_transposes(4 + b)
                queries1(b)

            transposed = {"maxima": 0, "outputs": 0}

            def max_scores(m):
                b, hp, i = m // NH, m % NH // 2, m % 2
                if m >= 2:
                    pe.wait_ge(a_max, m - 1)
                if m % NH == 0:
                    pe.wait_ge(qs_in[b], 48)
                for j in range(2):
                    h = 2 * hp + j
                    ins = mm(bank[m % 2][:, j * KV:(j + 1) * KV], qs[:, b, h, chunk(i)],
                             ks[:, h, batch(b)])
                ins.then_inc(a_S, 1)

            def maxima_transposes(k):
                pe.wait_ge(a_nmp, k + 1)
                if transposed["outputs"]:
                    pe.wait_ge(a_on, transposed["outputs"])
                transposed["maxima"] += 1
                for i in range(2):
                    ins = pe.transpose(bank[4][0:24, :].bitcast(BF16)[:, chunk(i)],
                                       nmp[:, 2 * (k // 2) + i, k % 2, :, :].rearrange(
                                           "p j h -> p (j h)"),
                                       identb[:, :])
                ins.then_inc(a_nmTp, 1)

            def exp_scores(e):
                b, h = e // NH, e % NH
                if h % 8 == 0:
                    pe.wait_ge(nm_in[e // 8], 48)
                if e >= 2:
                    pe.wait_ge(a_exp, e - 1)
                for kc in range(2):
                    ins = mm(bank[2 + e % 2][:, kc * TB:(kc + 1) * TB],
                             ks[:, h, chunk(2 * b + kc)], qs[:, b, h, :])
                ins.then_inc(a_ST, 1)

            def head_values(hg, kc):
                b, g4 = hg // 4, hg % 4
                if hg == 0:
                    pe.wait_ge(a_zeros, 2)
                pe.wait_ge(a_exp, 4 * hg + 4)
                if hg >= 4 and g4 % 2 == 0 and kc == 0:
                    pe.wait_ge(a_oun, hg // 2 - 1)
                for i in range(4):
                    h = 4 * g4 + i
                    ins = mm(bank[5 + g4 // 2][32 * i:32 * i + VW,
                                               (g4 % 2) * TB:(g4 % 2 + 1) * TB],
                             vaug[:, 2 * b + kc, h, :],
                             prob1[:, (4 * hg + i) % NPROB, kc * TB:(kc + 1) * TB],
                             start=(kc == 0), stop=(kc == 1))
                if kc == 1:
                    ins.then_inc(a_O, 1)

            def output_transposes(c):
                b, i = c // 2, c % 2
                pe.wait_ge(a_oun, 2 * b + 2)
                pe.wait_ge(a_nmT, transposed["maxima"])
                if c >= 1:
                    pe.wait_ge(a_on, c)
                transposed["outputs"] += 1
                for g4 in range(4):
                    at = g4 * TB + i * P
                    ins = pe.transpose(bank[4][:, chunk(g4)], oun[:, at:at + P], ident[:, :])
                ins.then_inc(a_oT, 1)

            def normed_transposes(c):
                pe.wait_ge(a_on, c + 1)
                if 1 <= c < NC - 1:
                    pe.wait_ge(x3_sb, c)
                pe.transpose(bank[NORMED_BANK[c]][:, 0:P], onrm[:, c, :], ident[:, :]
                             ).then_inc(a_onTp, 1)

            def attention_out(c):
                pe.wait_ge(a_onT, c + 1)
                mm(bank[NORMED_BANK[c]][:, 0:P], onT[:, chunk(c)], packa[:, A_WO1:A_WO1 + P]
                   ).then_inc(a_out, 1)

            pe.wait_ge(c_all, 1 + NB)
            pe.wait_ge(v1_sb, 3)
            pe.wait_ge(ks_in, 16 * NCOMB)
            def router_logits(h2):
                pe.wait_ge(ln_tsb, 8 + h2 + 1)
                if h2 == 0:
                    pe.wait_ge(a_max, NB * NH)
                for c in range(4 * h2, 4 * h2 + 4):
                    ins = mm(bank[ROUTER_BANK[h2]][:, c * E1:(c + 1) * E1], xnT[:, chunk(c)],
                             packa[:, A_WR:A_WR + E1])
                ins.then_inc(r_ps, 1)

            def router_ranks(h2):
                pe.wait_ge(r_oh, h2 + 1)
                for c in range(4 * h2, 4 * h2 + 4):
                    o = bank[ROUTER_BANK[h2]][:, c * 2 * E1:(c + 1) * 2 * E1]
                    for cc in range(c):
                        mm(o, ones[:, :], roh[:, cc, :, :].rearrange("p k e -> p (k e)"),
                           start=(cc == 0), stop=False)
                    ins = mm(o, tri[:, :], roh[:, c, :, :].rearrange("p k e -> p (k e)"),
                             start=(c == 0))
                ins.then_inc(r_rank, 1)

            def router_transposes(h2):
                pe.wait_ge(r_wp, h2 + 1)
                for c in range(4 * h2, 4 * h2 + 4):
                    ins = pe.transpose(
                        bank[ROUTER_BANK_T[h2]][0:3 * E1, :].bitcast(BF16)[:, chunk(c)],
                        wparts[:, c, :, :].rearrange("p k e -> p (k e)"), identb[:, :])
                ins.then_inc(r_wTp, 1)

            def ffn_hidden(n):
                q, f = n // NF, n % NF
                e, h2 = QS[q]
                if f == 0:
                    pe.wait_ge(f_w1, e + 1)
                    pe.wait_ge(r_x, h2 + 1)
                if n == 0:
                    pe.wait_ge(r_wT, 1)
                if n == 2:
                    pe.wait_ge(a_exp, NB * NH - 1)
                if n >= 3:
                    pe.wait_ge(f_act, n - 2)
                wh, wl = w1h[:, e % 2, chunk(f)], w1l[:, e % 2, chunk(f)]
                o = bank[n % 3][:, :]
                mm(o, wh, xTh[:, half(h2)], stop=False)
                mm(o, wh, xTl[:, half(h2)], start=False, stop=False)
                mm(o, wl, xTh[:, half(h2)], start=False).then_inc(f_H, 1)

            def ffn_out(n):
                q, f = n // NF, n % NF
                e = QS[q][0]
                if n == 0:
                    pe.wait_ge(a_exp, NB * NH)
                if n == NF:
                    pe.wait_ge(x3_sb, NC)
                if f == 0 and q >= 2:
                    pe.wait_ge(f_yw, q - 1)
                if f == 0:
                    pe.wait_ge(f_w2, e + 1)
                pe.wait_ge(f_hi, n + 1)
                wh, wl = w2h[:, e % 2, chunk(f)], w2l[:, e % 2, chunk(f)]
                o = bank[3 + q % 2][:, :]
                mm(o, wh, acth[:, n % NA, :], start=(f == 0), stop=False)
                mm(o, wl, acth[:, n % NA, :], start=False, stop=False)
                pe.wait_ge(f_lo, n + 1)
                mm(o, wh, actl[:, n % NA, :], start=False, stop=(f == NF - 1)).then_inc(f_Y, 1)

            def weight_rows(q):
                e, h2 = QS[q]
                pe.wait_ge(r_wT, h2 + 1)
                if q < 2:
                    pe.wait_ge(a_oun, 2 * NB)
                else:
                    pe.wait_ge(f_wbc, q - 1)
                mm(bank[5 + q % 2][:, :], selw[:, e, :], wT[:, half(h2)]).then_inc(f_bc, 1)

            def sum_transposes(i):
                first, n = LAST_CHUNKS[i]
                pe.wait_ge(f_acc, 2 * (E1 - 1) - 1 + i)
                if i == 0:
                    pe.wait_ge(r_wT, 2)
                for c in range(n):
                    ins = pe.transpose(bank[SUM_BANK[i]][:, chunk(c)],
                                       accT[:, chunk(first + c)], ident[:, :])
                ins.then_inc(f_oT, 1)

            tail_steps = {"transposes": output_transposes, "normed transposes": normed_transposes,
                          "output": attention_out}
            for s in range(SLOTS):
                m, e = s, s - LAG
                if m < NB * NH:
                    max_scores(m)
                if m % 8 == 2 and 1 <= m // 8 <= 2 * NB:
                    maxima_transposes(m // 8 - 1)
                if 0 <= e < NB * NH:
                    exp_scores(e)
                n = e - TILE0
                if 0 <= n < NT:
                    ffn_hidden(n)
                for name in ("normed transposes", "output", "transposes"):
                    c = tail_chunk(name, e)
                    if c is not None:
                        tail_steps[name](c)
                for h2 in range(2):
                    for at, step in ((NORM_T, norm_transposes), (ROUTER_LOGITS, router_logits),
                                     (ROUTER_RANKS, router_ranks),
                                     (ROUTER_T, router_transposes)):
                        if e == at[h2]:
                            step(8 + h2 if step is norm_transposes else h2)
                for hg in range(4 * NB):
                    for kc in range(2):
                        if e == min(4 * hg + 6 + kc, NB * NH):
                            head_values(hg, kc)
                for q in range(2 * E1):
                    if n == rows_at(q):
                        weight_rows(q)
                if 2 <= n < NT + 2:
                    ffn_out(n - 2)
            for i in range(len(LAST_CHUNKS)):
                sum_transposes(i)

        @block.vector
        def _(v):
            steps = [0]

            def chained(ins):
                steps[0] += 1
                ins.then_inc(dve_step, 1)
                v.wait_ge(dve_step, steps[0])

            def statistics(step):
                cs = LN_CHUNKS[step]
                for c in cs:
                    ins = v.bn_stats(st[:, c, :], x[:, c, :])
                chained(ins)
                for c in cs:
                    ins = v.bn_aggr(mv[:, c, :], st[:, c, :])
                chained(ins)
                v.tensor_scalar(veps[:, cs[0]:cs[-1] + 1], mv[:, cs[0]:cs[-1] + 1, 1], EPS, None,
                                ALU.add).then_inc(ln_var, 1)

            def normalise(step):
                v.wait_ge(ln_rstd, step + 1)
                if ln_before(step):
                    v.wait_ge(ln_tps, ln_before(step))
                for c in LN_CHUNKS[step]:
                    ins = v.tensor_scalar(xn[:, c, :], x[:, c, :], mv[:, c, 0:1], rstd[:, c:c + 1],
                                          ALU.subtract, ALU.mult)
                ins.then_inc(ln_out, 1)

            v.wait_ge(ld_x, 16)
            statistics(0)
            statistics(1)
            normalise(0)
            normalise(1)

            def keys1_residual(h2):
                v.wait_ge(k1_hi, h2 + 1)
                v.tensor_tensor(out=(ra, rb)[h2][:, :], in0=bank[h2][:, :],
                                in1=parts[:, 0, half(h2)], op=ALU.subtract).then_inc(k1_res, 1)

            def keys1_last(h2):
                v.wait_ge(k1_mid, h2 + 1)
                v.tensor_tensor(out=parts[:, 2, half(h2)], in0=(ra, rb)[h2][:, :],
                                in1=parts[:, 1, half(h2)], op=ALU.subtract).then_inc(k1_lo, 1)

            v.wait_ge(ld_small, 64)
            for h2 in range(2):
                v.wait_ge(q0_ps, h2 + 1)
                v.tensor_scalar(q0T[:, half(h2)], bank[2 + h2][:, :], biases[:, B_BQ0:B_BQ0 + 1],
                                float(P) ** -0.5, ALU.add, ALU.mult).then_inc(q0_sb, 1)
            def maximum0(c):
                v.wait_ge(s0_ps, c + 1)
                v.tensor_reduce(nm0[:, c:c + 1], bank[4 + c % 2][:, 0:KV], X, ALU.max,
                                negate=True).then_inc(m0_sb, 1)

            def residual1(c):
                v.wait_ge(p0_sb, c + 1)
                chained(v.reciprocal(rs0[:, c:c + 1], sum0[:, c:c + 1]))
                v.wait_ge(o0_ps, c + 1)
                v.scalar_tensor_tensor(out=x[:, c, :], in0=bank[c % 2][:, 0:P],
                                       scalar=rs0[:, c:c + 1], in1=x[:, c, :], op0=ALU.mult,
                                       op1=ALU.add).then_inc(x1_sb, 1)

            maximum0(0)
            keys1_residual(0)
            for c in range(NC):
                if c + 1 < NC:
                    maximum0(c + 1)
                if c == 0:
                    keys1_residual(1)
                if c == 7:
                    normalise(2)
                if c >= 1:
                    residual1(c - 1)
                if c in (3, 4):
                    keys1_last(c - 3)
                if c == 5:
                    v.wait_ge(x1_sb, 4)
                    statistics(2)
            residual1(NC - 1)

            def gate_less_maximum(h2):
                cs = slice(4 * h2, 4 * h2 + 4)
                logits = bank[GATE_BANK[h2]][:, h2 * 256:(h2 + 1) * 256].rearrange(
                    "p (c e) -> p c e", c=4)
                v.wait_ge(g_ps, h2 + 1)
                chained(v.tensor_reduce(nmg[:, cs], logits, X, ALU.max, negate=True))
                v.tensor_tensor(out=ra[:, h2 * 256:(h2 + 1) * 256].rearrange(
                                    "p (c e) -> p c e", c=4), in0=logits,
                                in1=view(nmg[:, cs], (1, 4), (0, E0)), op=ALU.add
                                ).then_inc(g_sub, 1)

            def gate_choices(h2):
                cs, first = slice(4 * h2, 4 * h2 + 4), 4 * h2
                v.wait_ge(g_exp, h2 + 1)
                chained(v.reduce_sum(sumg[:, cs], score[:, cs, :], X))
                chained(v.reciprocal(rsg[:, cs], sumg[:, cs]))
                v.tensor_tensor(out=score[:, cs, :], in0=score[:, cs, :],
                                in1=view(rsg[:, cs], (1, 4), (0, E0)), op=ALU.mult
                                ).then_inc(g_score, 1)
                v.wait_ge(g_score, h2 + 1)
                chained(v.tensor_tensor(out=biased[:, cs, :], in0=score[:, cs, :],
                                        in1=view(gateb[:, :], (0, 4), (1, E0)), op=ALU.add))
                for c in range(first, first + 4):
                    ins = v.max(out=top8[:, c, :], in_=biased[:, c, :])
                chained(ins)
                for c in range(first, first + 4):
                    ins = v.max_index(out=idx8[:, c, :], in_max=top8[:, c, :],
                                      in_values=biased[:, c, :])
                chained(ins)
                lowest = view(top8[:, first, K0 - 1:K0], (8, 4), (0, E0))
                v.tensor_tensor(out=selb[:, cs, :], in0=biased[:, cs, :], in1=lowest, op=ALU.is_gt)
                v.tensor_tensor(out=equal[:, h2], in0=biased[:, cs, :], in1=lowest,
                                op=ALU.is_equal)
                chained(v.tensor_tensor(out=before[:, h2],
                                        in0=view(iota_e[:, :], (0, 4), (1, E0)),
                                        in1=view(idx8[:, first, K0 - 1:K0], (8, 4), (0, E0)),
                                        op=ALU.is_le))
                chained(v.tensor_tensor(out=equal[:, h2], in0=equal[:, h2],
                                        in1=before[:, h2], op=ALU.mult))
                v.tensor_tensor(out=selb[:, cs, :], in0=selb[:, cs, :], in1=equal[:, h2],
                                op=ALU.add).then_inc(g_sel, 1)

            def gate_slots(h2):
                v.wait_ge(g_rank, h2 + 1)
                for c in range(4 * h2, 4 * h2 + 4):
                    ins = v.tensor_tensor(
                        out=view(rk[:, 0, c, 0, 0:1], (NC * GE * 2, NG), (2, GE), (1, 2)),
                        in0=view(bank[GATE_BANK[h2]][:, c * E0:c * E0 + 1],
                                 (GE, NG), (1, GE), (0, 2)),
                        in1=view(selb[:, c, 0:1], (GE, NG), (1, GE), (0, 2)), op=ALU.mult)
                chained(ins)

            v.wait_ge(x1_sb, NC)
            statistics(3)
            gate_less_maximum(0)
            normalise(3)
            gate_choices(0)
            gate_less_maximum(1)
            gate_slots(0)
            gate_choices(1)

            def dispatch(g, chunks=range(NC)):
                if g >= 3:
                    v.wait_ge(e_T, NPAIR * (g - 2))
                n, c = len(chunks), chunks[0]
                v.tensor_tensor(out=view(onehots[g % 3][:, c * GS:c * GS + 1], (CAP0, n * GE),
                                         (2, CAP0 // 2), (1, 2)),
                                in0=view(rk[:, g, c, 0, 0:1], (2, n * GE), (0, CAP0 // 2), (1, 2)),
                                in1=view(iota_s[:, 0:1], (0, n * GE), (2, CAP0 // 2), (1, 2)),
                                op=ALU.is_equal).then_inc(e_P, n)

            dispatch(0, range(0, 4))
            gate_slots(1)

            def slot_values(g):
                v.wait_ge(e_W, g + 1)
                for s in range(2):
                    ps = slice(64 * s, 64 * s + 64)
                    v.reduce_sum(wslot[ps, g % 3, :],
                                 view(bank[2][ps, NW * s:NW * s + 1], (2 * NW, NPAIR), (1, 3)), X)
                    ins = v.reduce_sum(
                        token_f[ps, :],
                        view(bank[2][ps, NW * s + 3:NW * s + 4], (2 * NW, NPAIR), (1, 2)), X)
                chained(ins)
                v.tensor_copy(slot_token[:, g % 3, :], token_f[:, :]).then_inc(e_id, 1)

            def dispatch_even(g, j):
                v.wait_ge(e_T, NPAIR * g + j + 1)
                if g >= 1:
                    v.wait_ge(e_comb, g)
                v.tensor_copy(PTs[:, j, :], bank[3][:, :].bitcast(BF16)).then_inc(e_PTv, 1)

            dispatch(0, range(4, 8))
            dispatch(1, range(0, 4))
            slot_values(0)
            dispatch(1, range(4, 8))
            dispatch_even(0, 0)
            slot_values(1)
            dispatch(2)
            for g in range(NG):
                v.wait_ge(e_id, g + 1)
                v.wait_ge(e_sil, 2 * g + 2)
                if g >= 1:
                    v.wait_ge(e_gTp, g)
                for j in range(NPAIR):
                    at = (j % 2) * SI + I0
                    ins = v.scalar_tensor_tensor(out=gv[:, j, :],
                                                 in0=bank[5 + j // 2][:, at:at + I0],
                                                 scalar=wslot[:, g % 3, j:j + 1], in1=sil[:, j, :],
                                                 op0=ALU.mult, op1=ALU.mult)
                ins.then_inc(e_gv, 1)
                if g >= 1:
                    dispatch_even(g, 0)
                if g + 2 < NG:
                    slot_values(g + 2)
                dispatch_even(g, 2)
                v.wait_ge(e_yh, g + 1)
                v.tensor_tensor(out=yl, in0=bank[7][:, :].rearrange("p (j d) -> p j d", j=NPAIR),
                                in1=yh.bitcast(F32), op=ALU.subtract).then_inc(e_yl, 1)
                if g + 3 < NG:
                    dispatch(g + 3)

            def residual2(b):
                v.wait_ge(z_T, b + 1)
                xb2 = x[:, 2 * b:2 * b + 2, :]
                v.tensor_tensor(out=xb2, in0=xb2,
                                in1=bank[Z_BANK[b]][:, 0:TB].rearrange(
                                    "p (c d) -> p c d", c=2), op=ALU.add).then_inc(x2_sb, 1)

            def statistics2(b):
                v.wait_ge(x2_sb, b + 1)
                statistics(4 + b)

            def queries(b):
                v.wait_ge(q1_ps, b + 1)
                v.tensor_scalar(qf[:, batch(b)], bank[6 + b % 2][:, 0:TB],
                                biases[:, B_BQ1:B_BQ1 + 1], SCALE1, ALU.add,
                                ALU.mult).then_inc(q1_f, 1)

            def query_residual(b):
                v.wait_ge(q1_hi, b + 1)
                v.tensor_tensor(out=query_rest(b), in0=qf[:, batch(b)], in1=parts[:, 0, batch(b)],
                                op=ALU.subtract).then_inc(q1_res, 1)

            def query_last(b):
                v.wait_ge(q1_mid, b + 1)
                v.tensor_tensor(out=parts[:, 2, batch(b)], in0=query_rest(b),
                                in1=parts[:, 1, batch(b)], op=ALU.subtract).then_inc(q1_lo, 1)

            residual2(0)
            statistics2(0)
            residual2(1)
            statistics2(1)
            normalise(4)
            normalise(5)
            residual2(2)
            statistics2(2)
            queries(0)
            residual2(3)
            query_residual(0)
            normalise(6)
            query_last(0)
            statistics2(3)
            queries(1)
            query_residual(1)
            normalise(7)
            query_last(1)

            def operands(h2):
                v.wait_ge(ln_tsb, 8 + h2 + 1)
                chained(v.tensor_copy(xTh[:, half(h2)], xnT[:, half(h2)]))
                v.tensor_tensor(out=xTl[:, half(h2)], in0=xnT[:, half(h2)],
                                in1=xTh[:, half(h2)].bitcast(F32), op=ALU.subtract
                                ).then_inc(r_x, 1)

            def router_less_maximum(h2):
                cs = slice(4 * h2, 4 * h2 + 4)
                logits = bank[ROUTER_BANK[h2]][:, h2 * 4 * E1:(h2 + 1) * 4 * E1].rearrange(
                    "p (c e) -> p c e", c=4)
                v.wait_ge(r_ps, h2 + 1)
                chained(v.tensor_reduce(rsum[:, cs], logits, X, ALU.max, negate=True))
                v.tensor_tensor(out=rp[:, cs, :], in0=logits,
                                in1=view(rsum[:, cs], (1, 4), (0, E1)),
                                op=ALU.add).then_inc(r_sub, 1)

            def router_choices(h2):
                cs, first = slice(4 * h2, 4 * h2 + 4), 4 * h2
                v.wait_ge(r_exp, h2 + 1)
                for c in range(first, first + 4):
                    ins = v.max(out=rtop[:, c, :], in_=rp[:, c, :])
                chained(ins)
                for c in range(first, first + 4):
                    ins = v.max_index(out=ridx[:, c, :], in_max=rtop[:, c, :],
                                      in_values=rp[:, c, :])
                chained(ins)
                chained(v.tensor_copy(ridxf[:, cs, :], ridx[:, cs, :]))
                v.tensor_tensor(out=roh[:, cs, :, :],
                                in0=view(iota_e[:, :], (0, 4), (0, 2), (1, E1)),
                                in1=view(ridxf[:, first, 0:1], (8, 4), (1, 2), (0, E1)),
                                op=ALU.is_equal).then_inc(r_oh, 1)
                v.wait_ge(r_oh, h2 + 1)
                chained(v.tensor_tensor(out=rsum[:, cs], in0=rtop[:, cs, 0], in1=rtop[:, cs, 1],
                                        op=ALU.add))
                chained(v.reciprocal(rsum[:, cs], rsum[:, cs]))
                chained(v.tensor_tensor(out=rtv[:, cs, :], in0=rtop[:, cs, 0:2],
                                        in1=view(rsum[:, cs], (1, 4), (0, 2)), op=ALU.mult))

            def router_weights(h2):
                cs, first, n = slice(4 * h2, 4 * h2 + 4), 4 * h2, 4 * 2 * E1
                v.wait_ge(r_rank, h2 + 1)
                chained(v.scalar_tensor_tensor(
                    out=rkeep[:, cs, :, :].rearrange("p c k e -> p (c k e)"),
                    in0=bank[ROUTER_BANK[h2]][:, h2 * n:(h2 + 1) * n], scalar=float(CAP1),
                    in1=roh[:, cs, :, :].rearrange("p c k e -> p (c k e)"),
                    op0=ALU.is_le, op1=ALU.mult))
                chained(v.tensor_tensor(out=rkeep[:, cs, :, :], in0=rkeep[:, cs, :, :],
                                        in1=view(rtv[:, first, 0:1], (2, 4), (1, 2), (0, E1)),
                                        op=ALU.mult))
                chained(v.tensor_tensor(out=wtok[:, cs, :], in0=rkeep[:, cs, 0, :],
                                        in1=rkeep[:, cs, 1, :], op=ALU.add))
                chained(v.tensor_copy(wparts[:, cs, 0, :], wtok[:, cs, :]))
                chained(v.tensor_tensor(out=wres[:, cs, :], in0=wtok[:, cs, :],
                                        in1=wparts[:, cs, 0, :], op=ALU.subtract))
                chained(v.tensor_copy(wparts[:, cs, 1, :], wres[:, cs, :]))
                v.tensor_tensor(out=wparts[:, cs, 2, :], in0=wres[:, cs, :],
                                in1=wparts[:, cs, 1, :], op=ALU.subtract).then_inc(r_wp, 1)

            sums = [0]

            def weighted(q, at=0, n=512):
                e, h2 = QS[q]
                acc = accT[:, h2 * 512 + at:h2 * 512 + at + n]
                v.wait_ge(f_Y, NF * (q + 1))
                v.wait_ge(f_wbc, q + 1)
                v.scalar_tensor_tensor(out=acc if e == 0 else ywt[:, h2, at:at + n],
                                       in0=bank[3 + q % 2][:, at:at + n],
                                       scalar=biases[:, B_B2 + e:B_B2 + e + 1],
                                       in1=wbc[:, q % 2, at:at + n], op0=ALU.add,
                                       op1=ALU.mult).then_inc(f_yw, 1)

            def summed(q, at=0, n=512):
                e, h2 = QS[q]
                acc = accT[:, h2 * 512 + at:h2 * 512 + at + n]
                if e >= 1:
                    v.wait_ge(f_yw, q + 1 + at // n)
                    if sums[0]:
                        v.wait_ge(f_acc, sums[0])
                    sums[0] += 1
                    v.tensor_tensor(out=acc, in0=acc, in1=ywt[:, h2, at:at + n],
                                    op=ALU.add).then_inc(f_acc, 1)

            for s in range(SLOTS):
                m, e = s, s - LAG
                if m < NB * NH:
                    c, hp = 2 * (m // NH) + m % 2, m % NH // 2
                    v.wait_ge(a_S, m + 1)
                    v.tensor_reduce(nm1[:, c, 2 * hp:2 * hp + 2],
                                    bank[m % 2][:, :].rearrange("p (h k) -> p h k", h=2), X,
                                    ALU.max, negate=True).then_inc(a_max, 1)
                for i, step in enumerate((queries, query_residual, query_last)):
                    if s in (i, i + 1):
                        step(2 + s - i)
                c = tail_chunk("division", e)
                if c is not None:
                    v.wait_ge(a_oT, c + 1)
                    chained(v.reciprocal(rden[:, c, :], view(bank[4][:, HD:HD + 1], (32, NH))))
                    v.tensor_tensor(out=onrm[:, c, :].rearrange("p (h d) -> p h d", h=NH),
                                    in0=view(bank[4][:, 0:1], (32, NH), (1, HD)),
                                    in1=view(rden[:, c, :], (1, NH), (0, HD)),
                                    op=ALU.mult).then_inc(a_on, 1)
                c = tail_chunk("residual", e)
                if c is not None:
                    v.wait_ge(a_out, c + 1)
                    if c == 0:
                        v.wait_ge(x2_sb, NB + 1)
                    v.tensor_tensor(out=x[:, c, :], in0=x[:, c, :],
                                    in1=bank[NORMED_BANK[c]][:, 0:P],
                                    op=ALU.add).then_inc(x3_sb, 1)
                for h2 in range(2):
                    if e == STATISTICS[h2]:
                        v.wait_ge(x3_sb, 4 * h2 + 4)
                        statistics(8 + h2)
                    if e == NORMALISE[h2]:
                        normalise(8 + h2)
                    if e == OPERANDS[h2]:
                        operands(h2)
                    if e == ROUTER_SUB[h2]:
                        router_less_maximum(h2)
                    if e == ROUTER_CHOICES[h2]:
                        router_choices(h2)
                    if e == ROUTER_WEIGHTS[h2]:
                        router_weights(h2)
                n = e - TILE0 - 1
                if not 0 <= n < NT:
                    continue
                v.wait_ge(f_act, n + 1)
                v.wait_ge(f_hi, n + 1)
                if n >= NA:
                    v.wait_ge(f_Y, n - NA + 1)
                v.tensor_tensor(out=actl[:, n % NA, :], in0=act[:, n % 4, :],
                                in1=acth[:, n % NA, :].bitcast(F32), op=ALU.subtract
                                ).then_inc(f_lo, 1)
                for q in range(2 * E1 - 1):
                    if n == min(rows_at(q) + 1, NT - 1):
                        weighted(q)
                    if n == min(rows_at(q) + 2, NT - 1):
                        summed(q)
                for q in range(2 * E1):
                    if n == rows_at(q):
                        v.wait_ge(f_bc, q + 1)
                        v.tensor_copy(wbc[:, q % 2, :], bank[5 + q % 2][:, :]).then_inc(f_wbc, 1)

            def layer_sum(i):
                c, n = LAST_CHUNKS[i]
                v.wait_ge(f_oT, i + 1)
                v.tensor_tensor(out=x[:, c:c + n, :], in0=x[:, c:c + n, :],
                                in1=bank[SUM_BANK[i]][:, 0:n * P].rearrange(
                                    "p (c d) -> p c d", c=n), op=ALU.add).then_inc(x4_sb, 1)

            for at in (0, TB):
                weighted(2 * E1 - 1, at, TB)
            layer_sum(0)
            for at in (0, TB):
                summed(2 * E1 - 1, at, TB)
            layer_sum(1)
            layer_sum(2)


def kernel(**inputs):
    import numpy as np
    import concourse.bacc as bacc
    from concourse.bass_utils import run_bass_kernel_spmd

    a = {k: np.asarray(v) for k, v in inputs.items()}
    cat = np.concatenate

    def by_feature(w):
        return w.reshape(-1, NH, HD).transpose(0, 2, 1).reshape(-1, P)

    arrays = {
        "x": a["x"].reshape(T, P),
        "ctxT": a["ctx_768"].reshape(T, CD).T,
        "packa": cat([a["L0_xattn_Wq"], by_feature(a["L1_xattn_Wq"].T), a["L1_xattn_Wo"].T,
                      a["L0_ffn_gate_w"].T, a["L0_ffn_ws1"].T, a["L0_ffn_ws3"].T,
                      a["L1_ffn_Wr"]], axis=1),
        "packc": cat([cat([a["L0_xattn_Wk"], a["L0_xattn_bk"][None]], 0)[:, None],
                      cat([a["L0_xattn_Wv"], a["L0_xattn_bv"][None]], 0)[:, None],
                      by_feature(cat([a["L1_xattn_Wk"].T, a["L1_xattn_bk"][None]], 0))[:, None],
                      cat([a["L1_xattn_Wv"].T, a["L1_xattn_bv"][None]], 0)[:, None]], axis=1),
        "biases": cat([a["L0_xattn_bq"][:, None], by_feature(a["L1_xattn_bq"]).T,
                       a["L1_ffn_b1"].reshape(E1, NF, P).transpose(2, 0, 1).reshape(P, E1 * NF),
                       a["L1_ffn_b2"].T], axis=1),
        "gateb": a["L0_ffn_gate_b"][None],
        "bo": a["L1_xattn_bo"][None],
        "ws2": a["L0_ffn_ws2"].T.reshape(2, I0, P).transpose(1, 0, 2),
        "w13": cat([a["L0_ffn_w1"], a["L0_ffn_w3"]], axis=1).transpose(2, 0, 1),
        "w2": a["L0_ffn_w2"].transpose(2, 0, 1),
        "ew1": a["L1_ffn_W1"].transpose(1, 0, 2),
        "ew2": a["L1_ffn_W2"].reshape(E1, NF, P, P).transpose(2, 0, 1, 3),
    }
    arrays = {f"in_{k}": np.ascontiguousarray(v) for k, v in arrays.items()}
    nc = bacc.Bacc("TRN2", target_bir_lowering=False, num_devices=1)
    args = [nc.dram_tensor(k, v.shape, mybir.dt.from_np(v.dtype), kind="ExternalInput").ap()
            for k, v in arrays.items()]
    args.append(nc.dram_tensor("out_x", (T, P), F32, kind="ExternalOutput").ap())
    build(nc, *args)
    r = run_bass_kernel_spmd(nc, [arrays], core_ids=[0])
    return r.results[0]["out_x"].reshape(a["x"].shape)
```
